# Optimizing a Trainium2 kernel written in Bass

```python
import numpy as np
import jax
import jax.numpy as jnp

def _softmax(x, axis=-1):
    return jax.nn.softmax(x, axis=axis)

def _gelu(x):
    return jax.nn.gelu(x, approximate=True)

def _silu(x):
    return jax.nn.silu(x)

def _sigmoid(x):
    return jax.nn.sigmoid(x)

def _layernorm(x, axis=-1, eps=1e-05):
    m = jnp.mean(x, axis=axis, keepdims=True)
    v = jnp.var(x, axis=axis, keepdims=True)
    return (x - m) / jnp.sqrt(v + eps)

def _scatter_add(tgt, idx, src, axis=0):
    return tgt.at[idx].add(src)

def _segment_sum(src, seg, n):
    return jax.ops.segment_sum(src, seg, n)
kernel_name = 'mk_lm_tower_d4_tok_ids256_r4_27241c'

def setup_inputs(seed: int=0):
    np.random.seed(seed)
    _w = jnp.asarray

    def _rec_inputs():
        import jax
        import jax.numpy as jnp
        _rk = jax.random.key(seed)
        x = jax.random.randint(jax.random.fold_in(_rk, 1), (128, 128), 0, 50257, jnp.int32)
        return x
    x = _rec_inputs()

    def _L0_tok_setup():
        import jax, jax.numpy as jnp
        import numpy as np
        VOCAB = 50257
        DIM = 64

        def _positional_table(seq_len, dim, dtype=jnp.float32):
            pos = jnp.arange(seq_len, dtype=dtype)[:, None]
            d = jnp.arange(dim)
            exponent = (d - d % 2).astype(dtype) / dim
            inv_freq = jnp.power(jnp.asarray(10000.0, dtype), -exponent)
            angle = pos * inv_freq
            return jnp.where(d % 2 == 0, jnp.sin(angle), jnp.cos(angle))
        key = jax.random.key(seed)
        k1, k2 = jax.random.split(key)
        x = jax.random.randint(k1, (32, 1024), 0, VOCAB)
        W = jax.random.normal(k2, (VOCAB, DIM), dtype=jnp.float32)
        return {'x': x, 'W': W}
    _L0_tok_all = _L0_tok_setup()
    _L0_tok_in = {k: v for k, v in _L0_tok_all.items() if k in ('W',)}
    del _L0_tok_all

    def _L0_attn_setup():
        import jax, jax.numpy as jnp
        import numpy as np
        import math
        N_SEQ, L_RES, D_MODEL = (128, 96, 64)
        N_HEAD, C_HEAD = (8, 32)
        EPS = 1e-05
        key = jax.random.key(seed)
        ks = jax.random.split(key, 8)
        s = 1.0 / math.sqrt(D_MODEL)
        return {'m': jax.random.normal(ks[0], (N_SEQ, L_RES, D_MODEL), jnp.float32), 'gamma': jnp.ones((D_MODEL,), jnp.float32), 'beta': jnp.zeros((D_MODEL,), jnp.float32), 'Wq': jax.random.normal(ks[1], (D_MODEL, N_HEAD * C_HEAD), jnp.float32) * s, 'Wk': jax.random.normal(ks[2], (D_MODEL, N_HEAD * C_HEAD), jnp.float32) * s, 'Wv': jax.random.normal(ks[3], (D_MODEL, N_HEAD * C_HEAD), jnp.float32) * s, 'Wg': jax.random.normal(ks[4], (D_MODEL, N_HEAD * C_HEAD), jnp.float32) * s, 'bg': jnp.zeros((N_HEAD * C_HEAD,), jnp.float32), 'Wo': jax.random.normal(ks[5], (N_HEAD * C_HEAD, D_MODEL), jnp.float32) * s, 'bo': jnp.zeros((D_MODEL,), jnp.float32)}
    _L0_attn_all = _L0_attn_setup()
    _L0_attn_in = {k: v for k, v in _L0_attn_all.items() if k in ('gamma', 'beta', 'Wq', 'Wk', 'Wv', 'Wg', 'bg', 'Wo', 'bo')}
    del _L0_attn_all

    def _L0_ffn_setup():
        import jax, jax.numpy as jnp
        import numpy as np
        B, T, D, H, E = (16, 1024, 64, 128, 8)
        key = jax.random.key(seed)
        ks = jax.random.split(key, 5)
        x = jax.random.normal(ks[0], (B, T, D), dtype=jnp.float32)
        gate_w = jax.random.normal(ks[1], (D, E), dtype=jnp.float32) * 0.02
        gate_b = jnp.zeros((E,), dtype=jnp.float32)
        W1 = jax.random.normal(ks[2], (E, D, H), dtype=jnp.float32) * 0.02
        b1 = jnp.zeros((E, H), dtype=jnp.float32)
        W2 = jax.random.normal(ks[3], (E, H, D), dtype=jnp.float32) * 0.02
        b2 = jnp.zeros((E, D), dtype=jnp.float32)
        return {'x': x, 'gate_w': gate_w, 'gate_b': gate_b, 'W1': W1, 'b1': b1, 'W2': W2, 'b2': b2}
    _L0_ffn_all = _L0_ffn_setup()
    _L0_ffn_in = {k: v for k, v in _L0_ffn_all.items() if k in ('gate_w', 'gate_b', 'W1', 'b1', 'W2', 'b2')}
    del _L0_ffn_all

    def _L1_attn_setup():
        import jax, jax.numpy as jnp
        import numpy as np
        import math
        NUM_HEADS = 8
        HEAD_SIZE = 32

        def get_alibi_slopes(n_heads):

            def pow2_slopes(n):
                start = 2.0 ** (-2.0 ** (-(math.log2(n) - 3)))
                ratio = start
                return [start * ratio ** i for i in range(n)]
            if math.log2(n_heads).is_integer():
                return np.array(pow2_slopes(n_heads), dtype=np.float32)
            cp2 = 2 ** math.floor(math.log2(n_heads))
            extra = pow2_slopes(2 * cp2)[0::2][:n_heads - cp2]
            return np.array(pow2_slopes(cp2) + extra, dtype=np.float32)
        ALIBI_SLOPES = jnp.asarray(get_alibi_slopes(NUM_HEADS))
        key = jax.random.key(seed)
        ks = jax.random.split(key, 6)
        B, T, C = (32, 128, 64)
        s = 1.0 / math.sqrt(C)
        return {'x': jax.random.normal(ks[0], (B, T, C), dtype=jnp.float32), 'Wq': jax.random.normal(ks[1], (C, NUM_HEADS * HEAD_SIZE), dtype=jnp.float32) * s, 'Wk': jax.random.normal(ks[2], (C, NUM_HEADS * HEAD_SIZE), dtype=jnp.float32) * s, 'Wv': jax.random.normal(ks[3], (C, NUM_HEADS * HEAD_SIZE), dtype=jnp.float32) * s, 'Wo': jax.random.normal(ks[4], (NUM_HEADS * HEAD_SIZE, C), dtype=jnp.float32) * s, 'bo': jax.random.normal(ks[5], (C,), dtype=jnp.float32) * 0.01}
    _L1_attn_all = _L1_attn_setup()
    _L1_attn_in = {k: v for k, v in _L1_attn_all.items() if k in ('Wq', 'Wk', 'Wv', 'Wo', 'bo')}
    del _L1_attn_all

    def _L1_ffn_setup():
        import jax, jax.numpy as jnp
        import numpy as np
        E = 8
        K = 2
        D = 64
        H = 128
        DOUT = 64
        EPS = 1e-05
        key = jax.random.key(seed)
        ks = jax.random.split(key, 9)
        s = 0.02
        return {'x': jax.random.normal(ks[0], (4, 2048, D), jnp.float32), 'gamma': 1.0 + 0.05 * jax.random.normal(ks[1], (D,), jnp.float32), 'beta': 0.05 * jax.random.normal(ks[2], (D,), jnp.float32), 'Wr': 0.01 * jax.random.normal(ks[3], (D, E), jnp.float32), 'br': jnp.zeros((E,), jnp.float32), 'W1': s * jax.random.normal(ks[4], (E, D, H), jnp.float32), 'b1': s * jax.random.normal(ks[5], (E, H), jnp.float32), 'W2': s * jax.random.normal(ks[6], (E, H, DOUT), jnp.float32), 'b2': s * jax.random.normal(ks[7], (E, DOUT), jnp.float32)}
    _L1_ffn_all = _L1_ffn_setup()
    _L1_ffn_in = {k: v for k, v in _L1_ffn_all.items() if k in ('gamma', 'beta', 'Wr', 'br', 'W1', 'b1', 'W2', 'b2')}
    del _L1_ffn_all

    def _L2_attn_setup():
        import jax, jax.numpy as jnp
        import numpy as np
        import math
        EMBED_DIM = 64
        SEQ_LEN = 1024
        BATCH = 4
        NUM_SCALES = (24.0, 720.0)
        key = jax.random.key(seed)
        ks = jax.random.split(key, 8)
        d = EMBED_DIM
        x = jax.random.normal(ks[0], (BATCH, SEQ_LEN, d), dtype=jnp.float32)
        s = 1.0 / math.sqrt(d)
        Wq = jax.random.uniform(ks[1], (d, d), jnp.float32, -s, s)
        bq = jax.random.uniform(ks[2], (d,), jnp.float32, -s, s)
        Wk = jax.random.uniform(ks[3], (d, d), jnp.float32, -s, s)
        bk = jax.random.uniform(ks[4], (d,), jnp.float32, -s, s)
        Wv = jax.random.uniform(ks[5], (d, d), jnp.float32, -s, s)
        bv = jax.random.uniform(ks[6], (d,), jnp.float32, -s, s)
        beta = jnp.ones((len(NUM_SCALES),), dtype=jnp.float32)
        return {'x': x, 'Wq': Wq, 'bq': bq, 'Wk': Wk, 'bk': bk, 'Wv': Wv, 'bv': bv, 'beta': beta}
    _L2_attn_all = _L2_attn_setup()
    _L2_attn_in = {k: v for k, v in _L2_attn_all.items() if k in ('Wq', 'bq', 'Wk', 'bk', 'Wv', 'bv', 'beta')}
    del _L2_attn_all

    def _L2_ffn_setup():
        import jax, jax.numpy as jnp
        import numpy as np
        B, T, IN_DIM = (64, 64, 64)
        HID, OUT_DIM = (128, 64)
        N_LAYERS, N_EXPERTS, N_SHARED = (2, 16, 1)
        key = jax.random.key(seed)
        ks = jax.random.split(key, 10)
        s = 0.02
        x = jax.random.normal(ks[0], (B, T, IN_DIM), dtype=jnp.float32)
        route_id = jax.random.randint(ks[1], (B,), 0, N_EXPERTS)
        Wi = jax.random.normal(ks[2], (HID, IN_DIM), dtype=jnp.float32) * s
        bi = jnp.zeros((HID,), dtype=jnp.float32)
        Wr = jax.random.normal(ks[3], (N_LAYERS, N_EXPERTS, HID, HID), dtype=jnp.float32) * s
        br = jax.random.normal(ks[4], (N_LAYERS, N_EXPERTS, HID), dtype=jnp.float32) * s
        Ws = jax.random.normal(ks[5], (N_LAYERS, N_SHARED, HID, HID), dtype=jnp.float32) * s
        bs = jax.random.normal(ks[6], (N_LAYERS, N_SHARED, HID), dtype=jnp.float32) * s
        Wo = jax.random.normal(ks[7], (OUT_DIM, HID), dtype=jnp.float32) * s
        bo = jnp.zeros((OUT_DIM,), dtype=jnp.float32)
        return {'x': x, 'route_id': route_id, 'Wi': Wi, 'bi': bi, 'Wr': Wr, 'br': br, 'Ws': Ws, 'bs': bs, 'Wo': Wo, 'bo': bo}
    _L2_ffn_all = _L2_ffn_setup()
    _L2_ffn_in = {k: v for k, v in _L2_ffn_all.items() if k in ('route_id', 'Wi', 'bi', 'Wr', 'br', 'Ws', 'bs', 'Wo', 'bo')}
    del _L2_ffn_all

    def _L3_attn_setup():
        import jax, jax.numpy as jnp
        import numpy as np
        D_MODEL = 64
        D_STATE = 16
        D_CONV = 4
        EXPAND = 2
        D_INNER = EXPAND * D_MODEL
        DT_RANK = (D_MODEL + 15) // 16
        B_SZ = 4
        SEQ = 1024

        def _mamba_params(key, prefix):
            ks = jax.random.split(key, 6)
            s = 0.02
            return {f'{prefix}_in_w': jax.random.normal(ks[0], (2 * D_INNER, D_MODEL), dtype=jnp.float32) * s, f'{prefix}_conv_w': jax.random.normal(ks[1], (D_INNER, D_CONV), dtype=jnp.float32) * s, f'{prefix}_conv_b': jnp.zeros((D_INNER,), dtype=jnp.float32), f'{prefix}_xproj_w': jax.random.normal(ks[2], (DT_RANK + 2 * D_STATE, D_INNER), dtype=jnp.float32) * s, f'{prefix}_dt_w': jax.random.normal(ks[3], (D_INNER, DT_RANK), dtype=jnp.float32) * s, f'{prefix}_dt_b': jax.random.normal(ks[4], (D_INNER,), dtype=jnp.float32) * s, f'{prefix}_A_log': jnp.log(jnp.tile(jnp.arange(1, D_STATE + 1, dtype=jnp.float32), (D_INNER, 1))), f'{prefix}_D': jnp.ones((D_INNER,), dtype=jnp.float32), f'{prefix}_out_w': jax.random.normal(ks[5], (D_MODEL, D_INNER), dtype=jnp.float32) * s}

        def _mamba(x, in_w, conv_w, conv_b, xproj_w, dt_w, dt_b, A_log, D_param, out_w):
            Bn, L, _ = x.shape
            xz = x @ in_w.T
            xin, z = jnp.split(xz, 2, axis=-1)
            lhs = xin.swapaxes(1, 2)
            rhs = conv_w[:, None, :]
            conv = jax.lax.conv_general_dilated(lhs, rhs, (1,), [(D_CONV - 1, 0)], dimension_numbers=('NCL', 'OIL', 'NCL'), feature_group_count=D_INNER)
            xc = jax.nn.silu(conv.swapaxes(1, 2) + conv_b)
            x_dbl = xc @ xproj_w.T
            dt_low = x_dbl[..., :DT_RANK]
            Bm = x_dbl[..., DT_RANK:DT_RANK + D_STATE]
            Cm = x_dbl[..., DT_RANK + D_STATE:]
            dt = jax.nn.softplus(dt_low @ dt_w.T + dt_b)
            A = -jnp.exp(A_log)

            def step(h, inps):
                dt_t, B_t, C_t, u_t = inps
                dA = jnp.exp(dt_t[:, :, None] * A)
                h = dA * h + dt_t[:, :, None] * B_t[:, None, :] * u_t[:, :, None]
                y = jnp.einsum('bdn,bn->bd', h, C_t)
                return (h, y)
            h0 = jnp.zeros((Bn, D_INNER, D_STATE), dtype=x.dtype)
            xs = (dt.swapaxes(0, 1), Bm.swapaxes(0, 1), Cm.swapaxes(0, 1), xc.swapaxes(0, 1))
            _, ys = jax.lax.scan(step, h0, xs)
            y = ys.swapaxes(0, 1) + D_param * xc
            y = y * jax.nn.silu(z)
            return y @ out_w.T
        key = jax.random.key(seed)
        k1, k2, k3 = jax.random.split(key, 3)
        inp = {'g_data': jax.random.normal(k1, (B_SZ, SEQ, D_MODEL), dtype=jnp.float32)}
        inp.update(_mamba_params(k2, 'f'))
        inp.update(_mamba_params(k3, 'b'))
        return inp
    _L3_attn_all = _L3_attn_setup()
    _L3_attn_in = {k: v for k, v in _L3_attn_all.items() if k in ('f_in_w', 'f_conv_w', 'f_conv_b', 'f_xproj_w', 'f_dt_w', 'f_dt_b', 'f_A_log', 'f_D', 'f_out_w', 'b_in_w', 'b_conv_w', 'b_conv_b', 'b_xproj_w', 'b_dt_w', 'b_dt_b', 'b_A_log', 'b_D', 'b_out_w')}
    del _L3_attn_all

    def _L3_ffn_setup():
        import jax, jax.numpy as jnp
        import numpy as np
        BN_EPS = 0.001

        def _bn(h, g, b, m, v):
            return g * (h - m) * jax.lax.rsqrt(v + BN_EPS) + b
        key = jax.random.key(seed)
        ks = jax.random.split(key, 8)
        B, F, Df = (64, 64, 64)
        E, H, D = (8, 64, 64)
        s1 = 1.0 / np.sqrt(Df)
        s2 = 1.0 / np.sqrt(H)
        return {'x': jax.random.normal(ks[0], (B, F, Df), jnp.float32), 'Wr': jax.random.normal(ks[1], (Df, E), jnp.float32) * s1, 'br': jnp.zeros((E,), jnp.float32), 'W1': jax.random.normal(ks[2], (E, Df, H), jnp.float32) * s1, 'b1': jnp.zeros((E, H), jnp.float32), 'g1': jnp.ones((E, H), jnp.float32), 'be1': jnp.zeros((E, H), jnp.float32), 'm1': jnp.zeros((E, H), jnp.float32), 'v1': jnp.ones((E, H), jnp.float32), 'W2': jax.random.normal(ks[3], (E, H, H), jnp.float32) * s2, 'b2': jnp.zeros((E, H), jnp.float32), 'g2': jnp.ones((E, H), jnp.float32), 'be2': jnp.zeros((E, H), jnp.float32), 'm2': jnp.zeros((E, H), jnp.float32), 'v2': jnp.ones((E, H), jnp.float32), 'Wo': jax.random.normal(ks[4], (E, H, D), jnp.float32) * s2, 'bo': jnp.zeros((E, D), jnp.float32)}
    _L3_ffn_all = _L3_ffn_setup()
    _L3_ffn_in = {k: v for k, v in _L3_ffn_all.items() if k in ('Wr', 'br', 'W1', 'b1', 'g1', 'be1', 'm1', 'v1', 'W2', 'b2', 'g2', 'be2', 'm2', 'v2', 'Wo', 'bo')}
    del _L3_ffn_all
    return {'x': x, 'L0_tok_W': _L0_tok_in['W'], 'L0_attn_gamma': _L0_attn_in['gamma'], 'L0_attn_beta': _L0_attn_in['beta'], 'L0_attn_Wq': _L0_attn_in['Wq'], 'L0_attn_Wk': _L0_attn_in['Wk'], 'L0_attn_Wv': _L0_attn_in['Wv'], 'L0_attn_Wg': _L0_attn_in['Wg'], 'L0_attn_bg': _L0_attn_in['bg'], 'L0_attn_Wo': _L0_attn_in['Wo'], 'L0_attn_bo': _L0_attn_in['bo'], 'L0_ffn_gate_w': _L0_ffn_in['gate_w'], 'L0_ffn_gate_b': _L0_ffn_in['gate_b'], 'L0_ffn_W1': _L0_ffn_in['W1'], 'L0_ffn_b1': _L0_ffn_in['b1'], 'L0_ffn_W2': _L0_ffn_in['W2'], 'L0_ffn_b2': _L0_ffn_in['b2'], 'L1_attn_Wq': _L1_attn_in['Wq'], 'L1_attn_Wk': _L1_attn_in['Wk'], 'L1_attn_Wv': _L1_attn_in['Wv'], 'L1_attn_Wo': _L1_attn_in['Wo'], 'L1_attn_bo': _L1_attn_in['bo'], 'L1_ffn_gamma': _L1_ffn_in['gamma'], 'L1_ffn_beta': _L1_ffn_in['beta'], 'L1_ffn_Wr': _L1_ffn_in['Wr'], 'L1_ffn_br': _L1_ffn_in['br'], 'L1_ffn_W1': _L1_ffn_in['W1'], 'L1_ffn_b1': _L1_ffn_in['b1'], 'L1_ffn_W2': _L1_ffn_in['W2'], 'L1_ffn_b2': _L1_ffn_in['b2'], 'L2_attn_Wq': _L2_attn_in['Wq'], 'L2_attn_bq': _L2_attn_in['bq'], 'L2_attn_Wk': _L2_attn_in['Wk'], 'L2_attn_bk': _L2_attn_in['bk'], 'L2_attn_Wv': _L2_attn_in['Wv'], 'L2_attn_bv': _L2_attn_in['bv'], 'L2_attn_beta': _L2_attn_in['beta'], 'L2_ffn_route_id': _L2_ffn_in['route_id'], 'L2_ffn_Wi': _L2_ffn_in['Wi'], 'L2_ffn_bi': _L2_ffn_in['bi'], 'L2_ffn_Wr': _L2_ffn_in['Wr'], 'L2_ffn_br': _L2_ffn_in['br'], 'L2_ffn_Ws': _L2_ffn_in['Ws'], 'L2_ffn_bs': _L2_ffn_in['bs'], 'L2_ffn_Wo': _L2_ffn_in['Wo'], 'L2_ffn_bo': _L2_ffn_in['bo'], 'L3_attn_f_in_w': _L3_attn_in['f_in_w'], 'L3_attn_f_conv_w': _L3_attn_in['f_conv_w'], 'L3_attn_f_conv_b': _L3_attn_in['f_conv_b'], 'L3_attn_f_xproj_w': _L3_attn_in['f_xproj_w'], 'L3_attn_f_dt_w': _L3_attn_in['f_dt_w'], 'L3_attn_f_dt_b': _L3_attn_in['f_dt_b'], 'L3_attn_f_A_log': _L3_attn_in['f_A_log'], 'L3_attn_f_D': _L3_attn_in['f_D'], 'L3_attn_f_out_w': _L3_attn_in['f_out_w'], 'L3_attn_b_in_w': _L3_attn_in['b_in_w'], 'L3_attn_b_conv_w': _L3_attn_in['b_conv_w'], 'L3_attn_b_conv_b': _L3_attn_in['b_conv_b'], 'L3_attn_b_xproj_w': _L3_attn_in['b_xproj_w'], 'L3_attn_b_dt_w': _L3_attn_in['b_dt_w'], 'L3_attn_b_dt_b': _L3_attn_in['b_dt_b'], 'L3_attn_b_A_log': _L3_attn_in['b_A_log'], 'L3_attn_b_D': _L3_attn_in['b_D'], 'L3_attn_b_out_w': _L3_attn_in['b_out_w'], 'L3_ffn_Wr': _L3_ffn_in['Wr'], 'L3_ffn_br': _L3_ffn_in['br'], 'L3_ffn_W1': _L3_ffn_in['W1'], 'L3_ffn_b1': _L3_ffn_in['b1'], 'L3_ffn_g1': _L3_ffn_in['g1'], 'L3_ffn_be1': _L3_ffn_in['be1'], 'L3_ffn_m1': _L3_ffn_in['m1'], 'L3_ffn_v1': _L3_ffn_in['v1'], 'L3_ffn_W2': _L3_ffn_in['W2'], 'L3_ffn_b2': _L3_ffn_in['b2'], 'L3_ffn_g2': _L3_ffn_in['g2'], 'L3_ffn_be2': _L3_ffn_in['be2'], 'L3_ffn_m2': _L3_ffn_in['m2'], 'L3_ffn_v2': _L3_ffn_in['v2'], 'L3_ffn_Wo': _L3_ffn_in['Wo'], 'L3_ffn_bo': _L3_ffn_in['bo']}

def reference(x, L0_tok_W, L0_attn_gamma, L0_attn_beta, L0_attn_Wq, L0_attn_Wk, L0_attn_Wv, L0_attn_Wg, L0_attn_bg, L0_attn_Wo, L0_attn_bo, L0_ffn_gate_w, L0_ffn_gate_b, L0_ffn_W1, L0_ffn_b1, L0_ffn_W2, L0_ffn_b2, L1_attn_Wq, L1_attn_Wk, L1_attn_Wv, L1_attn_Wo, L1_attn_bo, L1_ffn_gamma, L1_ffn_beta, L1_ffn_Wr, L1_ffn_br, L1_ffn_W1, L1_ffn_b1, L1_ffn_W2, L1_ffn_b2, L2_attn_Wq, L2_attn_bq, L2_attn_Wk, L2_attn_bk, L2_attn_Wv, L2_attn_bv, L2_attn_beta, L2_ffn_route_id, L2_ffn_Wi, L2_ffn_bi, L2_ffn_Wr, L2_ffn_br, L2_ffn_Ws, L2_ffn_bs, L2_ffn_Wo, L2_ffn_bo, L3_attn_f_in_w, L3_attn_f_conv_w, L3_attn_f_conv_b, L3_attn_f_xproj_w, L3_attn_f_dt_w, L3_attn_f_dt_b, L3_attn_f_A_log, L3_attn_f_D, L3_attn_f_out_w, L3_attn_b_in_w, L3_attn_b_conv_w, L3_attn_b_conv_b, L3_attn_b_xproj_w, L3_attn_b_dt_w, L3_attn_b_dt_b, L3_attn_b_A_log, L3_attn_b_D, L3_attn_b_out_w, L3_ffn_Wr, L3_ffn_br, L3_ffn_W1, L3_ffn_b1, L3_ffn_g1, L3_ffn_be1, L3_ffn_m1, L3_ffn_v1, L3_ffn_W2, L3_ffn_b2, L3_ffn_g2, L3_ffn_be2, L3_ffn_m2, L3_ffn_v2, L3_ffn_Wo, L3_ffn_bo):
    import jax
    import jax.numpy as jnp

    def _L0_tok_ref(x, W):
        import jax, jax.numpy as jnp
        import numpy as np
        VOCAB = 50257
        DIM = 64

        def _positional_table(seq_len, dim, dtype=jnp.float32):
            pos = jnp.arange(seq_len, dtype=dtype)[:, None]
            d = jnp.arange(dim)
            exponent = (d - d % 2).astype(dtype) / dim
            inv_freq = jnp.power(jnp.asarray(10000.0, dtype), -exponent)
            angle = pos * inv_freq
            return jnp.where(d % 2 == 0, jnp.sin(angle), jnp.cos(angle))
        seq_len = x.shape[1]
        pe = _positional_table(seq_len, W.shape[1], W.dtype)
        return W[x] + pe[None, :, :]

    def _L0_attn_ref(m, gamma, beta, Wq, Wk, Wv, Wg, bg, Wo, bo):
        import jax, jax.numpy as jnp
        import numpy as np
        import math
        N_SEQ, L_RES, D_MODEL = (128, 96, 64)
        N_HEAD, C_HEAD = (8, 32)
        EPS = 1e-05
        N, L, D = m.shape
        H, C = (N_HEAD, C_HEAD)
        mu = jnp.mean(m, axis=-1, keepdims=True)
        var = jnp.mean(jnp.square(m - mu), axis=-1, keepdims=True)
        mn = (m - mu) * jax.lax.rsqrt(var + EPS) * gamma + beta
        q = (mn @ Wq).reshape(N, L, H, C)
        k = (mn @ Wk).reshape(N, L, H, C)
        v = (mn @ Wv).reshape(N, L, H, C)
        g = jax.nn.sigmoid(mn @ Wg + bg).reshape(N, L, H, C)
        scale = 1.0 / math.sqrt(C) / math.sqrt(L)
        att = jnp.einsum('slhc,tlhc->sth', q, k) * scale
        att = jax.nn.softmax(att, axis=1)
        o = jnp.einsum('sth,tlhc->slhc', att, v) * g
        return o.reshape(N, L, H * C) @ Wo + bo

    def _L0_ffn_ref(x, gate_w, gate_b, W1, b1, W2, b2):
        import jax, jax.numpy as jnp
        import numpy as np
        B, T, D, H, E = (16, 1024, 64, 128, 8)
        Bb, Tt, Dd = x.shape
        Ee = gate_w.shape[1]
        xf = x.reshape(-1, Dd)
        N = xf.shape[0]
        logits = xf @ gate_w + gate_b
        probs = jax.nn.softmax(logits, axis=-1)
        top2_vals, top2_idx = jax.lax.top_k(probs, 2)
        cw = jnp.zeros((N, Ee), dtype=xf.dtype).at[jnp.arange(N)[:, None], top2_idx].add(top2_vals)

        def step(acc, params):
            w1, bb1, w2, bb2, we = params
            h = jax.nn.gelu(xf @ w1 + bb1, approximate=False)
            y = h @ w2 + bb2
            return (acc + we[:, None] * y, None)
        out, _ = jax.lax.scan(step, jnp.zeros_like(xf), (W1, b1, W2, b2, cw.T))
        return out.reshape(Bb, Tt, Dd)

    def _L1_attn_ref(x, Wq, Wk, Wv, Wo, bo):
        import jax, jax.numpy as jnp
        import numpy as np
        import math
        NUM_HEADS = 8
        HEAD_SIZE = 32

        def get_alibi_slopes(n_heads):

            def pow2_slopes(n):
                start = 2.0 ** (-2.0 ** (-(math.log2(n) - 3)))
                ratio = start
                return [start * ratio ** i for i in range(n)]
            if math.log2(n_heads).is_integer():
                return np.array(pow2_slopes(n_heads), dtype=np.float32)
            cp2 = 2 ** math.floor(math.log2(n_heads))
            extra = pow2_slopes(2 * cp2)[0::2][:n_heads - cp2]
            return np.array(pow2_slopes(cp2) + extra, dtype=np.float32)
        ALIBI_SLOPES = jnp.asarray(get_alibi_slopes(NUM_HEADS))
        B, T, C = x.shape
        H, D = (NUM_HEADS, HEAD_SIZE)
        q = (x @ Wq).reshape(B, T, H, D).transpose(0, 2, 1, 3)
        k = (x @ Wk).reshape(B, T, H, D).transpose(0, 2, 1, 3)
        v = (x @ Wv).reshape(B, T, H, D).transpose(0, 2, 1, 3)
        scale = 1.0 / math.sqrt(D)
        wei = jnp.einsum('bhtd,bhsd->bhts', q, k) * scale
        pos = jnp.arange(T)
        rel = (pos[None, :] - pos[:, None]).astype(jnp.float32)
        bias = ALIBI_SLOPES[:, None, None] * rel[None, :, :]
        wei = wei + bias[None]
        causal = pos[None, :] <= pos[:, None]
        wei = jnp.where(causal[None, None], wei, -jnp.inf)
        wei = jax.nn.softmax(wei, axis=-1)
        out = jnp.einsum('bhts,bhsd->bhtd', wei, v)
        out = out.transpose(0, 2, 1, 3).reshape(B, T, H * D)
        return out @ Wo + bo

    def _L1_ffn_ref(x, gamma, beta, Wr, br, W1, b1, W2, b2):
        import jax, jax.numpy as jnp
        import numpy as np
        E = 8
        K = 2
        D = 64
        H = 128
        DOUT = 64
        EPS = 1e-05
        mu = jnp.mean(x, axis=-1, keepdims=True)
        var = jnp.mean(jnp.square(x - mu), axis=-1, keepdims=True)
        xn = (x - mu) * jax.lax.rsqrt(var + EPS) * gamma + beta
        logits = jnp.einsum('bsd,de->bse', xn, Wr) + br
        top_vals, top_idx = jax.lax.top_k(logits, K)
        w = jax.nn.softmax(top_vals, axis=-1)
        w_full = jnp.einsum('bsk,bske->bse', w, jax.nn.one_hot(top_idx, E, dtype=w.dtype))
        y = jnp.zeros(x.shape[:-1] + (DOUT,), x.dtype)
        for e in range(E):
            h = jax.nn.gelu(jnp.einsum('bsd,dh->bsh', xn, W1[e]) + b1[e], approximate=False)
            y_e = jnp.einsum('bsh,hd->bsd', h, W2[e]) + b2[e]
            y = y + y_e * w_full[..., e, None]
        return y

    def _L2_attn_ref(x, Wq, bq, Wk, bk, Wv, bv, beta):
        import jax, jax.numpy as jnp
        import numpy as np
        import math
        EMBED_DIM = 64
        SEQ_LEN = 1024
        BATCH = 4
        NUM_SCALES = (24.0, 720.0)
        d = x.shape[-1]
        seq_len = x.shape[1]
        sqrt_d = jnp.asarray(math.sqrt(d), x.dtype)
        Q = jnp.einsum('bsd,ed->bse', x, Wq) + bq
        K = jnp.einsum('bsd,ed->bse', x, Wk) + bk
        V = jnp.einsum('bsd,ed->bse', x, Wv) + bv
        attn = jnp.einsum('bse,bte->bst', Q, K) / sqrt_d
        idx = jnp.arange(seq_len, dtype=jnp.float32)
        absdiff = jnp.abs(idx[:, None] - idx[None, :])
        two_pi = jnp.asarray(2.0 * math.pi, jnp.float32)
        bias = jnp.zeros((seq_len, seq_len), dtype=jnp.float32)
        for n, T in enumerate(NUM_SCALES):
            bias = bias + beta[n] * jnp.cos(two_pi * absdiff / T)
        scores = jax.nn.softmax(attn + bias[None, :, :], axis=-1)
        return jnp.einsum('bst,bte->bse', scores, V)

    def _L2_ffn_ref(x, route_id, Wi, bi, Wr, br, Ws, bs, Wo, bo):
        import jax, jax.numpy as jnp
        import numpy as np
        B, T, IN_DIM = (64, 64, 64)
        HID, OUT_DIM = (128, 64)
        N_LAYERS, N_EXPERTS, N_SHARED = (2, 16, 1)
        flat = x.reshape(-1, x.shape[-1])
        n_tok = flat.shape[0]
        route = jnp.repeat(route_id, n_tok // route_id.shape[0])
        h = jax.nn.relu(flat @ Wi.T + bi)
        n_layers, n_experts = (Wr.shape[0], Wr.shape[1])
        for l in range(n_layers):
            shared = (jnp.einsum('nd,shd->snh', h, Ws[l]) + bs[l][:, None, :]).mean(axis=0)
            routed = jnp.zeros_like(h)
            for e in range(n_experts):
                ye = h @ Wr[l, e].T + br[l, e]
                routed = routed + jnp.where((route == e)[:, None], ye, 0.0)
            h = jax.nn.relu(shared + routed + h)
        out = h @ Wo.T + bo
        return out.reshape(*x.shape[:-1], out.shape[-1])

    def _L3_attn_ref(g_data, f_in_w, f_conv_w, f_conv_b, f_xproj_w, f_dt_w, f_dt_b, f_A_log, f_D, f_out_w, b_in_w, b_conv_w, b_conv_b, b_xproj_w, b_dt_w, b_dt_b, b_A_log, b_D, b_out_w):
        import jax, jax.numpy as jnp
        import numpy as np
        D_MODEL = 64
        D_STATE = 16
        D_CONV = 4
        EXPAND = 2
        D_INNER = EXPAND * D_MODEL
        DT_RANK = (D_MODEL + 15) // 16
        B_SZ = 4
        SEQ = 1024

        def _mamba_params(key, prefix):
            ks = jax.random.split(key, 6)
            s = 0.02
            return {f'{prefix}_in_w': jax.random.normal(ks[0], (2 * D_INNER, D_MODEL), dtype=jnp.float32) * s, f'{prefix}_conv_w': jax.random.normal(ks[1], (D_INNER, D_CONV), dtype=jnp.float32) * s, f'{prefix}_conv_b': jnp.zeros((D_INNER,), dtype=jnp.float32), f'{prefix}_xproj_w': jax.random.normal(ks[2], (DT_RANK + 2 * D_STATE, D_INNER), dtype=jnp.float32) * s, f'{prefix}_dt_w': jax.random.normal(ks[3], (D_INNER, DT_RANK), dtype=jnp.float32) * s, f'{prefix}_dt_b': jax.random.normal(ks[4], (D_INNER,), dtype=jnp.float32) * s, f'{prefix}_A_log': jnp.log(jnp.tile(jnp.arange(1, D_STATE + 1, dtype=jnp.float32), (D_INNER, 1))), f'{prefix}_D': jnp.ones((D_INNER,), dtype=jnp.float32), f'{prefix}_out_w': jax.random.normal(ks[5], (D_MODEL, D_INNER), dtype=jnp.float32) * s}

        def _mamba(x, in_w, conv_w, conv_b, xproj_w, dt_w, dt_b, A_log, D_param, out_w):
            Bn, L, _ = x.shape
            xz = x @ in_w.T
            xin, z = jnp.split(xz, 2, axis=-1)
            lhs = xin.swapaxes(1, 2)
            rhs = conv_w[:, None, :]
            conv = jax.lax.conv_general_dilated(lhs, rhs, (1,), [(D_CONV - 1, 0)], dimension_numbers=('NCL', 'OIL', 'NCL'), feature_group_count=D_INNER)
            xc = jax.nn.silu(conv.swapaxes(1, 2) + conv_b)
            x_dbl = xc @ xproj_w.T
            dt_low = x_dbl[..., :DT_RANK]
            Bm = x_dbl[..., DT_RANK:DT_RANK + D_STATE]
            Cm = x_dbl[..., DT_RANK + D_STATE:]
            dt = jax.nn.softplus(dt_low @ dt_w.T + dt_b)
            A = -jnp.exp(A_log)

            def step(h, inps):
                dt_t, B_t, C_t, u_t = inps
                dA = jnp.exp(dt_t[:, :, None] * A)
                h = dA * h + dt_t[:, :, None] * B_t[:, None, :] * u_t[:, :, None]
                y = jnp.einsum('bdn,bn->bd', h, C_t)
                return (h, y)
            h0 = jnp.zeros((Bn, D_INNER, D_STATE), dtype=x.dtype)
            xs = (dt.swapaxes(0, 1), Bm.swapaxes(0, 1), Cm.swapaxes(0, 1), xc.swapaxes(0, 1))
            _, ys = jax.lax.scan(step, h0, xs)
            y = ys.swapaxes(0, 1) + D_param * xc
            y = y * jax.nn.silu(z)
            return y @ out_w.T
        fwd = _mamba(g_data, f_in_w, f_conv_w, f_conv_b, f_xproj_w, f_dt_w, f_dt_b, f_A_log, f_D, f_out_w)
        bwd = _mamba(jnp.flip(g_data, axis=-1), b_in_w, b_conv_w, b_conv_b, b_xproj_w, b_dt_w, b_dt_b, b_A_log, b_D, b_out_w)
        return fwd + jnp.flip(bwd, axis=-1) + g_data

    def _L3_ffn_ref(x, Wr, br, W1, b1, g1, be1, m1, v1, W2, b2, g2, be2, m2, v2, Wo, bo):
        import jax, jax.numpy as jnp
        import numpy as np
        BN_EPS = 0.001

        def _bn(h, g, b, m, v):
            return g * (h - m) * jax.lax.rsqrt(v + BN_EPS) + b
        feat = jnp.mean(x, axis=0)
        w = jax.nn.softmax(feat @ Wr + br, axis=-1)
        h = jnp.einsum('bfd,edh->bfeh', x, W1) + b1
        h = jax.nn.relu(_bn(h, g1, be1, m1, v1))
        h = jnp.einsum('bfeh,ehk->bfek', h, W2) + b2
        h = jax.nn.relu(_bn(h, g2, be2, m2, v2))
        y = jnp.einsum('bfeh,ehd->bfed', h, Wo) + bo
        return jnp.einsum('bfed,fe->bfd', y, w)
    h = _L0_tok_ref(x, L0_tok_W)
    h = h + _L0_attn_ref(_layernorm(h, axis=-1), L0_attn_gamma, L0_attn_beta, L0_attn_Wq, L0_attn_Wk, L0_attn_Wv, L0_attn_Wg, L0_attn_bg, L0_attn_Wo, L0_attn_bo)
    h = h + _L0_ffn_ref(_layernorm(h, axis=-1), L0_ffn_gate_w, L0_ffn_gate_b, L0_ffn_W1, L0_ffn_b1, L0_ffn_W2, L0_ffn_b2)
    h = h + _L1_attn_ref(_layernorm(h, axis=-1), L1_attn_Wq, L1_attn_Wk, L1_attn_Wv, L1_attn_Wo, L1_attn_bo)
    h = h + _L1_ffn_ref(_layernorm(h, axis=-1), L1_ffn_gamma, L1_ffn_beta, L1_ffn_Wr, L1_ffn_br, L1_ffn_W1, L1_ffn_b1, L1_ffn_W2, L1_ffn_b2)
    h = h + _L2_attn_ref(_layernorm(h, axis=-1), L2_attn_Wq, L2_attn_bq, L2_attn_Wk, L2_attn_bk, L2_attn_Wv, L2_attn_bv, L2_attn_beta)
    h = h + _L2_ffn_ref(_layernorm(h, axis=-1), L2_ffn_route_id, L2_ffn_Wi, L2_ffn_bi, L2_ffn_Wr, L2_ffn_br, L2_ffn_Ws, L2_ffn_bs, L2_ffn_Wo, L2_ffn_bo)
    h = h + _L3_attn_ref(_layernorm(h, axis=-1), L3_attn_f_in_w, L3_attn_f_conv_w, L3_attn_f_conv_b, L3_attn_f_xproj_w, L3_attn_f_dt_w, L3_attn_f_dt_b, L3_attn_f_A_log, L3_attn_f_D, L3_attn_f_out_w, L3_attn_b_in_w, L3_attn_b_conv_w, L3_attn_b_conv_b, L3_attn_b_xproj_w, L3_attn_b_dt_w, L3_attn_b_dt_b, L3_attn_b_A_log, L3_attn_b_D, L3_attn_b_out_w)
    h = h + _L3_ffn_ref(_layernorm(h, axis=-1), L3_ffn_Wr, L3_ffn_br, L3_ffn_W1, L3_ffn_b1, L3_ffn_g1, L3_ffn_be1, L3_ffn_m1, L3_ffn_v1, L3_ffn_W2, L3_ffn_b2, L3_ffn_g2, L3_ffn_be2, L3_ffn_m2, L3_ffn_v2, L3_ffn_Wo, L3_ffn_bo)
    return h

_drawn_inputs = setup_inputs


def setup_inputs(seed=0):
    import zlib

    import numpy as np

    out = dict(_drawn_inputs(seed))
    spreads = {'L0_attn_gamma': (1.0, 0.2),
     'L0_attn_beta': (0.0, 0.1),
     'L0_attn_bg': (0.0, 0.348),
     'L0_attn_bo': (0.0, 0.1),
     'L0_ffn_gate_b': (0.0, 0.58),
     'L0_ffn_b1': (0.0, 0.8),
     'L0_ffn_b2': (0.0, 0.471),
     'L1_ffn_br': (0.0, 0.75),
     'L2_attn_beta': (1.0, 0.6),
     'L2_ffn_bi': (0.0, 0.8),
     'L2_ffn_bo': (0.0, 0.8),
     'L3_attn_f_conv_b': (0.0, 0.8),
     'L3_attn_f_D': (1.0, 0.6),
     'L3_attn_b_conv_b': (0.0, 0.8),
     'L3_attn_b_D': (1.0, 0.6),
     'L3_ffn_br': (0.0, 0.8),
     'L3_ffn_b1': (0.0, 2.0),
     'L3_ffn_g1': (1.0, 0.6),
     'L3_ffn_be1': (0.0, 2.0),
     'L3_ffn_m1': (0.0, 2.0),
     'L3_ffn_v1': (1.0, 0.6),
     'L3_ffn_b2': (0.0, 2.0),
     'L3_ffn_g2': (1.0, 0.6),
     'L3_ffn_be2': (0.0, 2.0),
     'L3_ffn_m2': (0.0, 2.0),
     'L3_ffn_v2': (1.0, 0.6),
     'L3_ffn_bo': (0.0, 2.0)}
    factors = {'L0_ffn_gate_w': 4.611,
     'L0_ffn_W1': 8.0,
     'L0_ffn_W2': 8.0,
     'L1_attn_bo': 8.0,
     'L1_ffn_gamma': 8.0,
     'L1_ffn_beta': 8.0,
     'L1_ffn_Wr': 7.407,
     'L1_ffn_W1': 7.528,
     'L1_ffn_b1': 28.646,
     'L1_ffn_W2': 7.625,
     'L1_ffn_b2': 35.785,
     'L2_attn_Wq': 3.626,
     'L2_attn_bq': 38.238,
     'L2_attn_Wk': 3.311,
     'L2_attn_bk': 64.0,
     'L2_ffn_Wi': 5.175,
     'L2_ffn_Wr': 8.0,
     'L2_ffn_br': 25.897,
     'L2_ffn_Ws': 8.0,
     'L2_ffn_bs': 25.299,
     'L2_ffn_Wo': 3.105,
     'L3_attn_f_in_w': 8.0,
     'L3_attn_f_conv_w': 8.0,
     'L3_attn_f_xproj_w': 8.0,
     'L3_attn_f_dt_w': 64.0,
     'L3_attn_f_dt_b': 64.0,
     'L3_attn_f_A_log': 8.0,
     'L3_attn_f_out_w': 8.0,
     'L3_attn_b_in_w': 8.0,
     'L3_attn_b_conv_w': 8.0,
     'L3_attn_b_xproj_w': 8.0,
     'L3_attn_b_dt_w': 25.798,
     'L3_attn_b_dt_b': 39.047,
     'L3_attn_b_A_log': 55.774,
     'L3_attn_b_out_w': 8.0,
     'L2_attn_bv': 7.377}
    for name, (base, spread) in spreads.items():
        noise = np.random.default_rng([zlib.crc32(name.encode()), seed]).standard_normal(out[name].shape)
        drawn = base * np.exp(spread * noise) if base else spread * noise
        out[name] = jnp.asarray(drawn.astype(out[name].dtype))
    for name, factor in factors.items():
        out[name] = (out[name] * factor).astype(out[name].dtype)
    return out
```

```python
from contextlib import ExitStack, contextmanager

import numpy as np
import concourse.bass as bass
from concourse import mybir

ALU = mybir.AluOpType
ACT = mybir.ActivationFunctionType
F32 = mybir.dt.float32
BF16 = mybir.dt.bfloat16
I32 = mybir.dt.int32
U32 = mybir.dt.uint32
X = mybir.AxisListType.X

P = 128
B = 128
T = 128
D = 64
G = 4
COLS = G * P
TILES = B // G
EPS = 1e-5
NE = 8
HID = 128
HD = 256
NH, CH = 8, 32


@contextmanager
def semaphores(nc, prefix):
    taken = []

    def sem(name):
        taken.append(nc.alloc_semaphore(name=f"{prefix}_{name}"))
        return taken[-1]

    yield sem
    nc.clear_and_free_semaphores(taken)
    nc.all_engine_barrier()


class Chain:

    def __init__(self, eng, sem, n, per):
        self.eng, self.sem, self.base, self.per, self.k = eng, sem, n * per, per, 0

    def __call__(self, ins):
        self.k += 1
        ins.then_inc(self.sem, 1)
        self.eng.wait_ge(self.sem, self.base + self.k)

    def end(self):
        assert self.k == self.per, (self.k, self.per)


def wait_reuse(eng, sem, count):
    if isinstance(count, int) and count <= 0:
        return
    eng.wait_ge(sem, count)


def pipeline(eng, stages, tiles):
    lag = len(stages) - 1

    def step(s, parity, full=False):
        for k, stage in enumerate(stages):
            if stage is not None and (full or 0 <= s - k < tiles):
                stage(s - k, (parity - k) % 2)

    first = lag + 2
    if (tiles - first) % 2:
        first += 1
    for s in range(first):
        step(s, s % 2)
    with eng.Fori(first, tiles - 1, 2) as s:
        step(s, first % 2, full=True)
        step(s + 1, (first + 1) % 2, full=True)
    for s in range(tiles, tiles + lag):
        step(s, s % 2)


def bc(ap, n):
    return ap.unsqueeze(len(ap.shape)).to_broadcast([*ap.shape, n])


def mid(ap, n):
    return ap.unsqueeze(1).to_broadcast([ap.shape[0], n, ap.shape[1]])


def norm_stats(eng, nc, chain, x, xc, sq, total, var):
    chain(nc.vector.tensor_reduce(total, x, X, ALU.add))
    chain(nc.vector.scalar_tensor_tensor(out=xc, in0=bc(total, D), scalar=-1.0 / D, in1=x,
                                         op0=ALU.mult, op1=ALU.add))
    chain(nc.vector.tensor_tensor(sq, xc, xc, ALU.mult))
    chain(nc.vector.tensor_reduce(total, sq, X, ALU.add))
    return nc.vector.tensor_scalar(var, total, 1.0 / D, EPS, ALU.mult, ALU.add)


def constants_A(c):
    pos = np.arange(T, dtype=np.float32)[:, None]
    d = np.arange(D)
    inv = np.power(np.float32(10000.0), -((d - d % 2).astype(np.float32) / np.float32(D))).astype(np.float32)
    angle = (pos * inv).astype(np.float32)
    c["positions"] = np.where(d % 2 == 0, np.sin(angle), np.cos(angle)).astype(np.float32)


def loads_A(nc, S, A, sb, load, zeroed):
    q = "L0_attn_"
    wqk = sb("A_wqk", [D, 2 * HD])
    load(wqk[:, 0:HD], A[q + "Wq"][:, :])
    load(wqk[:, HD:2 * HD], A[q + "Wk"][:, :])
    wvg = sb("A_wvg", [D + 1, 2 * HD])
    zeroed.append(wvg)
    load(wvg[0:D, 0:HD], A[q + "Wv"][:, :])
    load(wvg[0:D, HD:2 * HD], A[q + "Wg"][:, :])
    load(wvg[D:D + 1, HD:2 * HD], A[q + "bg"].rearrange("(a n) -> a n", a=1))
    load(sb("A_wo", [P, 2, D])[:], A[q + "Wo"].rearrange("(u p) d -> p u d", p=P))
    load(sb("A_bo", [P, D])[:, :], A[q + "bo"].rearrange("(a n) -> a n", a=1).to_broadcast([P, D]))
    for v in ("gamma", "beta"):
        two = sb("A_" + v, [2 * D, 1])
        for k in range(2):
            load(two[k * D:(k + 1) * D, :], A[q + v].rearrange("(d a) -> d a", a=1))
    load(sb("A_ids", [P, T], I32)[:, :], A["x"][:, :])


def column_attention(nc, S, A):
    h, ident = S["h"], S["ident"]
    SCALE = 1.0 / float(np.sqrt(CH)) / float(np.sqrt(T))
    with ExitStack() as ctx:
        def sb(name, shape, dt=F32):
            return ctx.enter_context(nc.sbuf_tensor(f"A_{name}", shape, dt))

        sem = ctx.enter_context(semaphores(nc, "A"))

        hs = sb("hs", [P, T, D])
        mnT = sb("mnT", [D, T * B])
        attT = sb("attT", [P, NH, P])

        with ExitStack() as c2:
            table = c2.enter_context(nc.sbuf_tensor("A_table", [P, T, D], F32))
            gathered, table_in, summed = sem("gathered"), sem("table_in"), sem("summed")
            with nc.Block() as block:
                @block.sync
                def _(sp):
                    sp.dma_start(table[:].rearrange("p t d -> p (t d)"),
                                 A["positions"].rearrange("t d -> (t d)").rearrange("(a n) -> a n", a=1).to_broadcast([P, T * D])).then_inc(table_in, 16)
                    sp.wait_ge(table_in, 16)

                @block.gpsimd
                def _(pool):
                    for t in range(T):
                        nc.gpsimd.indirect_dma_start(
                            out=hs[:, t, :], out_offset=None, in_=A["L0_tok_W"][:, :],
                            in_offset=bass.IndirectOffsetOnAxis(ap=S["A_ids"][:, t:t + 1].bitcast(U32), axis=0),
                        ).then_inc(gathered, 16)
                    pool.wait_ge(gathered, 16 * T)

                @block.vector
                def _(dve):
                    dve.wait_ge(gathered, 16 * T)
                    dve.wait_ge(table_in, 16)
                    nc.vector.tensor_tensor(hs[:], hs[:], table[:], ALU.add).then_inc(summed, 1)

        acc_ctx = ExitStack()
        acc = acc_ctx.enter_context(nc.psum_tensor("A_acc", [P, NH, P], F32))
        column_scores(nc, S, hs, mnT, acc)
        column_softmax(nc, S, acc, attT, SCALE)
        acc_ctx.close()
        column_values(nc, S, hs, mnT, attT)
        swap_axes(nc, S, hs)


def column_scores(nc, S, hs, mnT, acc):
    ident = S["ident"]
    with ExitStack() as ctx:
        def sb(name, shape, dt=F32):
            return ctx.enter_context(nc.sbuf_tensor(f"As_{name}", shape, dt))

        def ps(name, shape):
            return ctx.enter_context(nc.psum_tensor(f"As_{name}", shape, F32))

        sem = ctx.enter_context(semaphores(nc, "As"))

        xc = sb("xc", [P, G, D])
        sq = sb("sq", [P, G, D])
        total, var, rstd = sb("total", [P, G]), sb("var", [P, G]), sb("rstd", [P, G])
        xn = sb("xn", [P, 2, G, D])
        xT = sb("xT", [D, 2, COLS])
        qk = sb("qk", [P, 2, 2 * NH, G, CH])
        qkT = sb("qkT", [P, 2, 2 * NH, P])
        zero = sb("zero", [1, P])
        xT_ps = ps("xT_ps", [P, G // 2, P])
        tok_ps = ps("tok_ps", [P, 2, 2 * HD])
        turn_ps = ps("turn_ps", [P, 2, 4, P])
        stats_chain, var_ready, rstd_ready, xn_ready = sem("stats_chain"), sem("var_ready"), sem("rstd_ready"), sem("xn_ready")
        xT_ps_ready, xT_ready, kept = sem("xT_ps_ready"), sem("xT_ready"), sem("kept")
        tok_ps_ready, tok_a, tok_d = sem("tok_ps_ready"), sem("tok_a"), sem("tok_d")
        turn_ready, turned_a, turned_d = sem("turn_ready"), sem("turned_a"), sem("turned_d")
        scored, consts_set = sem("scored"), sem("consts_set")

        with nc.Block() as block:
            @block.vector
            def _(dve):
                nc.vector.memset(zero[:, :], 0.0).then_inc(consts_set, 1)

                def norm(n, p):
                    chain = Chain(dve, stats_chain, n, 8)
                    for m in range(2):
                        x = hs[:, bass.ds(n * G, G), :] if m == 0 else xn[:, p, :, :]
                        norm_stats(dve, nc, chain, x, xc[:, :, :], sq[:, :, :], total[:, :], var[:, :]).then_inc(var_ready, 1)
                        dve.wait_ge(rstd_ready, n * 2 + m + 1)
                        if m == 0:
                            wait_reuse(dve, xT_ps_ready, n - 1)
                        nc.vector.tensor_tensor(xn[:, p, :, :], xc[:, :, :], bc(rstd[:, :], D), ALU.mult).then_inc(xn_ready, 1)
                        dve.wait_ge(xn_ready, n * 2 + m + 1)
                    chain.end()

                def copies(n, p):
                    for u in range(2):
                        dve.wait_ge(tok_ps_ready, n * G + 2 * u + 2)
                        if u == 0:
                            wait_reuse(dve, turn_ready, (n - 1) * 4)
                        nc.vector.tensor_copy(qk[:, p, :, 2 * u + 1, :], tok_ps[:, 1, :].rearrange("p (h c) -> p h c", c=CH)).then_inc(tok_d, 1)
                    for u in range(2):
                        dve.wait_ge(turn_ready, n * 4 + 2 * u + 2)
                        if u == 0:
                            wait_reuse(dve, scored, n - 1)
                        nc.vector.tensor_copy(qkT[:, p, 4 * (2 * u + 1):4 * (2 * u + 2), :], turn_ps[:, 1, :, :]).then_inc(turned_d, 1)

                pipeline(dve, [norm, copies], TILES)

            @block.gpsimd
            def _(pool):
                def powers(n, p):
                    for m in range(2):
                        pool.wait_ge(var_ready, n * 2 + m + 1)
                        nc.gpsimd.tensor_tensor(rstd[:, :], var[:, :], S["neg_half"][:, 0:G], ALU.pow).then_inc(rstd_ready, 1)

                def keep(n, p):
                    pool.wait_ge(xT_ready, n + 1)
                    nc.gpsimd.tensor_copy(mnT[:, bass.ds(n * COLS, COLS)], xT[:, p, :]).then_inc(kept, 1)

                pipeline(pool, [powers, keep], TILES)

            @block.scalar
            def _(act):
                def copies(n, p):
                    act.wait_ge(xT_ps_ready, n + 1)
                    wait_reuse(act, kept, n - 1)
                    wait_reuse(act, tok_ps_ready, (n - 1) * G)
                    for q in range(2):
                        dst = xT[:, p, :].rearrange("d (g q t) -> d g q t", g=G // 2, q=2)[:, :, q, :]
                        ins = nc.scalar.activation(dst, xT_ps[q * D:(q + 1) * D, :, :], ACT.Identity,
                                                   bias=S["A_beta"][q * D:(q + 1) * D, :], scale=S["A_gamma"][q * D:(q + 1) * D, :])
                    ins.then_inc(xT_ready, 1)
                    for u in range(2):
                        act.wait_ge(tok_ps_ready, n * G + 2 * u + 1)
                        if u == 0:
                            wait_reuse(act, turn_ready, (n - 1) * 4)
                        nc.scalar.copy(qk[:, p, :, 2 * u, :], tok_ps[:, 0, :].rearrange("p (h c) -> p h c", c=CH)).then_inc(tok_a, 1)
                    for u in range(2):
                        act.wait_ge(turn_ready, n * 4 + 2 * u + 1)
                        if u == 0:
                            wait_reuse(act, scored, n - 1)
                        nc.scalar.copy(qkT[:, p, 8 * u:8 * u + 4, :], turn_ps[:, 0, :, :]).then_inc(turned_a, 1)

                pipeline(act, [None, copies], TILES)

            @block.tensor
            def _(pe):
                pe.wait_ge(consts_set, 1)
                for u in range(2):
                    nc.tensor.matmul(acc[:, 4 * u:4 * u + 4, :], zero[:, :],
                                     zero[:, :].unsqueeze(1).to_broadcast([1, 4, P]), start=True, stop=True)

                def tile(n, p):
                    pe.wait_ge(xn_ready, (n + 1) * 2)
                    wait_reuse(pe, xT_ready, n)
                    for q in range(G // 2):
                        ins = nc.tensor.transpose(xT_ps[:, q, :], xn[:, p, 2 * q:2 * q + 2, :].rearrange("p g d -> p (g d)"), ident[:, :])
                    ins.then_inc(xT_ps_ready, 1)
                    pe.wait_ge(xT_ready, n + 1)
                    for g in range(G):
                        wait_reuse(pe, (tok_a, tok_d)[g % 2], n * 2 + g // 2)
                        nc.tensor.matmul(tok_ps[:, g % 2, :], xT[:, p, g * P:(g + 1) * P], S["A_wqk"][:, :],
                                         start=True, stop=True).then_inc(tok_ps_ready, 1)
                    pe.wait_ge(tok_a, (n + 1) * 2)
                    pe.wait_ge(tok_d, (n + 1) * 2)
                    for u in range(4):
                        wait_reuse(pe, (turned_a, turned_d)[u % 2], n * 2 + u // 2)
                        for k in range(4):
                            head, which = 2 * u + k // 2, k % 2
                            ins = nc.tensor.transpose(turn_ps[:, u % 2, k, :],
                                                      qk[:, p, NH * which + head, :, :].rearrange("p g c -> p (g c)"), ident[:, :])
                        ins.then_inc(turn_ready, 1)
                    pe.wait_ge(turned_a, (n + 1) * 2)
                    pe.wait_ge(turned_d, (n + 1) * 2)
                    for head in range(NH):
                        ins = nc.tensor.matmul(acc[:, head, :], qkT[:, p, 2 * head, :], qkT[:, p, 2 * head + 1, :],
                                               start=False, stop=True, skip_group_check=True)
                    ins.then_inc(scored, 1)

                pipeline(pe, [None, tile], TILES)


def column_softmax(nc, S, acc, attT, scale):
    ident = S["ident"]
    with ExitStack() as ctx:
        top = ctx.enter_context(nc.sbuf_tensor("Am_top", [P, NH], F32))
        total = ctx.enter_context(nc.sbuf_tensor("Am_total", [P, NH], F32))
        att = ctx.enter_context(nc.sbuf_tensor("Am_att", [P, NH, P], F32))
        att_ps = ctx.enter_context(nc.psum_tensor("Am_ps", [P, NH, P], F32))
        sem = ctx.enter_context(semaphores(nc, "Am"))
        chain_sem, shifted, exps, normed, flipped = map(sem, ("chain", "shifted", "exps", "normed", "flipped"))
        with nc.Block() as block:
            @block.vector
            def _(dve):
                chain = Chain(dve, chain_sem, 0, 3)
                chain(nc.vector.tensor_reduce(top[:, :], acc[:, :, :], X, ALU.max))
                nc.vector.tensor_tensor(att[:, :, :], acc[:, :, :], bc(top[:, :], P), ALU.subtract).then_inc(shifted, 1)
                dve.wait_ge(exps, 1)
                chain(nc.vector.tensor_reduce(total[:, :], att[:, :, :], X, ALU.add))
                chain(nc.vector.reciprocal(total[:, :], total[:, :]))
                chain.end()
                nc.vector.tensor_tensor(att[:, :, :], att[:, :, :], bc(total[:, :], P), ALU.mult).then_inc(normed, 1)
                dve.wait_ge(flipped, 1)
                nc.vector.tensor_copy(attT[:, :, :], att_ps[:, :, :])

            @block.scalar
            def _(act):
                act.wait_ge(shifted, 1)
                nc.scalar.activation(att[:, :, :], att[:, :, :], ACT.Exp, scale=scale).then_inc(exps, 1)

            @block.tensor
            def _(pe):
                pe.wait_ge(normed, 1)
                for head in range(NH):
                    ins = nc.tensor.transpose(att_ps[:, head, :], att[:, head, :], ident[:, :])
                ins.then_inc(flipped, 1)


def column_values(nc, S, hs, mnT, attT):
    ident = S["ident"]
    with ExitStack() as ctx:
        def sb(name, shape, dt=F32):
            return ctx.enter_context(nc.sbuf_tensor(f"Av_{name}", shape, dt))

        def ps(name, shape):
            return ctx.enter_context(nc.psum_tensor(f"Av_{name}", shape, F32))

        sem = ctx.enter_context(semaphores(nc, "Av"))

        xs = sb("xs", [D + 1, 2, COLS])
        v = sb("v", [P, 2, G, HD])
        gate = sb("gate", [P, 2, G, HD])
        og = sb("og", [P, 2, G, HD])
        ogT = sb("ogT", [P, 2, 2, COLS])
        vg_ps = ps("vg_ps", [P, 2, 2 * HD])
        o_ps = ps("o_ps", [P, NH, G, CH])
        turn_ps = ps("turn_ps", [P, 2, COLS])
        y_ps = ps("y_ps", [P, G, D])
        fetched, vg_ready, v_ready, g_ready = sem("fetched"), sem("vg_ready"), sem("v_ready"), sem("g_ready")
        o_ready, og_ready, turn_ready, turned_a, turned_d = sem("o_ready"), sem("og_ready"), sem("turn_ready"), sem("turned_a"), sem("turned_d")
        y_ready, y_used, consts_set, chain_sem = sem("y_ready"), sem("y_used"), sem("consts_set"), sem("chain")

        with nc.Block() as block:
            @block.vector
            def _(dve):
                nc.vector.memset(xs[D:D + 1, :, :], 1.0).then_inc(consts_set, 1)

                def values(n, p):
                    for g in range(G):
                        dve.wait_ge(vg_ready, n * G + g + 1)
                        dve.wait_ge(g_ready, n * G + g + 1)
                        if g == 0:
                            wait_reuse(dve, o_ready, n - 1)
                        nc.vector.tensor_copy(v[:, p, g, :], vg_ps[:, g % 2, 0:HD]).then_inc(v_ready, 1)
                    dve.wait_ge(o_ready, n + 1)
                    wait_reuse(dve, turn_ready, n - 1)
                    for u in range(2):
                        half = slice(u * HD // 2, (u + 1) * HD // 2)
                        ins = nc.vector.tensor_tensor(og[:, p, :, half].rearrange("p g (h c) -> p g h c", c=CH),
                                                      o_ps[:, 4 * u:4 * u + 4, :, :].rearrange("p h g c -> p g h c"),
                                                      gate[:, p, :, half].rearrange("p g (h c) -> p g h c", c=CH), ALU.mult)
                    ins.then_inc(og_ready, 1)

                def output(n, p):
                    chain = Chain(dve, chain_sem, n, 1)
                    dve.wait_ge(turn_ready, n + 1)
                    wait_reuse(dve, y_ready, n - 1)
                    nc.vector.tensor_copy(ogT[:, p, 1, :], turn_ps[:, 1, :]).then_inc(turned_d, 1)
                    dve.wait_ge(y_ready, n + 1)
                    hn = hs[:, bass.ds(n * G, G), :]
                    nc.vector.tensor_tensor(hn, hn, y_ps[:, :, :], ALU.add).then_inc(y_used, 1)
                    dve.wait_ge(y_used, n + 1)
                    chain(nc.vector.tensor_tensor(hn, hn, mid(S["A_bo"][:, :], G), ALU.add))
                    chain.end()

                pipeline(dve, [None, values, output], TILES)

            @block.gpsimd
            def _(pool):
                pool.wait_ge(consts_set, 1)

                def fetch(n, p):
                    wait_reuse(pool, vg_ready, (n - 1) * G)
                    nc.gpsimd.tensor_copy(xs[0:D, p, :], mnT[:, bass.ds(n * COLS, COLS)]).then_inc(fetched, 1)

                pipeline(pool, [fetch, None, None], TILES)

            @block.scalar
            def _(act):
                def gates(n, p):
                    for g in range(G):
                        act.wait_ge(vg_ready, n * G + g + 1)
                        if g == 0:
                            wait_reuse(act, og_ready, n - 1)
                        nc.scalar.activation(gate[:, p, g, :], vg_ps[:, g % 2, HD:2 * HD], ACT.Sigmoid).then_inc(g_ready, 1)

                def turn(n, p):
                    act.wait_ge(turn_ready, n + 1)
                    wait_reuse(act, y_ready, n - 1)
                    nc.scalar.copy(ogT[:, p, 0, :], turn_ps[:, 0, :]).then_inc(turned_a, 1)

                pipeline(act, [None, gates, turn], TILES)

            @block.tensor
            def _(pe):
                def attend(n, p):
                    pe.wait_ge(fetched, n + 1)
                    for g in range(G):
                        wait_reuse(pe, v_ready, n * G + g - 1)
                        nc.tensor.matmul(vg_ps[:, g % 2, :], xs[:, p, g * P:(g + 1) * P], S["A_wvg"][:, :],
                                         start=True, stop=True).then_inc(vg_ready, 1)
                    pe.wait_ge(v_ready, (n + 1) * G)
                    wait_reuse(pe, og_ready, n)
                    for head in range(NH):
                        ins = nc.tensor.matmul(o_ps[:, head, :, :], attT[:, head, :], v[:, p, :, CH * head:CH * (head + 1)],
                                               start=True, stop=True)
                    ins.then_inc(o_ready, 1)

                def output(n, p):
                    pe.wait_ge(og_ready, n + 1)
                    wait_reuse(pe, turned_a, n)
                    wait_reuse(pe, turned_d, n)
                    for u in range(2):
                        for g in range(G):
                            ins = nc.tensor.transpose(turn_ps[:, u, g * P:(g + 1) * P], og[:, p, g, u * P:(u + 1) * P], ident[:, :])
                    ins.then_inc(turn_ready, 1)
                    pe.wait_ge(turned_a, n + 1)
                    pe.wait_ge(turned_d, n + 1)
                    wait_reuse(pe, y_used, n)
                    for g in range(G):
                        for u in range(2):
                            ins = nc.tensor.matmul(y_ps[:, g, :], ogT[:, p, u, g * P:(g + 1) * P], S["A_wo"][:, u, :],
                                                   start=(u == 0), stop=(u == 1))
                    ins.then_inc(y_ready, 1)

                pipeline(pe, [None, attend, output], TILES)


def swap_axes(nc, S, hs):
    h, ident = S["h"], S["ident"]
    with ExitStack() as ctx:
        turn_ps = ctx.enter_context(nc.psum_tensor("Ax_ps", [P, 4, 4, P], F32))
        turned, copied_a, copied_d = map(ctx.enter_context(semaphores(nc, "Ax")), ("turned", "copied_a", "copied_d"))
        with nc.Block() as block:
            @block.tensor
            def _(pe):
                for q in range(D // 4):
                    if q >= 4:
                        pe.wait_ge((copied_a, copied_d)[q % 2], q // 2 - 1)
                    for k in range(4):
                        ins = nc.tensor.transpose(turn_ps[:, q % 4, k, :], hs[:, :, 4 * q + k], ident[:, :])
                    ins.then_inc(turned, 1)

            def copy_out(eng, copy, first, done):
                for q in range(first, D // 4, 2):
                    eng.wait_ge(turned, q + 1)
                    copy(h[:, :, 4 * q:4 * q + 4], turn_ps[:, q % 4, :, :].rearrange("p k s -> p s k")).then_inc(done, 1)

            @block.scalar
            def _(act):
                copy_out(act, nc.scalar.copy, 0, copied_a)

            @block.vector
            def _(dve):
                copy_out(dve, nc.vector.tensor_copy, 1, copied_d)


def loads_moe(nc, S, A, sb, load, layer, wr_name, br_name):
    q = f"{layer}_ffn_"
    w1 = sb(q + "w1", [D + 1, NE, HID])
    load(w1[0:D], A[q + "W1"].rearrange("e d f -> d e f"))
    load(w1[D:D + 1], A[q + "b1"].rearrange("(a e) f -> a e f", a=1))
    w2 = sb(q + "w2", [HID, NE, D])
    load(w2[:], A[q + "W2"].rearrange("e f d -> f e d"))
    wr = sb(q + "wr", [D + 1, NE])
    load(wr[0:D], A[q + wr_name][:, :])
    load(wr[D:D + 1], A[q + br_name].rearrange("(a e) -> a e", a=1))
    load(sb(q + "b2", [1, NE * D])[:, :], A[q + "b2"].rearrange("(a e) d -> a (e d)", a=1))
    if layer == "L1":
        for v in ("gamma", "beta"):
            two = sb("L1m_" + v, [2 * D, 1])
            for k in range(2):
                load(two[k * D:(k + 1) * D, :], A[q + v].rearrange("(d a) -> d a", a=1))


def moe_layer(nc, S, pre, w1, w2, b2, wr, affine):
    h, ident, half = S["h"], S["ident"], S["neg_half"]
    with ExitStack() as ctx:
        def sb(name, shape, dt=F32):
            return ctx.enter_context(nc.sbuf_tensor(f"{pre}_{name}", shape, dt))

        def ps(name, shape):
            return ctx.enter_context(nc.psum_tensor(f"{pre}_{name}", shape, F32))

        sem = ctx.enter_context(semaphores(nc, pre))

        xc = sb("xc", [P, G, D])
        sq = sb("sq", [P, G, D])
        total = sb("total", [P, G])
        var = sb("var", [P, G])
        rstd = sb("rstd", [P, G])
        xn = sb("xn", [P, 2, G, D])
        xT = sb("xT", [D + 1, 2, COLS])
        rw = sb("rw", [P, 8, G, NE])
        small = sb("small", [P, 6, G])
        ex_in = sb("ex_in", [P, G, NE])
        ex = sb("ex", [P, G, NE])
        ebase = sb("ebase", [P, G, NE])
        cw = sb("cw", [P, 2, G, NE])
        hid = sb("hid", [P, 2, COLS])
        weighted = sb("weighted", [P, G, NE, D])
        mixed = sb("mixed", [P, G, D])

        b2_parts = sb("b2_parts", [96, NE * D], BF16)
        b2_head = sb("b2_head", [1, 3, NE * D], BF16)
        b2_rest = sb("b2_rest", [1, 2, NE * D])
        ones = sb("ones", [96, P], BF16)

        xT_ps = ps("xT_ps", [P, G // 2, P])
        logits_ps = ps("logits_ps", [P, G, NE])
        hid_ps = ps("hid_ps", [P, 2, COLS])
        y_ps = ps("y_ps", [P, G, NE, D])

        stats_chain, route_chain, back_chain, split_chain = sem("stats_chain"), sem("route_chain"), sem("back_chain"), sem("split_chain")
        var_ready, rstd_ready, xn_ready = sem("var_ready"), sem("rstd_ready"), sem("xn_ready")
        xT_ps_ready, xT_ready = sem("xT_ps_ready"), sem("xT_ready")
        logits_ready, ex_in_ready, ex_ready, cw_ready = sem("logits_ready"), sem("ex_in_ready"), sem("ex_ready"), sem("cw_ready")
        hid_ps_ready, hid_ready, down_done = sem("hid_ps_ready"), sem("hid_ready"), sem("down_done")
        y_used = sem("y_used")
        consts_set = sem("consts_set")
        norms = 2 if affine else 1

        with nc.Block() as block:
            @block.vector
            def _(dve):
                nc.vector.memset(xT[D:D + 1, :, :], 1.0)
                nc.vector.memset(ebase[:, :, :], float(np.e))
                nc.vector.memset(ones[:, :], 1.0)
                chain = Chain(dve, split_chain, 0, 6)
                chain(nc.vector.memset(b2_parts[:, :], 0.0))
                rest = b2[:, :]
                for k in range(3):
                    chain(nc.vector.tensor_copy(b2_head[:, k, :], rest))
                    nc.vector.tensor_copy(b2_parts[32 * k:32 * k + 1, :], b2_head[:, k, :])
                    if k < 2:
                        chain(nc.vector.tensor_tensor(b2_rest[:, k, :], rest, b2_head[:, k, :], ALU.subtract))
                        rest = b2_rest[:, k, :]
                chain.end()
                nc.vector.memset(xT[D:D + 1, :, :], 1.0).then_inc(consts_set, 1)
                dve.wait_ge(consts_set, 1)

                def norm(n, p):
                    chain = Chain(dve, stats_chain, n, 4 * norms)
                    for m in range(norms):
                        x = h[:, bass.ds(n * G, G), :] if m == 0 else xn[:, p, :, :]
                        norm_stats(dve, nc, chain, x, xc[:, :, :], sq[:, :, :], total[:, :], var[:, :]).then_inc(var_ready, 1)
                        dve.wait_ge(rstd_ready, n * norms + m + 1)
                        if m == 0:
                            wait_reuse(dve, xT_ps_ready, n - 1)
                        nc.vector.tensor_tensor(xn[:, p, :, :], xc[:, :, :], bc(rstd[:, :], D),
                                                ALU.mult).then_inc(xn_ready, 1)
                        dve.wait_ge(xn_ready, n * norms + m + 1)
                    chain.end()

                def best(chain, score, slot, k):
                    chain(nc.vector.tensor_reduce(small[:, k, :], score, X, ALU.max))
                    chain(nc.vector.tensor_tensor(rw[:, slot, :, :], score, bc(small[:, k, :], NE), ALU.is_equal))
                    chain(nc.vector.tensor_tensor(rw[:, slot, :, :], rw[:, slot, :, :], mid(S["rev8"][:, :], G), ALU.mult))
                    chain(nc.vector.tensor_reduce(small[:, k + 1, :], rw[:, slot, :, :], X, ALU.max))
                    chain(nc.vector.tensor_tensor(rw[:, slot, :, :], rw[:, slot, :, :], bc(small[:, k + 1, :], NE), ALU.is_equal))

                def route(n, p):
                    chain = Chain(dve, route_chain, n, 17)
                    dve.wait_ge(logits_ready, n + 1)
                    chain(nc.vector.tensor_copy(rw[:, 0, :, :], logits_ps[:, :, :]))
                    chain(nc.vector.tensor_reduce(small[:, 0, :], rw[:, 0, :, :], X, ALU.max))
                    wait_reuse(dve, ex_ready, n)
                    nc.vector.tensor_tensor(ex_in[:, :, :], rw[:, 0, :, :], bc(small[:, 0, :], NE),
                                            ALU.subtract).then_inc(ex_in_ready, 1)
                    if not affine:
                        dve.wait_ge(ex_ready, n + 1)
                        chain(nc.vector.tensor_reduce(small[:, 1, :], ex[:, :, :], X, ALU.add))
                        chain(nc.vector.reciprocal(small[:, 1, :], small[:, 1, :]))
                        chain(nc.vector.tensor_tensor(rw[:, 0, :, :], ex[:, :, :], bc(small[:, 1, :], NE), ALU.mult))
                    best(chain, rw[:, 0, :, :], 1, 2)
                    chain(nc.vector.scalar_tensor_tensor(out=rw[:, 2, :, :], in0=rw[:, 1, :, :], scalar=-1e30,
                                                         in1=rw[:, 0, :, :], op0=ALU.mult, op1=ALU.add))
                    best(chain, rw[:, 2, :, :], 3, 4)
                    chain(nc.vector.tensor_tensor(rw[:, 4, :, :], rw[:, 1, :, :], rw[:, 3, :, :], ALU.add))
                    if affine:
                        dve.wait_ge(ex_ready, n + 1)
                        chain(nc.vector.tensor_tensor(rw[:, 5, :, :], ex[:, :, :], rw[:, 4, :, :], ALU.mult))
                        chain(nc.vector.tensor_reduce(small[:, 1, :], rw[:, 5, :, :], X, ALU.add))
                        chain(nc.vector.reciprocal(small[:, 1, :], small[:, 1, :]))
                        nc.vector.tensor_tensor(cw[:, p, :, :], rw[:, 5, :, :], bc(small[:, 1, :], NE), ALU.mult).then_inc(cw_ready, 1)
                    else:
                        nc.vector.tensor_tensor(cw[:, p, :, :], rw[:, 0, :, :], rw[:, 4, :, :], ALU.mult).then_inc(cw_ready, 1)
                    chain.end()

                def combine(n, p):
                    chain = Chain(dve, back_chain, n, 2)
                    dve.wait_ge(down_done, (n + 1) * NE)
                    for g in range(G):
                        nc.vector.tensor_tensor(weighted[:, g, :, :], y_ps[:, g, :, :],
                                                bc(cw[:, p, g, :], D), ALU.mult).then_inc(y_used, 1)
                    dve.wait_ge(y_used, (n + 1) * G)
                    chain(nc.vector.tensor_reduce(mixed[:, :, :], weighted[:, :, :, :].rearrange("p g e d -> p g d e"), X, ALU.add))
                    chain(nc.vector.tensor_tensor(h[:, bass.ds(n * G, G), :], h[:, bass.ds(n * G, G), :], mixed[:, :, :], ALU.add))
                    chain.end()

                pipeline(dve, [norm, route, combine], TILES)

            @block.gpsimd
            def _(pool):
                pool.wait_ge(consts_set, 1)

                def powers(n, p):
                    for m in range(norms):
                        pool.wait_ge(var_ready, n * norms + m + 1)
                        nc.gpsimd.tensor_tensor(rstd[:, :], var[:, :], half[:, 0:G], ALU.pow).then_inc(rstd_ready, 1)

                def exponents(n, p):
                    pool.wait_ge(ex_in_ready, n + 1)
                    nc.gpsimd.tensor_tensor(ex[:, :, :], ebase[:, :, :], ex_in[:, :, :], ALU.pow).then_inc(ex_ready, 1)

                pipeline(pool, [powers, exponents, None], TILES)

            @block.scalar
            def _(act):
                act.wait_ge(consts_set, 1)

                def turn(n, p):
                    act.wait_ge(xT_ps_ready, n + 1)
                    wait_reuse(act, down_done, (n - 1) * NE)
                    for q in range(2):
                        src = xT_ps[q * D:(q + 1) * D, :, :]
                        dst = xT[0:D, p, :].rearrange("d (g q t) -> d g q t", g=G // 2, q=2)[:, :, q, :]
                        if affine:
                            ins = nc.scalar.activation(dst, src, ACT.Identity, bias=S[pre + "_beta"][q * D:(q + 1) * D, :],
                                                       scale=S[pre + "_gamma"][q * D:(q + 1) * D, :])
                        else:
                            ins = nc.scalar.copy(dst, src)
                    ins.then_inc(xT_ready, 1)

                def gelus(n, p):
                    for e in range(NE):
                        act.wait_ge(hid_ps_ready, n * NE + e + 1)
                        wait_reuse(act, down_done, n * NE + e - 1)
                        nc.scalar.activation(hid[:, e % 2, :], hid_ps[:, e % 2, :], ACT.Gelu).then_inc(hid_ready, 1)

                pipeline(act, [None, turn, gelus], TILES)

            @block.tensor
            def _(pe):
                pe.wait_ge(consts_set, 1)

                def front(n, p):
                    pe.wait_ge(xn_ready, (n + 1) * norms)
                    wait_reuse(pe, xT_ready, n)
                    for q in range(G // 2):
                        ins = nc.tensor.transpose(xT_ps[:, q, :], xn[:, p, 2 * q:2 * q + 2, :].rearrange("p g d -> p (g d)"), ident[:, :])
                    ins.then_inc(xT_ps_ready, 1)
                    pe.wait_ge(xT_ready, n + 1)
                    wait_reuse(pe, ex_in_ready, n)
                    for g in range(G):
                        ins = nc.tensor.matmul(logits_ps[:, g, :], xT[:, p, g * P:(g + 1) * P], wr[:, :], start=True, stop=True)
                    ins.then_inc(logits_ready, 1)

                def experts(n, p):
                    def up(e):
                        wait_reuse(pe, hid_ready, n * NE + e - 1)
                        nc.tensor.matmul(hid_ps[:, e % 2, :], w1[:, e, :], xT[:, p, :], start=True, stop=True).then_inc(hid_ps_ready, 1)

                    def down(e):
                        pe.wait_ge(hid_ready, n * NE + e + 1)
                        for g in range(G):
                            if e == 0:
                                wait_reuse(pe, y_used, (n - 1) * G + g + 1)
                                nc.tensor.matmul(y_ps[:, g, :, :], ones[:, :], b2_parts[:, :], start=True, stop=True)
                            ins = nc.tensor.matmul(y_ps[:, g, e, :], hid[:, e % 2, g * P:(g + 1) * P], w2[:, e, :],
                                                   start=False, stop=True, skip_group_check=True)
                        ins.then_inc(down_done, 1)

                    up(0)
                    for e in range(1, NE):
                        up(e)
                        down(e - 1)
                    down(NE - 1)

                pipeline(pe, [None, front, experts], TILES)


def upto(count):
    return min(count, TILES) if isinstance(count, int) else count


def constants_C(c):
    slopes = 2.0 ** -np.arange(1, NH + 1)
    rel = np.arange(T)[None, :] - np.arange(T)[:, None]
    bias = slopes[None, :, None] * rel[:, None, :]
    c["alibi"] = np.where(rel[:, None, :] <= 0, bias, -1e30).astype(np.float32).reshape(T, NH * T)


def loads_C(nc, S, A, sb, load, zeroed):
    q = "L1_attn_"
    for w in "qkv":
        load(sb("C_w" + w, [D, HD])[:, :], A[q + "W" + w][:, :])
    load(sb("C_wo", [P, 2, D])[:], A[q + "Wo"].rearrange("(u p) d -> p u d", p=P))
    load(sb("C_bo", [P, D])[:, :], A[q + "bo"].rearrange("(a n) -> a n", a=1).to_broadcast([P, D]))


def alibi_attention(nc, S, A):
    h, ident = S["h"], S["ident"]
    SCALE = 1.0 / float(np.sqrt(CH))
    with ExitStack() as ctx:
        def sb(name, shape, dt=F32):
            return ctx.enter_context(nc.sbuf_tensor(f"C_{name}", shape, dt))

        def ps(name, shape):
            return ctx.enter_context(nc.psum_tensor(f"C_{name}", shape, F32))

        sem = ctx.enter_context(semaphores(nc, "C"))

        xc, sq = sb("xc", [P, G, D]), sb("sq", [P, G, D])
        total, var, rstd = sb("total", [P, G]), sb("var", [P, G]), sb("rstd", [P, G])
        xn = sb("xn", [P, 2, G, D])
        xT = sb("xT", [D, 2, COLS])
        qT = sb("qT", [P, 2, 2, COLS])
        kD = sb("kD", [P, 2, 2, G, 4, P])
        v = sb("v", [P, 2, G, NH, CH + 1])
        bias = sb("bias", [P, NH, P], BF16)
        ident16 = sb("ident16", [P, P], BF16)
        top = sb("top", [P, NH])
        e = sb("e", [P, 2, NH, P])
        eT = sb("eT", [P, 2, NH, P])
        rsum = sb("rsum", [P, NH])
        o = sb("o", [P, 2, G, HD])
        oT = sb("oT", [P, 2, COLS])
        xT_ps = ps("xT_ps", [P, G // 2, P])
        ring_ps = ps("ring_ps", [P, 2, COLS])
        s_ps = ps("s_ps", [P, NH, P])
        eT_ps = ps("eT_ps", [P, NH, P])
        o_ps = ps("o_ps", [P, NH, CH + 1])
        with ExitStack() as c2:
            alibi = c2.enter_context(nc.sbuf_tensor("C_alibi", [P, NH * P], F32))
            alibi_in = c2.enter_context(semaphores(nc, "C_setup"))("alibi_in")
            with nc.Block() as block:
                @block.sync
                def _(sp):
                    sp.dma_start(alibi[:, :], A["alibi"][:, :]).then_inc(alibi_in, 16)

                @block.vector
                def _(dve):
                    dve.wait_ge(alibi_in, 16)
                    nc.vector.tensor_copy(bias[:, :, :].rearrange("p h s -> p (h s)"), alibi[:, :])
                    nc.vector.tensor_copy(ident16[:, :], ident[:, :])
                    nc.vector.memset(kD[:], 0.0)
                    nc.vector.memset(v[:, :, :, :, CH:CH + 1], 1.0)

        stats_chain, var_ready, rstd_ready, xn_ready = sem("stats_chain"), sem("var_ready"), sem("rstd_ready"), sem("xn_ready")
        xT_ps_ready, xT_ready = sem("xT_ps_ready"), sem("xT_ready")
        filled = [[sem(f"{w}{u}_filled") for w in ("q", "k", "v", "oT")] for u in range(2)]
        emptied = [[sem(f"{w}{u}_emptied") for w in ("q", "k", "v", "oT")] for u in range(2)]
        y_ready, y_used = sem("y_ready"), sem("y_used")
        s_ready, top_ready, shifted, e_ready = sem("s_ready"), sem("top_ready"), sem("shifted"), sem("e_ready")
        eT_ps_ready, eT_a, eT_d = sem("eT_ps_ready"), sem("eT_a"), sem("eT_d")
        o_ready, rsum_ready, o_done = sem("o_ready"), sem("rsum_ready"), sem("o_done")

        def empty_front(eng, n, p, u, copy, scaled):
            eng.wait_ge(filled[u][0], n + 1)
            wait_reuse(eng, eT_ps_ready, (n - 1) * G)
            scaled(qT[:, p, u, :], ring_ps[:, u, :]).then_inc(emptied[u][0], 1)
            eng.wait_ge(filled[u][1], n + 1)
            for j in range(4):
                rows = slice(32 * j, 32 * j + 32)
                ins = copy(kD[rows, p, u, :, j, :], ring_ps[rows, u, :].rearrange("p (g t) -> p g t", g=G))
            ins.then_inc(emptied[u][1], 1)
            eng.wait_ge(filled[u][2], n + 1)
            wait_reuse(eng, o_ready, (n - 1) * G)
            for g in range(2):
                ins = copy(v[:, p, 2 * u + g, :, 0:CH], ring_ps[:, u, HD * g:HD * (g + 1)].rearrange("p (h c) -> p h c", c=CH))
            ins.then_inc(emptied[u][2], 1)

        with nc.Block() as block:
            @block.vector
            def _(dve):
                def norm(n, p):
                    chain = Chain(dve, stats_chain, n, 4)
                    norm_stats(dve, nc, chain, h[:, bass.ds(n * G, G), :], xc[:, :, :], sq[:, :, :], total[:, :], var[:, :]).then_inc(var_ready, 1)
                    dve.wait_ge(rstd_ready, n + 1)
                    wait_reuse(dve, xT_ps_ready, n - 1)
                    nc.vector.tensor_tensor(xn[:, p, :, :], xc[:, :, :], bc(rstd[:, :], D), ALU.mult).then_inc(xn_ready, 1)
                    dve.wait_ge(xn_ready, n + 1)
                    chain.end()

                def front(n, p):
                    empty_front(dve, n, p, 1, nc.vector.tensor_copy,
                                lambda out, in_: nc.vector.tensor_scalar(out, in_, SCALE, None, ALU.mult))

                def attend(n, p):
                    def softmax(g):
                        m = n * G + g
                        dve.wait_ge(s_ready, m + 1)
                        nc.vector.tensor_reduce(top[:, :], s_ps[:, :, :], X, ALU.max).then_inc(top_ready, 1)
                        dve.wait_ge(top_ready, m + 1)
                        wait_reuse(dve, eT_ps_ready, m - 1)
                        nc.vector.tensor_tensor(e[:, g % 2, :, :], s_ps[:, :, :], bc(top[:, :], P), ALU.subtract).then_inc(shifted, 1)

                    def turned(g):
                        m = n * G + g
                        dve.wait_ge(eT_ps_ready, m + 1)
                        wait_reuse(dve, o_ready, m - 1)
                        nc.vector.tensor_copy(eT[:, g % 2, 4:8, :], eT_ps[:, 4:8, :]).then_inc(eT_d, 1)

                    def output(g):
                        m = n * G + g
                        dve.wait_ge(o_ready, m + 1)
                        nc.vector.reciprocal(rsum[:, :], o_ps[:, :, CH]).then_inc(rsum_ready, 1)
                        dve.wait_ge(rsum_ready, m + 1)
                        if g == 0:
                            wait_reuse(dve, filled[1][3], n - 1)
                        nc.vector.tensor_tensor(o[:, p, g, :].rearrange("p (h c) -> p h c", c=CH), o_ps[:, :, 0:CH],
                                                bc(rsum[:, :], CH), ALU.mult).then_inc(o_done, 1)

                    for g in range(G + 2):
                        if g < G:
                            softmax(g)
                        if 1 <= g <= G:
                            turned(g - 1)
                        if g >= 2:
                            output(g - 2)
                    dve.wait_ge(filled[1][3], n + 1)
                    wait_reuse(dve, y_ready, n)
                    nc.vector.tensor_copy(oT[:, 1, :], ring_ps[:, 1, :]).then_inc(emptied[1][3], 1)
                    dve.wait_ge(y_ready, n + 1)
                    hn = h[:, bass.ds(n * G, G), :]
                    nc.vector.tensor_tensor(hn, hn, ring_ps[:, 1, 0:G * D].rearrange("p (g d) -> p g d", g=G), ALU.add).then_inc(y_used, 1)
                    dve.wait_ge(y_used, 2 * n + 1)
                    nc.vector.tensor_tensor(hn, hn, mid(S["C_bo"][:, :], G), ALU.add).then_inc(y_used, 1)

                pipeline(dve, [norm, front, attend], TILES)

            @block.gpsimd
            def _(pool):
                def powers(n, p):
                    pool.wait_ge(var_ready, n + 1)
                    nc.gpsimd.tensor_tensor(rstd[:, :], var[:, :], S["neg_half"][:, 0:G], ALU.pow).then_inc(rstd_ready, 1)

                pipeline(pool, [powers, None, None], TILES)

            @block.scalar
            def _(act):
                def front(n, p):
                    act.wait_ge(xT_ps_ready, n + 1)
                    wait_reuse(act, filled[1][2], n - 1)
                    for q in range(2):
                        ins = nc.scalar.copy(xT[:, p, :].rearrange("d (g q t) -> d g q t", g=G // 2, q=2)[:, :, q, :],
                                             xT_ps[q * D:(q + 1) * D, :, :])
                    ins.then_inc(xT_ready, 1)
                    empty_front(act, n, p, 0, nc.scalar.copy, lambda out, in_: nc.scalar.mul(out, in_, SCALE))

                def attend(n, p):
                    for g in range(G + 1):
                        m = n * G + g
                        if g < G:
                            act.wait_ge(shifted, m + 1)
                            nc.scalar.activation(e[:, g % 2, :, :], e[:, g % 2, :, :], ACT.Exp).then_inc(e_ready, 1)
                        if g >= 1:
                            act.wait_ge(eT_ps_ready, m)
                            wait_reuse(act, o_ready, m - 2)
                            nc.scalar.copy(eT[:, (g - 1) % 2, 0:4, :], eT_ps[:, 0:4, :]).then_inc(eT_a, 1)
                    act.wait_ge(filled[0][3], n + 1)
                    wait_reuse(act, y_ready, n)
                    nc.scalar.copy(oT[:, 0, :], ring_ps[:, 0, :]).then_inc(emptied[0][3], 1)

                pipeline(act, [None, front, attend], TILES)

            @block.tensor
            def _(pe):
                def front(n, p):
                    pe.wait_ge(xn_ready, n + 1)
                    wait_reuse(pe, xT_ready, n)
                    for q in range(G // 2):
                        ins = nc.tensor.transpose(xT_ps[:, q, :], xn[:, p, 2 * q:2 * q + 2, :].rearrange("p g d -> p (g d)"), ident[:, :])
                    ins.then_inc(xT_ps_ready, 1)
                    pe.wait_ge(xT_ready, n + 1)
                    for u in range(2):
                        wait_reuse(pe, emptied[u][2], n)
                        if u == 0:
                            wait_reuse(pe, emptied[0][3], n - 1)
                        else:
                            wait_reuse(pe, y_used, 2 * (n - 1))
                        nc.tensor.matmul(ring_ps[:, u, :], S["C_wq"][:, u * P:(u + 1) * P], xT[:, p, :], start=True, stop=True).then_inc(filled[u][0], 1)
                    for u in range(2):
                        pe.wait_ge(emptied[u][0], n + 1)
                        nc.tensor.matmul(ring_ps[:, u, :], S["C_wk"][:, u * P:(u + 1) * P], xT[:, p, :], start=True, stop=True).then_inc(filled[u][1], 1)
                    for u in range(2):
                        pe.wait_ge(emptied[u][1], n + 1)
                        for g in range(2):
                            b = 2 * u + g
                            ins = nc.tensor.matmul(ring_ps[:, u, HD * g:HD * (g + 1)], xT[:, p, b * P:(b + 1) * P], S["C_wv"][:, :], start=True, stop=True)
                        ins.then_inc(filled[u][2], 1)

                def attend(n, p):
                    def scores(g):
                        wait_reuse(pe, shifted, n * G + g)
                        if g == 0:
                            pe.wait_ge(emptied[0][1], n + 1)
                            pe.wait_ge(emptied[1][1], n + 1)
                        for u in range(2):
                            nc.tensor.matmul(s_ps[:, 4 * u:4 * u + 4, :], ident16[:, :], bias[:, 4 * u:4 * u + 4, :], start=True, stop=False)
                            ins = nc.tensor.matmul(s_ps[:, 4 * u:4 * u + 4, :], qT[:, p, u, g * P:(g + 1) * P], kD[:, p, u, g, :, :], start=False, stop=True)
                        ins.then_inc(s_ready, 1)

                    def turn(g):
                        m = n * G + g
                        pe.wait_ge(e_ready, m + 1)
                        wait_reuse(pe, eT_a, m)
                        wait_reuse(pe, eT_d, m)
                        for head in range(NH):
                            ins = nc.tensor.transpose(eT_ps[:, head, :], e[:, g % 2, head, :], ident[:, :])
                        ins.then_inc(eT_ps_ready, 1)

                    def values(g):
                        m = n * G + g
                        pe.wait_ge(eT_a, m + 1)
                        pe.wait_ge(eT_d, m + 1)
                        if g == 0:
                            pe.wait_ge(emptied[0][2], n + 1)
                            pe.wait_ge(emptied[1][2], n + 1)
                        wait_reuse(pe, o_done, m)
                        for head in range(NH):
                            ins = nc.tensor.matmul(o_ps[:, head, :], eT[:, g % 2, head, :], v[:, p, g, head, :], start=True, stop=True)
                        ins.then_inc(o_ready, 1)

                    for g in range(G + 2):
                        if g < G:
                            scores(g)
                        if 1 <= g <= G:
                            turn(g - 1)
                        if g >= 2:
                            values(g - 2)
                    pe.wait_ge(o_done, (n + 1) * G)
                    for u in range(2):
                        pe.wait_ge(emptied[u][2], upto(n + 2))
                        for g in range(G):
                            ins = nc.tensor.transpose(ring_ps[:, u, g * P:(g + 1) * P], o[:, p, g, u * P:(u + 1) * P], ident[:, :])
                        ins.then_inc(filled[u][3], 1)
                    pe.wait_ge(emptied[0][3], n + 1)
                    pe.wait_ge(emptied[1][3], n + 1)
                    for g in range(G):
                        for u in range(2):
                            ins = nc.tensor.matmul(ring_ps[:, 1, D * g:D * (g + 1)], oT[:, u, g * P:(g + 1) * P], S["C_wo"][:, u, :],
                                                   start=(u == 0), stop=(u == 1))
                    ins.then_inc(y_ready, 1)

                pipeline(pe, [None, front, attend], TILES)


PERIODS = (24.0, 720.0)
NS = len(PERIODS)


def constants_E(c):
    idx = np.arange(T, dtype=np.float32)
    dist = np.abs(idx[:, None] - idx[None, :])
    c["cosines"] = np.stack([np.cos(np.float32(2.0 * np.pi) * dist / np.float32(t)) for t in PERIODS], axis=1).astype(np.float32)


def loads_E(nc, S, A, sb, load, zeroed):
    q = "L2_attn_"
    for w in "qkv":
        tile = sb("E_w" + w, [D + 1, D])
        load(tile[0:D, :], A[q + "W" + w][:, :])
        load(tile[D:D + 1, :], A[q + "b" + w].rearrange("(a e) -> a e", a=1))
    load(sb("E_beta", [P, NS])[:, :], A[q + "beta"].rearrange("(a n) -> a n", a=1).to_broadcast([P, NS]))
    load(sb("E_cos", [P, NS, T])[:], A["cosines"][:, :, :])


def periodic_attention(nc, S):
    h, ident = S["h"], S["ident"]
    SCALE = 1.0 / float(np.sqrt(D))
    with ExitStack() as ctx:
        def sb(name, shape, dt=F32):
            return ctx.enter_context(nc.sbuf_tensor(f"E_{name}", shape, dt))

        def ps(name, shape):
            return ctx.enter_context(nc.psum_tensor(f"E_{name}", shape, F32))

        sem = ctx.enter_context(semaphores(nc, "E"))

        xc, sq = sb("xc", [P, G, D]), sb("sq", [P, G, D])
        total, var, rstd = sb("total", [P, G]), sb("var", [P, G]), sb("rstd", [P, G])
        xn = sb("xn", [P, 2, G, D])
        xT = sb("xT", [D + 1, 2, COLS])
        qT, kT = sb("qT", [D, 2, COLS]), sb("kT", [D, 2, COLS])
        v = sb("v", [P, 2, G, D + 1])
        bias = sb("bias", [P, NS, T])
        s = sb("s", [P, G, T])
        top = sb("top", [P, G])
        e = sb("e", [P, G, T])
        eT = sb("eT", [P, G, P])
        rsum = sb("rsum", [P, G])
        o = sb("o", [P, G, D])
        xT_ps = ps("xT_ps", [P, G // 2, P])
        q_ps, k_ps, v_ps = ps("q_ps", [D, COLS]), ps("k_ps", [D, COLS]), ps("v_ps", [P, G, D])
        s_ps, eT_ps, o_ps = ps("s_ps", [P, G, T]), ps("eT_ps", [P, G, P]), ps("o_ps", [P, G, D + 1])
        names = ("stats_chain var_ready rstd_ready xn_ready xT_ps_ready xT_ready q_ready q_done k_ready k_done v_ready v_done "
                 "s_ready back_chain biased shifted e_ready eT_ready eT_done o_ready o_chain consts_set").split()
        (stats_chain, var_ready, rstd_ready, xn_ready, xT_ps_ready, xT_ready, q_ready, q_done, k_ready, k_done, v_ready, v_done,
         s_ready, back_chain, biased, shifted, e_ready, eT_ready, eT_done, o_ready, o_chain, consts_set) = map(sem, names)

        with nc.Block() as block:
            @block.vector
            def _(dve):
                nc.vector.memset(xT[D:D + 1, :, :], 1.0)
                nc.vector.memset(v[:, :, :, D:D + 1], 1.0)
                nc.vector.tensor_scalar(bias[:, 0, :], S["E_cos"][:, 0, :], S["E_beta"][:, 0:1], None, ALU.mult).then_inc(consts_set, 1)
                dve.wait_ge(consts_set, 1)
                nc.vector.scalar_tensor_tensor(out=bias[:, 1, :], in0=S["E_cos"][:, 1, :], scalar=S["E_beta"][:, 1:2],
                                               in1=bias[:, 0, :], op0=ALU.mult, op1=ALU.add).then_inc(consts_set, 1)
                dve.wait_ge(consts_set, 2)

                def norm(n, p):
                    chain = Chain(dve, stats_chain, n, 4)
                    norm_stats(dve, nc, chain, h[:, bass.ds(n * G, G), :], xc[:, :, :], sq[:, :, :], total[:, :], var[:, :]).then_inc(var_ready, 1)
                    dve.wait_ge(rstd_ready, n + 1)
                    wait_reuse(dve, xT_ps_ready, n - 1)
                    nc.vector.tensor_tensor(xn[:, p, :, :], xc[:, :, :], bc(rstd[:, :], D), ALU.mult).then_inc(xn_ready, 1)
                    dve.wait_ge(xn_ready, n + 1)
                    chain.end()

                def front(n, p):
                    dve.wait_ge(k_ready, n + 1)
                    wait_reuse(dve, s_ready, n - 1)
                    nc.vector.tensor_copy(kT[:, p, :], k_ps[:, :]).then_inc(k_done, 1)
                    dve.wait_ge(v_ready, n + 1)
                    wait_reuse(dve, o_ready, n - 1)
                    nc.vector.tensor_copy(v[:, p, :, 0:D], v_ps[:, :, :]).then_inc(v_done, 1)

                def attend(n, p):
                    chain = Chain(dve, back_chain, n, 1)
                    dve.wait_ge(s_ready, n + 1)
                    nc.vector.tensor_tensor(s[:, :, :], s_ps[:, :, :], mid(bias[:, 1, :], G), ALU.add).then_inc(biased, 1)
                    dve.wait_ge(biased, n + 1)
                    chain(nc.vector.tensor_reduce(top[:, :], s[:, :, :], X, ALU.max))
                    chain.end()
                    wait_reuse(dve, eT_ready, n)
                    nc.vector.tensor_tensor(e[:, :, :], s[:, :, :], bc(top[:, :], T), ALU.subtract).then_inc(shifted, 1)
                    dve.wait_ge(eT_ready, n + 1)
                    wait_reuse(dve, o_ready, n)
                    nc.vector.tensor_copy(eT[:, :, :], eT_ps[:, :, :]).then_inc(eT_done, 1)
                    chain = Chain(dve, o_chain, n, 3)
                    dve.wait_ge(o_ready, n + 1)
                    chain(nc.vector.reciprocal(rsum[:, :], o_ps[:, :, D]))
                    chain(nc.vector.tensor_tensor(o[:, :, :], o_ps[:, :, 0:D], bc(rsum[:, :], D), ALU.mult))
                    hn = h[:, bass.ds(n * G, G), :]
                    chain(nc.vector.tensor_tensor(hn, hn, o[:, :, :], ALU.add))
                    chain.end()

                pipeline(dve, [norm, front, attend], TILES)

            @block.gpsimd
            def _(pool):
                def powers(n, p):
                    pool.wait_ge(var_ready, n + 1)
                    nc.gpsimd.tensor_tensor(rstd[:, :], var[:, :], S["neg_half"][:, 0:G], ALU.pow).then_inc(rstd_ready, 1)

                pipeline(pool, [powers, None, None], TILES)

            @block.scalar
            def _(act):
                def front(n, p):
                    act.wait_ge(xT_ps_ready, n + 1)
                    wait_reuse(act, v_ready, n - 1)
                    for q in range(2):
                        ins = nc.scalar.copy(xT[0:D, p, :].rearrange("d (g q t) -> d g q t", g=G // 2, q=2)[:, :, q, :],
                                             xT_ps[q * D:(q + 1) * D, :, :])
                    ins.then_inc(xT_ready, 1)
                    act.wait_ge(q_ready, n + 1)
                    wait_reuse(act, s_ready, n - 1)
                    nc.scalar.mul(qT[:, p, :], q_ps[:, :], SCALE).then_inc(q_done, 1)

                def attend(n, p):
                    act.wait_ge(shifted, n + 1)
                    nc.scalar.activation(e[:, :, :], e[:, :, :], ACT.Exp).then_inc(e_ready, 1)

                pipeline(act, [None, front, attend], TILES)

            @block.tensor
            def _(pe):
                pe.wait_ge(consts_set, 2)

                def front(n, p):
                    pe.wait_ge(xn_ready, n + 1)
                    wait_reuse(pe, xT_ready, n)
                    for q in range(G // 2):
                        ins = nc.tensor.transpose(xT_ps[:, q, :], xn[:, p, 2 * q:2 * q + 2, :].rearrange("p g d -> p (g d)"), ident[:, :])
                    ins.then_inc(xT_ps_ready, 1)
                    pe.wait_ge(xT_ready, n + 1)
                    wait_reuse(pe, v_done, n)
                    for g in range(G):
                        ins = nc.tensor.matmul(v_ps[:, g, :], xT[:, p, g * P:(g + 1) * P], S["E_wv"][:, :], start=True, stop=True)
                    ins.then_inc(v_ready, 1)
                    wait_reuse(pe, q_done, n)
                    nc.tensor.matmul(q_ps[:, :], S["E_wq"][:, :], xT[:, p, :], start=True, stop=True).then_inc(q_ready, 1)
                    wait_reuse(pe, k_done, n)
                    nc.tensor.matmul(k_ps[:, :], S["E_wk"][:, :], xT[:, p, :], start=True, stop=True).then_inc(k_ready, 1)

                def scores(n, p):
                    pe.wait_ge(q_done, n + 1)
                    pe.wait_ge(k_done, n + 1)
                    wait_reuse(pe, biased, n)
                    for g in range(G):
                        ins = nc.tensor.matmul(s_ps[:, g, :], qT[:, p, g * P:(g + 1) * P], kT[:, p, g * P:(g + 1) * P], start=True, stop=True)
                    ins.then_inc(s_ready, 1)
                    pe.wait_ge(e_ready, n + 1)
                    wait_reuse(pe, eT_done, n)
                    for g in range(G):
                        ins = nc.tensor.transpose(eT_ps[:, g, :], e[:, g, :], ident[:, :])
                    ins.then_inc(eT_ready, 1)
                    pe.wait_ge(eT_done, n + 1)
                    pe.wait_ge(v_done, n + 1)
                    wait_reuse(pe, o_chain, n * 3)
                    for g in range(G):
                        ins = nc.tensor.matmul(o_ps[:, g, :], eT[:, g, :], v[:, p, g, :], start=True, stop=True)
                    ins.then_inc(o_ready, 1)

                pipeline(pe, [None, front, scores], TILES)


NR = 16
NL = 2
PER_ROUTE = 2


def loads_F(nc, S, A, sb, load, zeroed):
    q = "L2_ffn_"
    load(sb("F_wi", [D + 1, HID])[0:D, :], A[q + "Wi"][:, :])
    load(S["F_wi"][D:D + 1, :], A[q + "bi"].rearrange("(a e) -> a e", a=1))
    mix = sb("F_mix", [HID, NL, NR, HID + 1])
    for l in range(NL):
        load(mix[:, l, :, 0:HID], A[q + "Wr"][l].rearrange("e d j -> d e j"))
    load(sb("F_ws", [HID, NL, HID])[:], A[q + "Ws"].rearrange("l a d j -> d (l a) j"))
    load(sb("F_br", [HID, NL, NR])[:], A[q + "br"][:, :, :])
    load(sb("F_bs", [HID, NL])[:, :], A[q + "bs"].rearrange("j l a -> j (l a)"))
    load(sb("F_wo", [HID, D])[:, :], A[q + "Wo"][:, :])
    load(sb("F_bo", [P, D])[:, :], A[q + "bo"].rearrange("(a n) -> a n", a=1).to_broadcast([P, D]))
    load(sb("F_route", [1, B // PER_ROUTE], I32)[:, :], A[q + "route_id"].rearrange("(a n) -> a n", a=1))


def routed_mlp(nc, S):
    h, ident, mix = S["h"], S["ident"], S["F_mix"]
    R = G // PER_ROUTE
    with ExitStack() as ctx:
        def sb(name, shape, dt=F32):
            return ctx.enter_context(nc.sbuf_tensor(f"F_{name}", shape, dt))

        def ps(name, shape):
            return ctx.enter_context(nc.psum_tensor(f"F_{name}", shape, F32))

        sem = ctx.enter_context(semaphores(nc, "F"))

        xc, sq = sb("xc", [P, G, D]), sb("sq", [P, G, D])
        total, var, rstd = sb("total", [P, G]), sb("var", [P, G]), sb("rstd", [P, G])
        xn = sb("xn", [P, 2, G, D])
        xT = sb("xT", [D + 1, 2, COLS])
        chosen = sb("chosen", [HID, 2, R, NL, HID + 1])
        hid = sb("hid", [HID, 2, COLS])
        deep = sb("deep", [HID, NL, COLS])
        xT_ps = ps("xT_ps", [P, G // 2, P])
        hid_ps, deep_ps, y_ps = ps("hid_ps", [P, COLS]), ps("deep_ps", [P, NL, COLS]), ps("y_ps", [P, G, D])
        names = ("stats_chain var_ready rstd_ready xn_ready xT_ps_ready xT_ready hid_ps_ready hid_ready chosen_ready "
                 "deep_ps_ready deep_ready y_ready y_used mixed").split()
        (stats_chain, var_ready, rstd_ready, xn_ready, xT_ps_ready, xT_ready, hid_ps_ready, hid_ready, chosen_ready,
         deep_ps_ready, deep_ready, y_ready, y_used, mixed) = map(sem, names)

        with nc.Block() as block:
            @block.vector
            def _(dve):
                nc.vector.memset(xT[D:D + 1, :, :], 1.0)
                for l in range(NL):
                    nc.vector.tensor_tensor(S["F_ws"][:, l, :], S["F_ws"][:, l, :], ident[:, :], ALU.add).then_inc(mixed, 1)
                dve.wait_ge(mixed, NL)
                for l in range(NL):
                    nc.vector.tensor_tensor(mix[:, l, :, 0:HID], mix[:, l, :, 0:HID], mid(S["F_ws"][:, l, :], NR), ALU.add)
                    ins = nc.vector.tensor_tensor(mix[:, l, :, HID], S["F_br"][:, l, :],
                                                  S["F_bs"][:, l:l + 1].to_broadcast([HID, NR]), ALU.add)
                ins.then_inc(mixed, 1)

                def norm(n, p):
                    chain = Chain(dve, stats_chain, n, 4)
                    norm_stats(dve, nc, chain, h[:, bass.ds(n * G, G), :], xc[:, :, :], sq[:, :, :], total[:, :], var[:, :]).then_inc(var_ready, 1)
                    dve.wait_ge(rstd_ready, n + 1)
                    wait_reuse(dve, xT_ps_ready, n - 1)
                    nc.vector.tensor_tensor(xn[:, p, :, :], xc[:, :, :], bc(rstd[:, :], D), ALU.mult).then_inc(xn_ready, 1)
                    dve.wait_ge(xn_ready, n + 1)
                    chain.end()

                def output(n, p):
                    dve.wait_ge(y_ready, n + 1)
                    hn = h[:, bass.ds(n * G, G), :]
                    nc.vector.tensor_tensor(hn, hn, y_ps[:, :, :], ALU.add).then_inc(y_used, 1)
                    dve.wait_ge(y_used, 2 * n + 1)
                    nc.vector.tensor_tensor(hn, hn, mid(S["F_bo"][:, :], G), ALU.add).then_inc(y_used, 1)

                pipeline(dve, [norm, None, output], TILES)

            @block.gpsimd
            def _(pool):
                pool.wait_ge(mixed, NL + 1)

                def powers(n, p):
                    pool.wait_ge(var_ready, n + 1)
                    nc.gpsimd.tensor_tensor(rstd[:, :], var[:, :], S["neg_half"][:, 0:G], ALU.pow).then_inc(rstd_ready, 1)

                def choose(n, p):
                    wait_reuse(pool, deep_ready, (n - 1) * NL)
                    for r in range(R):
                        expert = nc.gpsimd.value_load(S["F_route"][0:1, bass.ds(n * R + r, 1)], min_val=0, max_val=NR - 1)
                        ins = nc.gpsimd.tensor_copy(chosen[:, p, r, :, :], mix[:, :, bass.ds(expert, 1), :].rearrange("p l a j -> p l (a j)"))
                    ins.then_inc(chosen_ready, 1)

                pipeline(pool, [powers, choose, None], TILES)

            @block.scalar
            def _(act):
                def front(n, p):
                    act.wait_ge(xT_ps_ready, n + 1)
                    wait_reuse(act, hid_ps_ready, n - 1)
                    for q in range(2):
                        ins = nc.scalar.copy(xT[0:D, p, :].rearrange("d (g q t) -> d g q t", g=G // 2, q=2)[:, :, q, :],
                                             xT_ps[q * D:(q + 1) * D, :, :])
                    ins.then_inc(xT_ready, 1)
                    act.wait_ge(hid_ps_ready, n + 1)
                    wait_reuse(act, deep_ps_ready, (n - 1) * NL)
                    nc.scalar.activation(hid[:, p, :], hid_ps[:, :], ACT.Relu).then_inc(hid_ready, 1)

                def layers(n, p):
                    for l in range(NL):
                        act.wait_ge(deep_ps_ready, n * NL + l + 1)
                        if l == NL - 1:
                            wait_reuse(act, y_ready, n)
                        for r in range(R):
                            cols = slice(r * COLS // R, (r + 1) * COLS // R)
                            ins = nc.scalar.activation(deep[:, l, cols], deep_ps[:, l, cols], ACT.Relu,
                                                       bias=chosen[:, p, r, l, HID:HID + 1])
                        ins.then_inc(deep_ready, 1)

                pipeline(act, [None, front, layers], TILES)

            @block.tensor
            def _(pe):
                pe.wait_ge(mixed, NL + 1)

                def front(n, p):
                    pe.wait_ge(xn_ready, n + 1)
                    wait_reuse(pe, xT_ready, n)
                    for q in range(G // 2):
                        ins = nc.tensor.transpose(xT_ps[:, q, :], xn[:, p, 2 * q:2 * q + 2, :].rearrange("p g d -> p (g d)"), ident[:, :])
                    ins.then_inc(xT_ps_ready, 1)
                    pe.wait_ge(xT_ready, n + 1)
                    wait_reuse(pe, hid_ready, n)
                    nc.tensor.matmul(hid_ps[:, :], S["F_wi"][:, :], xT[:, p, :], start=True, stop=True).then_inc(hid_ps_ready, 1)

                def layers(n, p):
                    pe.wait_ge(chosen_ready, n + 1)
                    pe.wait_ge(hid_ready, n + 1)
                    for l in range(NL):
                        if l:
                            pe.wait_ge(deep_ready, n * NL + l)
                        wait_reuse(pe, deep_ready, (n - 1) * NL + l + 1)
                        src = deep[:, l - 1, :] if l else hid[:, p, :]
                        for r in range(R):
                            cols = slice(r * COLS // R, (r + 1) * COLS // R)
                            ins = nc.tensor.matmul(deep_ps[:, l, cols], chosen[:, p, r, l, 0:HID], src[:, cols], start=True, stop=True)
                        ins.then_inc(deep_ps_ready, 1)
                    pe.wait_ge(deep_ready, (n + 1) * NL)
                    wait_reuse(pe, y_used, 2 * n - 1)
                    for g in range(G):
                        ins = nc.tensor.matmul(y_ps[:, g, :], deep[:, NL - 1, g * P:(g + 1) * P], S["F_wo"][:, :], start=True, stop=True)
                    ins.then_inc(y_ready, 1)

                pipeline(pe, [None, front, layers], TILES)


NST = 16
TAPS = 4
RANK = 4
DIRS = "fb"
PAD = T + TAPS


def constants_G(c):
    c["part_rows"] = np.tile(np.eye(2 * NST, dtype=np.float32), (3, 1))


def loads_G(nc, S, A, sb, load, zeroed):
    load(sb("G_rows", [96, 2 * NST])[:, :], A["part_rows"][:, :])
    for k, c in enumerate(DIRS):
        q = f"L3_attn_{c}_"
        w_in = sb("G_in" + c, [2 * D, 2 * P])
        for u in range(2):
            load(w_in[u * D:(u + 1) * D, :], A[q + "in_w"][:, :])
        taps = sb("G_taps" + c, [2 * D, 2, P])
        for u in range(2):
            for j in range(2):
                k_tap = TAPS - 1 - (2 * j + u)
                load(taps[u * D:(u + 1) * D, j, :], A[q + "conv_w"][k_tap:k_tap + 1, :].to_broadcast([D, P]))
        xp = sb("G_xproj" + c, [P, 2 * NST + RANK])
        load(xp[:, 0:2 * NST], A[q + "xproj_w"][:, RANK:])
        load(xp[:, 2 * NST:], A[q + "xproj_w"][:, 0:RANK])
        load(sb("G_dt" + c, [2 * NST + RANK, P])[2 * NST:, :], A[q + "dt_w"][:, :])
        for v in ("conv_b", "dt_b", "D"):
            load(sb(f"G_{v}{c}", [P, 1])[:, :], A[q + v].rearrange("(d a) -> d a", a=1))
        load(sb("G_a" + c, [P, NST])[:, :], A[q + "A_log"][:, :])
        load(sb("G_out" + c, [P, D])[:, :], A[q + "out_w"][:, :])


def mamba(nc, S):
    h, ident = S["h"], S["ident"]
    SLOTS = 2 * NST
    LAG = 3
    with ExitStack() as ctx:
        def sb(name, shape, dt=F32):
            return ctx.enter_context(nc.sbuf_tensor(f"G_{name}", shape, dt))

        def ps(name, shape):
            return ctx.enter_context(nc.psum_tensor(f"G_{name}", shape, F32))

        sem = ctx.enter_context(semaphores(nc, "G"))

        xc, sq = sb("xc", [P, G, D]), sb("sq", [P, G, D])
        total, var, rstd = sb("total", [P, G]), sb("var", [P, G]), sb("rstd", [P, G])
        xn = sb("xn", [P, 2, G, D])
        xp = sb("xp", [2 * D, 2, G, PAD])
        conv = sb("conv", [2 * D, 2, 2, P])
        u = sb("u", [P, 2, 2, COLS])
        zg = sb("zg", [P, 2, 2, COLS])
        low = sb("low", [2 * NST + RANK, 2, COLS])
        parts = sb("parts", [96, 2, 2, COLS], BF16)
        rest = sb("rest", [2 * NST, 2, COLS])
        middle = sb("middle", [2 * NST, COLS], BF16)
        rows = sb("rows16", [96, 2 * NST], BF16)
        mag, ln = sb("mag", [P, 2, COLS]), sb("ln", [P, 2, COLS])
        round1, one = sb("round1", [P, COLS]), sb("one", [P, 1])
        positive = sb("positive", [P, 2, COLS])
        dt, du = sb("dt", [P, 2, 2, COLS]), sb("du", [P, 2, 2, COLS])
        decay = sb("decay", [P, 4, G, T])
        drive = sb("drive", [P, 2, COLS])
        state = sb("state", [P, 4, COLS])
        c_wide = sb("c_wide", [P, 4, COLS])
        weighted = sb("weighted", [P, 4, COLS])
        mixed, gated = sb("mixed", [P, COLS]), sb("gated", [P, COLS])
        ring_ps, b_ps, c_ps = ps("ring_ps", [P, 2, COLS]), ps("b_ps", [P, 2, COLS]), ps("c_ps", [P, 2, COLS])
        y_ps, out_ps = ps("y_ps", [P, COLS]), ps("out_ps", [P, G, D])
        names = ("stats_chain var_ready rstd_ready xn_ready h_plus turned xp_ready conv_ready u_ready z_ready zg_ready low_ps low_ready "
                 "high_ready split_chain parts_ready dt_ps mag_ready exp_ready ln_ready positive_ready dt_chain dt_ready du_ready "
                 "b_ready c_ready decay_ready c_copied driven scanned weighted_done summed mixed_done gated_done out_ready h_done "
                 "setup setup_a").split()
        (stats_chain, var_ready, rstd_ready, xn_ready, h_plus, turned, xp_ready, conv_ready, u_ready, z_ready, zg_ready, low_ps, low_ready,
         high_ready, split_chain, parts_ready, dt_ps, mag_ready, exp_ready, ln_ready, positive_ready, dt_chain, dt_ready, du_ready,
         b_ready, c_ready, decay_ready, c_copied, driven, scanned, weighted_done, summed, mixed_done, gated_done, out_ready, h_done,
         setup, setup_a) = map(sem, names)

        with nc.Block() as block:
            @block.vector
            def _(dve):
                nc.vector.memset(xp[:], 0.0)
                nc.vector.memset(one[:], 1.0)
                nc.vector.memset(decay[:], 0.0)
                nc.vector.tensor_copy(rows[:, :], S["G_rows"][:, :])
                for k, c in enumerate(DIRS):
                    for j in range(2):
                        nc.vector.tensor_tensor(conv[:, k, j, :], S["G_in" + c][:, 0:P], S["G_taps" + c][:, j, :], ALU.mult)
                    nc.vector.tensor_scalar(S["G_a" + c][:, :], S["G_a" + c][:, :], 80.0, None, ALU.min).then_inc(setup, 1)
                dve.wait_ge(setup_a, 2)
                for c in DIRS:
                    nc.vector.tensor_scalar(S["G_a" + c][:, :], S["G_a" + c][:, :], -1.0, None, ALU.mult)

            @block.scalar
            def _(act):
                act.wait_ge(setup, 2)
                for c in DIRS:
                    nc.scalar.activation(S["G_a" + c][:, :], S["G_a" + c][:, :], ACT.Exp).then_inc(setup_a, 1)

        def run(eng, norm, front, finish, slot_work):
            def work(n, p):
                if isinstance(n, int) and n == 0:
                    for slot in range(SLOTS):
                        front(slot, 0, p)
                for slot in range(SLOTS):
                    if not (isinstance(n, int) and n == 0 and slot < SLOTS // 2):
                        finish(slot, n - 1 if slot < NST else n, 1 - p if slot < NST else p)
                    if not (isinstance(n, int) and n == TILES - 1):
                        front(slot, n + 1, 1 - p)
                    slot_work(slot, n, p)

            pipeline(eng, [norm, None, work], TILES)
            for slot in range(NST):
                finish(slot, TILES - 1, (TILES - 1) % 2)

        def nothing(*_):
            pass

        with nc.Block() as block:
            @block.vector
            def _(dve):
                def norm(n, p):
                    chain = Chain(dve, stats_chain, n, 4)
                    hn = h[:, bass.ds(n * G, G), :]
                    norm_stats(dve, nc, chain, hn, xc[:, :, :], sq[:, :, :], total[:, :], var[:, :]).then_inc(var_ready, 1)
                    dve.wait_ge(rstd_ready, n + 1)
                    wait_reuse(dve, turned, n - 1)
                    nc.vector.tensor_tensor(xn[:, p, :, :], xc[:, :, :], bc(rstd[:, :], D), ALU.mult).then_inc(xn_ready, 1)
                    dve.wait_ge(xn_ready, n + 1)
                    nc.vector.tensor_tensor(hn, hn, xn[:, p, :, :], ALU.add).then_inc(h_plus, 1)
                    chain.end()

                def front(slot, n, p):
                    if slot in (14, 15):
                        k = slot - 14
                        chain = Chain(dve, split_chain, n * 2 + k, 3)
                        dve.wait_ge(high_ready, n * 2 + k + 1)
                        wait_reuse(dve, c_ready, (n * 2 + k - 3) * NST)
                        chain(nc.vector.tensor_tensor(rest[:, 0, :], low[0:32, k, :], parts[0:32, p, k, :], ALU.subtract))
                        chain(nc.vector.tensor_copy(middle[:, :], rest[:, 0, :]))
                        nc.vector.tensor_copy(parts[32:64, p, k, :], middle[:, :])
                        chain(nc.vector.tensor_tensor(rest[:, 1, :], rest[:, 0, :], middle[:, :], ALU.subtract))
                        nc.vector.tensor_copy(parts[64:96, p, k, :], rest[:, 1, :]).then_inc(parts_ready, 1)
                        chain.end()
                    if slot in (17, 18):
                        k = slot - 17
                        dve.wait_ge(mag_ready, n * 2 + k + 1)
                        wait_reuse(dve, dt_ready, (n - 1) * 2 + k + 1)
                        nc.vector.tensor_scalar(positive[:, k, :], ring_ps[:, k, :], S["G_dt_b" + DIRS[k]][:, 0:1], 0.0,
                                                ALU.add, ALU.max).then_inc(positive_ready, 1)

                def finish(slot, n, p):
                    k = 1 if slot < NST else 0
                    m = n * 2 + k
                    if slot % NST == LAG:
                        dve.wait_ge(summed, (m + 1) * NST)
                        nc.vector.scalar_tensor_tensor(out=mixed[:, :], in0=u[:, p, k, :], scalar=S["G_D" + DIRS[k]][:, 0:1],
                                                       in1=y_ps[:, :], op0=ALU.mult, op1=ALU.add).then_inc(mixed_done, 1)
                        dve.wait_ge(mixed_done, m + 1)
                        wait_reuse(dve, out_ready, m)
                        nc.vector.tensor_tensor(gated[:, :], mixed[:, :], zg[:, p, k, :], ALU.mult).then_inc(gated_done, 1)
                    if slot % NST == LAG + 2:
                        dve.wait_ge(out_ready, m + 1)
                        wait_reuse(dve, h_done, m)
                        dve.wait_ge(h_plus, n + 1)
                        hn = h[:, bass.ds(n * G, G), :]
                        nc.vector.tensor_tensor(hn, hn, out_ps[:, :, :], ALU.add).then_inc(h_done, 1)

                def slot_work(slot, n, p):
                    k, s, m = slot // NST, slot % NST, n * SLOTS + slot
                    if s == 0:
                        dve.wait_ge(du_ready, n * 2 + k + 1)
                    dve.wait_ge(b_ready, m + 1)
                    wait_reuse(dve, scanned, m - 1)
                    nc.vector.tensor_tensor(drive[:, slot % 2, :], b_ps[:, slot % 2, :], du[:, p, k, :], ALU.mult).then_inc(driven, 1)
                    dve.wait_ge(decay_ready, m + 1)
                    wait_reuse(dve, weighted_done, m - 3)
                    dve.wait_ge(driven, m + 1)
                    nc.vector.tensor_tensor_scan(state[:, slot % 4, :], decay[:, slot % 4, :, :].rearrange("p g t -> p (g t)"),
                                                 drive[:, slot % 2, :], 0.0, ALU.mult, ALU.add).then_inc(scanned, 1)

                run(dve, norm, front, finish, slot_work)

            @block.gpsimd
            def _(pool):
                def norm(n, p):
                    pool.wait_ge(var_ready, n + 1)
                    nc.gpsimd.tensor_tensor(rstd[:, :], var[:, :], S["neg_half"][:, 0:G], ALU.pow).then_inc(rstd_ready, 1)

                def front(slot, n, p):
                    if slot in (20, 22):
                        k = (slot - 20) // 2
                        m = n * 2 + k
                        chain = Chain(pool, dt_chain, m, 4)
                        pool.wait_ge(exp_ready, m + 1)
                        ones = one[:, :].to_broadcast([P, COLS])
                        chain(nc.gpsimd.tensor_tensor(round1[:, :], mag[:, k, :], ones, ALU.add))
                        chain(nc.gpsimd.tensor_tensor(round1[:, :], round1[:, :], ones, ALU.subtract))
                        chain(nc.gpsimd.tensor_tensor(round1[:, :], round1[:, :], mag[:, k, :], ALU.subtract))
                        pool.wait_ge(ln_ready, m + 1)
                        chain(nc.gpsimd.tensor_tensor(round1[:, :], ln[:, k, :], round1[:, :], ALU.subtract))
                        pool.wait_ge(positive_ready, m + 1)
                        wait_reuse(pool, decay_ready, (m - 3) * NST)
                        nc.gpsimd.tensor_tensor(dt[:, p, k, :], round1[:, :], positive[:, k, :], ALU.add).then_inc(dt_ready, 1)
                        pool.wait_ge(dt_ready, m + 1)
                        wait_reuse(pool, driven, (m - 3) * NST)
                        nc.gpsimd.tensor_tensor(du[:, p, k, :], dt[:, p, k, :], u[:, p, k, :], ALU.mult).then_inc(du_ready, 1)
                        chain.end()

                def slot_work(slot, n, p):
                    m = n * SLOTS + slot
                    pool.wait_ge(scanned, m + 1)
                    pool.wait_ge(c_copied, m + 1)
                    wait_reuse(pool, summed, m - 3)
                    nc.gpsimd.tensor_tensor(weighted[:, slot % 4, :], state[:, slot % 4, :], c_wide[:, slot % 4, :], ALU.mult).then_inc(weighted_done, 1)

                run(pool, norm, front, nothing, slot_work)

            @block.scalar
            def _(act):
                def front(slot, n, p):
                    if slot == 7:
                        act.wait_ge(turned, n + 1)
                        wait_reuse(act, z_ready, (n - 1) * 2)
                        for q in range(2):
                            src = ring_ps[q * D:(q + 1) * D, 0, 0:2 * P].rearrange("p (g t) -> p g t", g=2)
                            for later in range(2):
                                dst = xp[later * D:(later + 1) * D, p, :, TAPS - 1 + later:TAPS - 1 + later + T]
                                ins = nc.scalar.copy(dst.rearrange("d (g q) t -> d g q t", q=2)[:, :, q, :], src)
                        ins.then_inc(xp_ready, 1)
                    if slot == 9:
                        for k in range(2):
                            act.wait_ge(conv_ready, n * 2 + k + 1)
                            wait_reuse(act, gated_done, (n - 1) * 2)
                            nc.scalar.activation(u[:, p, k, :], ring_ps[:, k, :], ACT.Silu, bias=S["G_conv_b" + DIRS[k]][:, :]).then_inc(u_ready, 1)
                    if slot == 11:
                        for k in range(2):
                            act.wait_ge(z_ready, n * 2 + k + 1)
                            nc.scalar.activation(zg[:, p, k, :], ring_ps[:, k, :], ACT.Silu).then_inc(zg_ready, 1)
                    if slot == 13:
                        for k in range(2):
                            m = n * 2 + k
                            act.wait_ge(low_ps, m + 1)
                            wait_reuse(act, parts_ready, m - 1)
                            wait_reuse(act, dt_ps, m - 1)
                            nc.scalar.copy(low[:, k, :], ring_ps[0:2 * NST + RANK, k, :]).then_inc(low_ready, 1)
                            act.wait_ge(low_ready, m + 1)
                            wait_reuse(act, c_ready, (m - 3) * NST)
                            nc.scalar.copy(parts[0:32, p, k, :], low[0:32, k, :]).then_inc(high_ready, 1)
                    if slot == 16:
                        for k in range(2):
                            m = n * 2 + k
                            act.wait_ge(dt_ps, m + 1)
                            wait_reuse(act, dt_ready, m - 1)
                            nc.scalar.activation(mag[:, k, :], ring_ps[:, k, :], ACT.Abs, bias=S["G_dt_b" + DIRS[k]][:, :]).then_inc(mag_ready, 1)
                    if slot == 18:
                        for k in range(2):
                            m = n * 2 + k
                            act.wait_ge(mag_ready, m + 1)
                            nc.scalar.activation(mag[:, k, :], mag[:, k, :], ACT.Exp, scale=-1.0).then_inc(exp_ready, 1)
                            act.wait_ge(exp_ready, m + 1)
                            nc.scalar.activation(ln[:, k, :], mag[:, k, :], ACT.Ln, bias=1.0).then_inc(ln_ready, 1)

                def slot_work(slot, n, p):
                    k, s, m = slot // NST, slot % NST, n * SLOTS + slot
                    if s == 0:
                        act.wait_ge(dt_ready, n * 2 + k + 1)
                    wait_reuse(act, scanned, m - 3)
                    nc.scalar.activation(decay[:, slot % 4, :, 1:], dt[:, p, k, :].rearrange("p (g t) -> p g t", g=G)[:, :, 1:],
                                         ACT.Exp, scale=S["G_a" + DIRS[k]][:, s:s + 1]).then_inc(decay_ready, 1)
                    act.wait_ge(c_ready, m + 1)
                    wait_reuse(act, weighted_done, m - 3)
                    nc.scalar.copy(c_wide[:, slot % 4, :], c_ps[:, slot % 2, :]).then_inc(c_copied, 1)

                run(act, None, front, nothing, slot_work)

            @block.tensor
            def _(pe):
                def front(slot, n, p):
                    if slot == 6:
                        pe.wait_ge(xn_ready, n + 1)
                        wait_reuse(pe, positive_ready, n * 2)
                        for q in range(G // 2):
                            ins = nc.tensor.transpose(ring_ps[:, 0, q * P:(q + 1) * P], xn[:, p, 2 * q:2 * q + 2, :].rearrange("p g d -> p (g d)"), ident[:, :])
                        ins.then_inc(turned, 1)
                    if slot == 8:
                        pe.wait_ge(xp_ready, n + 1)
                        for k in range(2):
                            for j in range(2):
                                at = TAPS - 1 - 2 * j
                                ins = nc.tensor.matmul(ring_ps[:, k, :], conv[:, k, j, :], xp[:, p, :, at:at + T], start=(j == 0), stop=(j == 1))
                            ins.then_inc(conv_ready, 1)
                    if slot == 10:
                        for k in range(2):
                            pe.wait_ge(u_ready, n * 2 + k + 1)
                            nc.tensor.matmul(ring_ps[:, k, :], S["G_in" + DIRS[k]][0:D, P:], xp[0:D, p, :, TAPS - 1:TAPS - 1 + T],
                                             start=True, stop=True).then_inc(z_ready, 1)
                    if slot == 12:
                        for k in range(2):
                            pe.wait_ge(zg_ready, n * 2 + k + 1)
                            nc.tensor.matmul(ring_ps[0:2 * NST + RANK, k, :], S["G_xproj" + DIRS[k]][:, :], u[:, p, k, :],
                                             start=True, stop=True).then_inc(low_ps, 1)
                    if slot == 15:
                        for k in range(2):
                            pe.wait_ge(low_ready, n * 2 + k + 1)
                            nc.tensor.matmul(ring_ps[:, k, :], S["G_dt" + DIRS[k]][2 * NST:, :], low[2 * NST:, k, :],
                                             start=True, stop=True).then_inc(dt_ps, 1)

                def finish(slot, n, p):
                    k = 1 if slot < NST else 0
                    m = n * 2 + k
                    if slot % NST < LAG:
                        add_state(NST - LAG + slot % NST, k, m)
                    if slot % NST == LAG + 1:
                        pe.wait_ge(gated_done, m + 1)
                        wait_reuse(pe, h_done, m)
                        for g in range(G):
                            ins = nc.tensor.matmul(out_ps[:, g, :], gated[:, g * P:(g + 1) * P], S["G_out" + DIRS[k]][:, :], start=True, stop=True)
                        ins.then_inc(out_ready, 1)

                def add_state(s, k, m):
                    pe.wait_ge(weighted_done, m * NST + s + 1)
                    if s == 0:
                        wait_reuse(pe, mixed_done, m)
                    nc.tensor.matmul(y_ps[:, :], ident[:, :], weighted[:, s % 4, :], start=(s == 0), stop=(s == NST - 1)).then_inc(summed, 1)

                def slot_work(slot, n, p):
                    k, s, m = slot // NST, slot % NST, n * SLOTS + slot
                    if s == 0:
                        pe.wait_ge(parts_ready, n * 2 + k + 1)
                    wait_reuse(pe, driven, m - 1)
                    nc.tensor.matmul(b_ps[:, slot % 2, :], rows[:, s:s + 1].to_broadcast([96, P]), parts[:, p, k, :], start=True, stop=True).then_inc(b_ready, 1)
                    wait_reuse(pe, c_copied, m - 1)
                    nc.tensor.matmul(c_ps[:, slot % 2, :], rows[:, NST + s:NST + s + 1].to_broadcast([96, P]), parts[:, p, k, :],
                                     start=True, stop=True).then_inc(c_ready, 1)
                    if s >= LAG:
                        add_state(s - LAG, k, n * 2 + k)

                run(pe, None, front, finish, slot_work)


NP = NE // 2
BN_EPS = 1e-3


def loads_H(nc, S, A, sb, load, zeroed):
    q = "L3_ffn_"
    load(sb("H_wr", [D + 1, NE])[0:D, :], A[q + "Wr"][:, :])
    load(S["H_wr"][D:D + 1, :], A[q + "br"].rearrange("(a e) -> a e", a=1))
    load(sb("H_w1", [D, NE, D])[:], A[q + "W1"].rearrange("e d k -> d e k"))
    w2 = sb("H_w2", [P, NP, P])
    zeroed.append(w2)
    wo = sb("H_wo", [P, NP, D])
    for k in range(2):
        rows = slice(k * D, (k + 1) * D)
        load(w2[rows, :, rows], A[q + "W2"].rearrange("(u k) h j -> k h u j", k=2)[k])
        load(wo[rows, :, :], A[q + "Wo"].rearrange("(u k) h d -> k h u d", k=2)[k])
    load(sb("H_bo", [NE, D])[:, :], A[q + "bo"][:, :])
    for k in "12":
        for v in ("b", "g", "be", "m", "v"):
            load(sb(f"H_{v}{k}", [P, NP])[:, :], A[f"{q}{v}{k}"][:, :])


def gated_towers(nc, S):
    h, ident = S["h"], S["ident"]
    with ExitStack() as ctx:
        def sb(name, shape, dt=F32):
            return ctx.enter_context(nc.sbuf_tensor(f"H_{name}", shape, dt))

        def ps(name, shape):
            return ctx.enter_context(nc.psum_tensor(f"H_{name}", shape, F32))

        sem = ctx.enter_context(semaphores(nc, "H"))

        xn_all = sb("xn_all", [P, B, D])
        xc, sq = sb("xc", [P, G, D]), sb("sq", [P, G, D])
        total, var, rstd = sb("total", [P, G]), sb("var", [P, G]), sb("rstd", [P, G])
        stats_chain, var_ready, rstd_ready, xn_ready = sem("stats_chain"), sem("var_ready"), sem("rstd_ready"), sem("xn_ready")
        scale = [sb("scale1", [P, NP]), sb("scale2", [P, NP])]
        shift = [sb("shift1", [P, NP]), sb("shift2", [P, NP])]
        feat = sb("feat", [P, D])
        featT = sb("featT", [D + 1, P])
        w = sb("w", [P, NE])
        w_wide = sb("w_wide", [P, NE, D])
        wT = sb("wT", [NE, P])
        w_pair = sb("w_pair", [P, NP, P])
        bo_mix = sb("bo_mix", [P, D])
        small = sb("small", [P, 2])

        with nc.Block() as block:
            @block.vector
            def _(dve):
                def norm(n, p):
                    chain = Chain(dve, stats_chain, n, 4)
                    norm_stats(dve, nc, chain, h[:, bass.ds(n * G, G), :], xc[:, :, :], sq[:, :, :], total[:, :], var[:, :]).then_inc(var_ready, 1)
                    dve.wait_ge(rstd_ready, n + 1)
                    nc.vector.tensor_tensor(xn_all[:, bass.ds(n * G, G), :], xc[:, :, :], bc(rstd[:, :], D), ALU.mult).then_inc(xn_ready, 1)
                    dve.wait_ge(xn_ready, n + 1)
                    chain.end()

                pipeline(dve, [norm], TILES)

            @block.gpsimd
            def _(pool):
                def powers(n, p):
                    pool.wait_ge(var_ready, n + 1)
                    nc.gpsimd.tensor_tensor(rstd[:, :], var[:, :], S["neg_half"][:, 0:G], ALU.pow).then_inc(rstd_ready, 1)

                pipeline(pool, [powers], TILES)

        with ExitStack() as c2:
            once = c2.enter_context(semaphores(nc, "H_once"))

            featT_ps = c2.enter_context(nc.psum_tensor("H_featT_ps", [D, P], F32))
            w_ps = c2.enter_context(nc.psum_tensor("H_w_ps", [P, NE], F32))
            wT_ps = c2.enter_context(nc.psum_tensor("H_wT_ps", [NE, P], F32))
            pair_ps = c2.enter_context(nc.psum_tensor("H_pair_ps", [P, NP, P], F32))
            mix_ps = c2.enter_context(nc.psum_tensor("H_mix_ps", [P, D], F32))
            chain_sem, feat_ready, turned, featT_ready, logits, shifted, exps, w_ready, wT_turned, wT_ready, mixed, vplus, vroot = map(
                once, "chain feat_ready turned featT_ready logits shifted exps w_ready wT_turned wT_ready mixed vplus vroot".split())
            with nc.Block() as block:
                @block.vector
                def _(dve):
                    chain = Chain(dve, chain_sem, 0, 14)
                    nc.vector.tensor_scalar(scale[0][:, :], S["H_v1"][:, :], BN_EPS, None, ALU.add)
                    nc.vector.tensor_scalar(scale[1][:, :], S["H_v2"][:, :], BN_EPS, None, ALU.add).then_inc(vplus, 1)
                    nc.vector.memset(featT[D:D + 1, :], 1.0)
                    chain(nc.vector.tensor_reduce(feat[:, :], xn_all[:, :, :].rearrange("p b d -> p d b"), X, ALU.add))
                    nc.vector.tensor_scalar(feat[:, :], feat[:, :], 1.0 / B, None, ALU.mult).then_inc(feat_ready, 1)
                    dve.wait_ge(turned, 1)
                    nc.vector.tensor_copy(featT[0:D, :], featT_ps[:, :]).then_inc(featT_ready, 1)
                    dve.wait_ge(vroot, 2)
                    for k in range(2):
                        c = "12"[k]
                        chain(nc.vector.tensor_tensor(scale[k][:, :], scale[k][:, :], S["H_g" + c][:, :], ALU.mult))
                        chain(nc.vector.tensor_tensor(shift[k][:, :], S["H_b" + c][:, :], S["H_m" + c][:, :], ALU.subtract))
                        chain(nc.vector.tensor_tensor(shift[k][:, :], shift[k][:, :], scale[k][:, :], ALU.mult))
                        chain(nc.vector.tensor_tensor(shift[k][:, :], shift[k][:, :], S["H_be" + c][:, :], ALU.add))
                    dve.wait_ge(logits, 1)
                    chain(nc.vector.tensor_reduce(small[:, 0:1], w_ps[:, :], X, ALU.max))
                    nc.vector.tensor_scalar(w[:, :], w_ps[:, :], small[:, 0:1], None, ALU.subtract).then_inc(shifted, 1)
                    dve.wait_ge(exps, 1)
                    chain(nc.vector.tensor_reduce(small[:, 0:1], w[:, :], X, ALU.add))
                    chain(nc.vector.reciprocal(small[:, 1:2], small[:, 0:1]))
                    chain(nc.vector.tensor_scalar(w[:, :], w[:, :], small[:, 1:2], None, ALU.mult))
                    nc.vector.tensor_copy(w_wide[:, :, :], bc(w[:, :], D)).then_inc(w_ready, 1)
                    dve.wait_ge(wT_turned, 1)
                    chain(nc.vector.tensor_copy(wT[:, :], wT_ps[:, :]))
                    nc.vector.tensor_copy(w_pair[:, :, :], pair_ps[:, :, :]).then_inc(wT_ready, 1)
                    dve.wait_ge(mixed, 1)
                    nc.vector.tensor_copy(bo_mix[:, :], mix_ps[:, :])
                    chain.end()

                @block.gpsimd
                def _(pool):
                    pool.wait_ge(vplus, 1)
                    for k in range(2):
                        nc.gpsimd.tensor_tensor(scale[k][:, :], scale[k][:, :], S["neg_half"][:, 0:NP], ALU.pow).then_inc(vroot, 1)

                @block.scalar
                def _(act):
                    act.wait_ge(shifted, 1)
                    nc.scalar.activation(w[:, :], w[:, :], ACT.Exp).then_inc(exps, 1)

                @block.tensor
                def _(pe):
                    pe.wait_ge(feat_ready, 1)
                    nc.tensor.transpose(featT_ps[:, :], feat[:, :], ident[:, :]).then_inc(turned, 1)
                    pe.wait_ge(featT_ready, 1)
                    nc.tensor.matmul(w_ps[:, :], featT[:, :], S["H_wr"][:, :], start=True, stop=True).then_inc(logits, 1)
                    pe.wait_ge(w_ready, 1)
                    for u in range(NP):
                        nc.tensor.transpose(pair_ps[:, u, :], w_wide[:, 2 * u:2 * u + 2, :].rearrange("p e d -> p (e d)"), ident[:, :])
                    nc.tensor.transpose(wT_ps[:, :], w[:, :], ident[:, :]).then_inc(wT_turned, 1)
                    pe.wait_ge(wT_ready, 1)
                    nc.tensor.matmul(mix_ps[:, :], wT[:, :], S["H_bo"][:, :], start=True, stop=True).then_inc(mixed, 1)

        xs = sb("xs", [P, 2, G, D])
        xT = sb("xT", [D, 2, COLS])
        one = sb("one", [P, NP, COLS])
        two = sb("two", [P, NP, COLS])
        out = sb("out", [P, COLS])
        xT_ps = ps("xT_ps", [P, G // 2, P])
        one_ps, two_ps = ps("one_ps", [P, 2, COLS]), ps("two_ps", [P, 2, COLS])
        out_ps, back_ps = ps("out_ps", [D, COLS]), ps("back_ps", [P, G, P])
        (fetched, xT_ps_ready, xT_ready, one_filled, one_ready, two_filled, two_ready, gated, out_filled, out_ready,
         back_ready, h_done, cleared) = map(sem, "fetched xT_ps_ready xT_ready one_filled one_ready two_filled two_ready gated out_filled out_ready back_ready h_done cleared".split())
        with nc.Block() as block:
            @block.gpsimd
            def _(pool):
                def fetch(n, p):
                    wait_reuse(pool, xT_ps_ready, n - 1)
                    nc.gpsimd.tensor_copy(xs[:, p, :, :], xn_all[:, bass.ds(n * G, G), :]).then_inc(fetched, 1)

                nc.gpsimd.memset(out[D:, :], 0.0).then_inc(cleared, 1)
                pool.wait_ge(cleared, 1)
                pipeline(pool, [fetch, None, None], TILES)

            @block.vector
            def _(dve):
                def towers(n, p):
                    for u in range(NP):
                        dve.wait_ge(two_ready, n * NP + u + 1)
                        nc.vector.tensor_tensor(two[:, u, :].rearrange("p (g t) -> p g t", g=G), two[:, u, :].rearrange("p (g t) -> p g t", g=G),
                                                mid(w_pair[:, u, :], G), ALU.mult).then_inc(gated, 1)
                    dve.wait_ge(back_ready, n + 1)
                    hn = h[:, bass.ds(n * G, G), :]
                    nc.vector.tensor_tensor(hn, hn, back_ps[:, :, 0:D], ALU.add).then_inc(h_done, 1)
                    dve.wait_ge(h_done, 2 * n + 1)
                    nc.vector.tensor_tensor(hn, hn, mid(bo_mix[:, :], G), ALU.add).then_inc(h_done, 1)

                pipeline(dve, [None, None, towers], TILES)

            @block.scalar
            def _(act):
                def front(n, p):
                    act.wait_ge(xT_ps_ready, n + 1)
                    wait_reuse(act, one_filled, (n - 1) * NP)
                    for q in range(2):
                        ins = nc.scalar.copy(xT[:, p, :].rearrange("d (g q t) -> d g q t", g=G // 2, q=2)[:, :, q, :],
                                             xT_ps[q * D:(q + 1) * D, :, :])
                    ins.then_inc(xT_ready, 1)

                def towers(n, p):
                    for u in range(NP):
                        act.wait_ge(one_filled, n * NP + u + 1)
                        wait_reuse(act, two_filled, (n - 1) * NP + u + 1)
                        nc.scalar.activation(one[:, u, :], one_ps[:, u % 2, :], ACT.Relu, bias=shift[0][:, u:u + 1],
                                             scale=scale[0][:, u:u + 1]).then_inc(one_ready, 1)
                    for u in range(NP):
                        act.wait_ge(two_filled, n * NP + u + 1)
                        wait_reuse(act, out_filled, n)
                        nc.scalar.activation(two[:, u, :], two_ps[:, u % 2, :], ACT.Relu, bias=shift[1][:, u:u + 1],
                                             scale=scale[1][:, u:u + 1]).then_inc(two_ready, 1)
                    act.wait_ge(out_filled, n + 1)
                    wait_reuse(act, back_ready, n)
                    nc.scalar.copy(out[0:D, :], out_ps[:, :]).then_inc(out_ready, 1)

                pipeline(act, [None, front, towers], TILES)

            @block.tensor
            def _(pe):
                def front(n, p):
                    pe.wait_ge(fetched, n + 1)
                    wait_reuse(pe, xT_ready, n)
                    for q in range(G // 2):
                        ins = nc.tensor.transpose(xT_ps[:, q, :], xs[:, p, 2 * q:2 * q + 2, :].rearrange("p g d -> p (g d)"), ident[:, :])
                    ins.then_inc(xT_ps_ready, 1)

                def towers(n, p):
                    pe.wait_ge(xT_ready, n + 1)
                    for u in range(NP):
                        wait_reuse(pe, one_ready, n * NP + u - 1)
                        nc.tensor.matmul(one_ps[:, u % 2, :], S["H_w1"][:, 2 * u:2 * u + 2, :].rearrange("d e k -> d (e k)"), xT[:, p, :],
                                         start=True, stop=True).then_inc(one_filled, 1)
                    for u in range(NP):
                        pe.wait_ge(one_ready, n * NP + u + 1)
                        wait_reuse(pe, two_ready, n * NP + u - 1)
                        nc.tensor.matmul(two_ps[:, u % 2, :], S["H_w2"][:, u, :], one[:, u, :], start=True, stop=True).then_inc(two_filled, 1)
                    wait_reuse(pe, out_ready, n)
                    for u in range(NP):
                        pe.wait_ge(gated, n * NP + u + 1)
                        ins = nc.tensor.matmul(out_ps[:, :], S["H_wo"][:, u, :], two[:, u, :], start=(u == 0), stop=(u == NP - 1))
                    ins.then_inc(out_filled, 1)
                    pe.wait_ge(out_ready, n + 1)
                    wait_reuse(pe, h_done, 2 * n - 1)
                    for g in range(G):
                        ins = nc.tensor.transpose(back_ps[:, g, :], out[:, g * P:(g + 1) * P], ident[:, :])
                    ins.then_inc(back_ready, 1)

                pe.wait_ge(cleared, 1)
                pipeline(pe, [None, front, towers], TILES)


def load_weights(nc, S, A, layers):
    def sb(name, shape, dt=F32):
        S[name] = S["ctx"].enter_context(nc.sbuf_tensor(name, shape, dt))
        return S[name]

    loads, zeroed = [], []

    def load(dst, src):
        loads.append((dst, src))

    if "first" in layers:
        S["h"] = sb("h", [P, B, D])
        load(sb("ident", [P, P])[:, :], A["ident"][:, :])
        load(sb("rev8", [P, NE])[:, :], A["rev8"][:, :])
        sb("neg_half", [P, NE])
    for layer, names in (("L0", ("gate_w", "gate_b")), ("L1", ("Wr", "br"))):
        if layer in layers:
            loads_moe(nc, S, A, sb, load, layer, *names)
    if "A" in layers:
        loads_A(nc, S, A, sb, load, zeroed)
    if "C" in layers:
        loads_C(nc, S, A, sb, load, zeroed)
    if "E" in layers:
        loads_E(nc, S, A, sb, load, zeroed)
    if "F" in layers:
        loads_F(nc, S, A, sb, load, zeroed)
    if "G" in layers:
        loads_G(nc, S, A, sb, load, zeroed)
    if "H" in layers:
        loads_H(nc, S, A, sb, load, zeroed)
    tag = "_".join(layers)
    loaded = S["ctx"].enter_context(nc.semaphore("loaded_" + tag))
    cleared = S["ctx"].enter_context(nc.semaphore("cleared_" + tag))
    with nc.Block() as block:
        @block.vector
        def _(dve):
            for tile in zeroed:
                nc.vector.memset(tile[:], 0.0)
            if "first" in layers:
                nc.vector.memset(S["neg_half"][:], -0.5)
            nc.vector.drain().then_inc(cleared, 1)

        @block.sync
        def _(sp):
            sp.wait_ge(cleared, 1)
            for dst, src in loads:
                sp.dma_start(dst, src).then_inc(loaded, 16)
    return loaded, 16 * len(loads)


def await_loads(nc, started):
    loaded, count = started
    with nc.Block() as block:
        @block.sync
        def _(sp):
            sp.wait_ge(loaded, count)


def build(nc, A, out):
    with ExitStack() as ctx:
        S = {"ctx": ctx}
        first = load_weights(nc, S, A, ["first", "A"])
        early = load_weights(nc, S, A, ["L0", "C", "L1"])
        await_loads(nc, first)
        column_attention(nc, S, A)
        late = load_weights(nc, S, A, ["E", "F", "G", "H"])
        await_loads(nc, early)
        moe_layer(nc, S, "L0m", S["L0_ffn_w1"], S["L0_ffn_w2"], S["L0_ffn_b2"], S["L0_ffn_wr"], False)
        alibi_attention(nc, S, A)
        moe_layer(nc, S, "L1m", S["L1_ffn_w1"], S["L1_ffn_w2"], S["L1_ffn_b2"], S["L1_ffn_wr"], True)
        await_loads(nc, late)
        periodic_attention(nc, S)
        routed_mlp(nc, S)
        mamba(nc, S)
        gated_towers(nc, S)
        stored = ctx.enter_context(nc.semaphore("stored"))
        with nc.Block() as block:
            @block.sync
            def _(sp):
                sp.dma_start(out.rearrange("b t d -> t b d"), S["h"][:]).then_inc(stored, 16)
                sp.wait_ge(stored, 16)


def shape_constants():
    c = {"ident": np.eye(P, dtype=np.float32),
         "rev8": np.tile(np.arange(NE, 0, -1, dtype=np.float32), (P, 1))}
    constants_A(c)
    constants_C(c)
    constants_E(c)
    constants_G(c)
    return c


TURNED = ("L2_attn_Wq", "L2_attn_Wk", "L2_attn_Wv", "L2_ffn_Wi", "L2_ffn_Wr", "L2_ffn_Ws", "L2_ffn_Wo",
          *(f"L3_attn_{c}_{w}" for c in "fb" for w in ("in_w", "conv_w", "xproj_w", "dt_w", "out_w")))
LAST_IN_FRONT = ("L2_ffn_br", "L2_ffn_bs")
PAIRED = tuple("L3_ffn_" + v + k for v in ("b", "g", "be", "m", "v") for k in "12")


def kernel(**inputs):
    import numpy as _np
    import concourse.bacc as _bacc
    from concourse import mybir as _mybir
    from concourse.bass_utils import run_bass_kernel_spmd as _run

    nc = _bacc.Bacc("TRN2", target_bir_lowering=False, num_devices=1)
    arrays, args = {}, {}
    for name, a in list(inputs.items()) + list(shape_constants().items()):
        a = _np.asarray(a)
        if name == "L3_attn_b_in_w":
            a = a[:, ::-1]
        if name == "L3_attn_b_out_w":
            a = a[::-1, :]
        if name in TURNED:
            a = _np.swapaxes(a, -1, -2)
        if name in LAST_IN_FRONT:
            a = _np.moveaxis(a, -1, 0)
        if name in PAIRED:
            a = a.reshape(NE // 2, 2 * D).T
        a = _np.ascontiguousarray(a)
        arrays[f"in_{name}_dram"] = a
        args[name] = nc.dram_tensor(f"in_{name}_dram", a.shape, _mybir.dt.from_np(a.dtype), kind="ExternalInput").ap()
    out = nc.dram_tensor("out_0_dram", (B, T, D), _mybir.dt.from_np(_np.dtype("float32")), kind="ExternalOutput").ap()
    build(nc, args, out)
    r = _run(nc, [arrays], core_ids=[0])
    return r.results[0]["out_0_dram"]
```

```python
from contextlib import ExitStack, contextmanager

import numpy as np
import concourse.bass as bass
from concourse import mybir

ALU = mybir.AluOpType
ACT = mybir.ActivationFunctionType
F32 = mybir.dt.float32
BF16 = mybir.dt.bfloat16
I32 = mybir.dt.int32
U32 = mybir.dt.uint32
X = mybir.AxisListType.X

P = 128
B = 128
T = 128
D = 64
G = 4
COLS = G * P
TILES = B // G
EPS = 1e-5
NE = 8
HID = 128
HD = 256
NH, CH = 8, 32


@contextmanager
def semaphores(nc, prefix):
    taken = []

    def sem(name):
        taken.append(nc.alloc_semaphore(name=f"{prefix}_{name}"))
        return taken[-1]

    yield sem
    nc.clear_and_free_semaphores(taken)
    nc.all_engine_barrier()


class Chain:

    def __init__(self, eng, sem, n, per):
        self.eng, self.sem, self.base, self.per, self.k = eng, sem, n * per, per, 0

    def __call__(self, ins):
        self.k += 1
        ins.then_inc(self.sem, 1)
        self.eng.wait_ge(self.sem, self.base + self.k)

    def end(self):
        assert self.k == self.per, (self.k, self.per)


def wait_reuse(eng, sem, count):
    if isinstance(count, int) and count <= 0:
        return
    eng.wait_ge(sem, count)


def pipeline(eng, stages, tiles):
    lag = len(stages) - 1

    def step(s, parity, full=False):
        for k, stage in enumerate(stages):
            if stage is not None and (full or 0 <= s - k < tiles):
                stage(s - k, (parity - k) % 2)

    first = lag + 2
    if (tiles - first) % 2:
        first += 1
    for s in range(first):
        step(s, s % 2)
    with eng.Fori(first, tiles - 1, 2) as s:
        step(s, first % 2, full=True)
        step(s + 1, (first + 1) % 2, full=True)
    for s in range(tiles, tiles + lag):
        step(s, s % 2)


def in_order(eng, pieces, tiles):
    lag = max(k for k, _ in pieces)

    def step(s, parity, full=False):
        for k, piece in pieces:
            if full or 0 <= s - k < tiles:
                piece(s - k, (parity - k) % 2)

    first = lag + 2
    if (tiles - first) % 2:
        first += 1
    for s in range(first):
        step(s, s % 2)
    with eng.Fori(first, tiles - 1, 2) as s:
        step(s, first % 2, full=True)
        step(s + 1, (first + 1) % 2, full=True)
    for s in range(tiles, tiles + lag):
        step(s, s % 2)


def exists(n):
    return not isinstance(n, int) or 0 <= n < TILES


def sweep(eng, slot, slots):
    def tile(n, p):
        for k in range(slots):
            slot(k, n, p)

    for n in (-1, 0, 1):
        tile(n, n % 2)
    with eng.Fori(2, TILES - 3, 2) as n:
        tile(n, 0)
        tile(n + 1, 1)
    for n in range(TILES - 2, TILES + 1):
        tile(n, n % 2)


def before(g, n, p, back):
    return (g - back, n, p) if g >= back else (g - back + G, n - 1, 1 - p)


def bc(ap, n):
    return ap.unsqueeze(len(ap.shape)).to_broadcast([*ap.shape, n])


def mid(ap, n):
    return ap.unsqueeze(1).to_broadcast([ap.shape[0], n, ap.shape[1]])


def norm_stats(eng, nc, chain, x, xc, sq, total, var):
    chain(nc.vector.tensor_reduce(total, x, X, ALU.add))
    chain(nc.vector.scalar_tensor_tensor(out=xc, in0=bc(total, D), scalar=-1.0 / D, in1=x,
                                         op0=ALU.mult, op1=ALU.add))
    chain(nc.vector.tensor_tensor(sq, xc, xc, ALU.mult))
    chain(nc.vector.tensor_reduce(total, sq, X, ALU.add))
    return nc.vector.tensor_scalar(var, total, 1.0 / D, EPS, ALU.mult, ALU.add)


def constants_A(c):
    pos = np.arange(T, dtype=np.float32)[:, None]
    d = np.arange(D)
    inv = np.power(np.float32(10000.0), -((d - d % 2).astype(np.float32) / np.float32(D))).astype(np.float32)
    angle = (pos * inv).astype(np.float32)
    c["positions"] = np.where(d % 2 == 0, np.sin(angle), np.cos(angle)).astype(np.float32)


def loads_A(nc, S, A, sb, load, zeroed):
    q = "L0_attn_"
    wqk = sb("A_wqk", [D, 2 * HD])
    load(wqk[:, 0:HD], A[q + "Wq"][:, :])
    load(wqk[:, HD:2 * HD], A[q + "Wk"][:, :])
    wvg = sb("A_wvg", [D + 1, 2 * HD])
    zeroed.append(wvg)
    load(wvg[0:D, 0:HD], A[q + "Wv"][:, :])
    load(wvg[0:D, HD:2 * HD], A[q + "Wg"][:, :])
    load(wvg[D:D + 1, HD:2 * HD], A[q + "bg"].rearrange("(a n) -> a n", a=1))
    load(sb("A_wo", [P, 2, D])[:], A[q + "Wo"].rearrange("(u p) d -> p u d", p=P))
    load(sb("A_bo", [P, D])[:, :], A[q + "bo"].rearrange("(a n) -> a n", a=1).to_broadcast([P, D]))
    for v in ("gamma", "beta"):
        two = sb("A_" + v, [2 * D, 1])
        for k in range(2):
            load(two[k * D:(k + 1) * D, :], A[q + v].rearrange("(d a) -> d a", a=1))
    load(sb("A_ids", [P, T], I32)[:, :], A["x"][:, :])


def column_attention(nc, S, A):
    h, ident = S["h"], S["ident"]
    SCALE = 1.0 / float(np.sqrt(CH)) / float(np.sqrt(T))
    with ExitStack() as ctx:
        def sb(name, shape, dt=F32):
            return ctx.enter_context(nc.sbuf_tensor(f"A_{name}", shape, dt))

        sem = ctx.enter_context(semaphores(nc, "A"))

        hs = sb("hs", [P, T, D])
        mnT = sb("mnT", [D, T * B])
        attT = sb("attT", [P, NH, P])

        acc_ctx = ExitStack()
        acc = acc_ctx.enter_context(nc.psum_tensor("A_acc", [P, NH, P], F32))
        column_scores(nc, S, A, hs, mnT, acc)
        column_softmax(nc, S, acc, attT, SCALE)
        acc_ctx.close()
        column_values(nc, S, hs, mnT, attT)
        swap_axes(nc, S, hs)


def column_scores(nc, S, A, hs, mnT, acc):
    ident = S["ident"]
    with ExitStack() as ctx:
        def sb(name, shape, dt=F32):
            return ctx.enter_context(nc.sbuf_tensor(f"As_{name}", shape, dt))

        def ps(name, shape):
            return ctx.enter_context(nc.psum_tensor(f"As_{name}", shape, F32))

        sem = ctx.enter_context(semaphores(nc, "As"))

        xc = sb("xc", [P, G, D])
        sq = sb("sq", [P, G, D])
        total, var, rstd = sb("total", [P, G]), sb("var", [P, G]), sb("rstd", [P, G])
        xn = sb("xn", [P, 2, G, D])
        xT = sb("xT", [D, 2, COLS])
        table = S["h"]
        ids, rows = sb("ids", [P, 2, G], I32), sb("rows", [P, 2, G, D])
        embedded = sb("embedded", [P, G, D])
        gathered, table_in, summed = map(sem, ("gathered", "table_in", "summed"))
        qk = sb("qk", [P, 2, 2 * NH, G, CH])
        qkT = sb("qkT", [P, 2, 2 * NH, P])
        zero = sb("zero", [1, P])
        xT_ps = ps("xT_ps", [P, G // 2, P])
        tok_ps = ps("tok_ps", [P, 2, 2 * HD])
        turn_ps = ps("turn_ps", [P, 2, 4, P])
        stats_chain, var_ready, rstd_ready, xn_ready = sem("stats_chain"), sem("var_ready"), sem("rstd_ready"), sem("xn_ready")
        xT_ps_ready, xT_ready, kept = sem("xT_ps_ready"), sem("xT_ready"), sem("kept")
        tok_ps_ready, tok_a, tok_d = sem("tok_ps_ready"), sem("tok_a"), sem("tok_d")
        turn_ready, turned_a, turned_d = sem("turn_ready"), sem("turned_a"), sem("turned_d")
        scored, consts_set = sem("scored"), sem("consts_set")

        with nc.Block() as block:
            @block.sync
            def _(sp):
                sp.dma_start(table[:].rearrange("p t d -> p (t d)"),
                             A["positions"].rearrange("t d -> (t d)").rearrange("(a n) -> a n", a=1).to_broadcast([P, T * D])).then_inc(table_in, 16)
                sp.wait_ge(table_in, 16)

            @block.vector
            def _(dve):
                nc.vector.memset(zero[:, :], 0.0).then_inc(consts_set, 1)
                dve.wait_ge(table_in, 16)

                def embed(n, p):
                    dve.wait_ge(gathered, (n + 1) * G * 16)
                    here = table[:, bass.ds(n * G, G), :]
                    nc.vector.tensor_tensor(hs[:, bass.ds(n * G, G), :], rows[:, p, :, :], here, ALU.add)
                    nc.vector.tensor_tensor(embedded[:, :, :], rows[:, p, :, :], here, ALU.add).then_inc(summed, 1)
                    dve.wait_ge(summed, n + 1)

                def stats(m, n, p):
                    chain = Chain(dve, stats_chain, n * 2 + m, 4)
                    x = embedded[:, :, :] if m == 0 else xn[:, p, :, :]
                    norm_stats(dve, nc, chain, x, xc[:, :, :], sq[:, :, :], total[:, :], var[:, :]).then_inc(var_ready, 1)
                    chain.end()

                def scaled(m, n, p):
                    dve.wait_ge(rstd_ready, n * 2 + m + 1)
                    if m == 0:
                        wait_reuse(dve, xT_ps_ready, n - 1)
                    nc.vector.tensor_tensor(xn[:, p, :, :], xc[:, :, :], bc(rstd[:, :], D), ALU.mult).then_inc(xn_ready, 1)
                    dve.wait_ge(xn_ready, n * 2 + m + 1)

                def between(n, p):
                    scaled(0, n, p)
                    stats(1, n, p)

                def tokens(u):
                    def piece(n, p):
                        dve.wait_ge(tok_ps_ready, n * G + 2 * u + 2)
                        if u == 0:
                            wait_reuse(dve, turn_ready, (n - 1) * 4)
                        nc.vector.tensor_copy(qk[:, p, :, 2 * u + 1, :], tok_ps[:, 1, :].rearrange("p (h c) -> p h c", c=CH)).then_inc(tok_d, 1)
                    return piece

                def turned(u):
                    def piece(n, p):
                        dve.wait_ge(turn_ready, n * 4 + 2 * u + 2)
                        if u == 0:
                            wait_reuse(dve, scored, n - 1)
                        nc.vector.tensor_copy(qkT[:, p, 4 * (2 * u + 1):4 * (2 * u + 2), :], turn_ps[:, 1, :, :]).then_inc(turned_d, 1)
                    return piece

                in_order(dve, [(1, embed), (1, lambda n, p: stats(0, n, p)), (3, turned(0)), (2, tokens(0)), (1, between), (3, turned(1)),
                               (2, tokens(1)), (1, lambda n, p: scaled(1, n, p))], TILES)

            @block.gpsimd
            def _(pool):
                def power(m):
                    def piece(n, p):
                        pool.wait_ge(var_ready, n * 2 + m + 1)
                        nc.gpsimd.tensor_tensor(rstd[:, :], var[:, :], S["neg_half"][:, 0:G], ALU.pow).then_inc(rstd_ready, 1)
                    return piece

                def keep(n, p):
                    pool.wait_ge(xT_ready, n + 1)
                    nc.gpsimd.tensor_copy(mnT[:, bass.ds(n * COLS, COLS)], xT[:, p, :]).then_inc(kept, 1)

                def gather(n, p):
                    wait_reuse(pool, summed, n)
                    nc.gpsimd.tensor_copy(ids[:, p, :], S["A_ids"][:, bass.ds(n * G, G)])
                    nc.gpsimd.drain()
                    for g in range(G):
                        nc.gpsimd.indirect_dma_start(
                            out=rows[:, p, g, :], out_offset=None, in_=A["L0_tok_W"][:, :],
                            in_offset=bass.IndirectOffsetOnAxis(ap=ids[:, p, g:g + 1].bitcast(U32), axis=0),
                        ).then_inc(gathered, 16)

                in_order(pool, [(1, power(0)), (0, gather), (2, keep), (1, power(1))], TILES)

            @block.scalar
            def _(act):
                def normed(n, p):
                    act.wait_ge(xT_ps_ready, n + 1)
                    wait_reuse(act, kept, n - 1)
                    wait_reuse(act, tok_ps_ready, (n - 1) * G)
                    for q in range(2):
                        dst = xT[:, p, :].rearrange("d (g q t) -> d g q t", g=G // 2, q=2)[:, :, q, :]
                        ins = nc.scalar.activation(dst, xT_ps[q * D:(q + 1) * D, :, :], ACT.Identity,
                                                   bias=S["A_beta"][q * D:(q + 1) * D, :], scale=S["A_gamma"][q * D:(q + 1) * D, :])
                    ins.then_inc(xT_ready, 1)

                def tokens(u):
                    def piece(n, p):
                        act.wait_ge(tok_ps_ready, n * G + 2 * u + 1)
                        if u == 0:
                            wait_reuse(act, turn_ready, (n - 1) * 4)
                        nc.scalar.copy(qk[:, p, :, 2 * u, :], tok_ps[:, 0, :].rearrange("p (h c) -> p h c", c=CH)).then_inc(tok_a, 1)
                    return piece

                def turned(u):
                    def piece(n, p):
                        act.wait_ge(turn_ready, n * 4 + 2 * u + 1)
                        if u == 0:
                            wait_reuse(act, scored, n - 1)
                        nc.scalar.copy(qkT[:, p, 8 * u:8 * u + 4, :], turn_ps[:, 0, :, :]).then_inc(turned_a, 1)
                    return piece

                in_order(act, [(2, normed), (3, turned(0)), (2, tokens(0)), (3, turned(1)), (2, tokens(1))], TILES)

            @block.tensor
            def _(pe):
                pe.wait_ge(consts_set, 1)
                for u in range(2):
                    nc.tensor.matmul(acc[:, 4 * u:4 * u + 4, :], zero[:, :],
                                     zero[:, :].unsqueeze(1).to_broadcast([1, 4, P]), start=True, stop=True)

                def turn_x(n, p):
                    pe.wait_ge(xn_ready, (n + 1) * 2)
                    wait_reuse(pe, xT_ready, n)
                    for q in range(G // 2):
                        ins = nc.tensor.transpose(xT_ps[:, q, :], xn[:, p, 2 * q:2 * q + 2, :].rearrange("p g d -> p (g d)"), ident[:, :])
                    ins.then_inc(xT_ps_ready, 1)

                def tokens(u):
                    def piece(n, p):
                        pe.wait_ge(xT_ready, n + 1)
                        for g in (2 * u, 2 * u + 1):
                            wait_reuse(pe, (tok_a, tok_d)[g % 2], n * 2 + u)
                            nc.tensor.matmul(tok_ps[:, g % 2, :], xT[:, p, g * P:(g + 1) * P], S["A_wqk"][:, :],
                                             start=True, stop=True).then_inc(tok_ps_ready, 1)
                    return piece

                def turns(half):
                    def piece(n, p):
                        pe.wait_ge(tok_a, (n + 1) * 2)
                        pe.wait_ge(tok_d, (n + 1) * 2)
                        for u in (2 * half, 2 * half + 1):
                            wait_reuse(pe, (turned_a, turned_d)[u % 2], n * 2 + half)
                            for k in range(4):
                                head, which = 2 * u + k // 2, k % 2
                                ins = nc.tensor.transpose(turn_ps[:, u % 2, k, :],
                                                          qk[:, p, NH * which + head, :, :].rearrange("p g c -> p (g c)"), ident[:, :])
                            ins.then_inc(turn_ready, 1)
                    return piece

                def scores(n, p):
                    pe.wait_ge(turned_a, (n + 1) * 2)
                    pe.wait_ge(turned_d, (n + 1) * 2)
                    for head in range(NH):
                        ins = nc.tensor.matmul(acc[:, head, :], qkT[:, p, 2 * head, :], qkT[:, p, 2 * head + 1, :],
                                               start=False, stop=True, skip_group_check=True)
                    ins.then_inc(scored, 1)

                in_order(pe, [(2, turn_x), (3, turns(0)), (2, tokens(0)), (3, turns(1)), (2, tokens(1)), (3, scores)], TILES)


def column_softmax(nc, S, acc, attT, scale):
    ident = S["ident"]
    with ExitStack() as ctx:
        top = ctx.enter_context(nc.sbuf_tensor("Am_top", [P, NH], F32))
        total = ctx.enter_context(nc.sbuf_tensor("Am_total", [P, NH], F32))
        att = ctx.enter_context(nc.sbuf_tensor("Am_att", [P, NH, P], F32))
        att_ps = ctx.enter_context(nc.psum_tensor("Am_ps", [P, NH, P], F32))
        sem = ctx.enter_context(semaphores(nc, "Am"))
        chain_sem, shifted, exps, normed, flipped = map(sem, ("chain", "shifted", "exps", "normed", "flipped"))
        with nc.Block() as block:
            @block.vector
            def _(dve):
                chain = Chain(dve, chain_sem, 0, 3)
                chain(nc.vector.tensor_reduce(top[:, :], acc[:, :, :], X, ALU.max))
                nc.vector.tensor_tensor(att[:, :, :], acc[:, :, :], bc(top[:, :], P), ALU.subtract).then_inc(shifted, 1)
                dve.wait_ge(exps, 1)
                chain(nc.vector.tensor_reduce(total[:, :], att[:, :, :], X, ALU.add))
                chain(nc.vector.reciprocal(total[:, :], total[:, :]))
                chain.end()
                nc.vector.tensor_tensor(att[:, :, :], att[:, :, :], bc(total[:, :], P), ALU.mult).then_inc(normed, 1)
                dve.wait_ge(flipped, 1)
                nc.vector.tensor_copy(attT[:, :, :], att_ps[:, :, :])

            @block.scalar
            def _(act):
                act.wait_ge(shifted, 1)
                nc.scalar.activation(att[:, :, :], att[:, :, :], ACT.Exp, scale=scale).then_inc(exps, 1)

            @block.tensor
            def _(pe):
                pe.wait_ge(normed, 1)
                for head in range(NH):
                    ins = nc.tensor.transpose(att_ps[:, head, :], att[:, head, :], ident[:, :])
                ins.then_inc(flipped, 1)


def column_values(nc, S, hs, mnT, attT):
    ident = S["ident"]
    with ExitStack() as ctx:
        def sb(name, shape, dt=F32):
            return ctx.enter_context(nc.sbuf_tensor(f"Av_{name}", shape, dt))

        def ps(name, shape):
            return ctx.enter_context(nc.psum_tensor(f"Av_{name}", shape, F32))

        sem = ctx.enter_context(semaphores(nc, "Av"))

        xs = sb("xs", [D + 1, 2, COLS])
        v = sb("v", [P, 2, G, HD])
        gate = sb("gate", [P, 2, G, HD])
        og = sb("og", [P, 2, G, HD])
        ogT = sb("ogT", [P, 2, 2, COLS])
        vg_ps = ps("vg_ps", [P, 2, 2 * HD])
        o_ps = ps("o_ps", [P, NH, G, CH])
        turn_ps = ps("turn_ps", [P, 2, COLS])
        y_ps = ps("y_ps", [P, G, D])
        fetched, vg_ready, v_ready, g_ready = sem("fetched"), sem("vg_ready"), sem("v_ready"), sem("g_ready")
        o_ready, og_ready, turn_ready, turned_a, turned_d = sem("o_ready"), sem("og_ready"), sem("turn_ready"), sem("turned_a"), sem("turned_d")
        y_ready, y_used, consts_set, chain_sem = sem("y_ready"), sem("y_used"), sem("consts_set"), sem("chain")

        with nc.Block() as block:
            @block.vector
            def _(dve):
                nc.vector.memset(xs[D:D + 1, :, :], 1.0).then_inc(consts_set, 1)

                def values(n, p, positions):
                    for g in positions:
                        dve.wait_ge(vg_ready, n * G + g + 1)
                        dve.wait_ge(g_ready, n * G + g + 1)
                        if g == 0:
                            wait_reuse(dve, o_ready, n - 1)
                        nc.vector.tensor_copy(v[:, p, g, :], vg_ps[:, g % 2, 0:HD]).then_inc(v_ready, 1)

                def gated(n, p):
                    dve.wait_ge(o_ready, n + 1)
                    wait_reuse(dve, turn_ready, n - 1)
                    for u in range(2):
                        half = slice(u * HD // 2, (u + 1) * HD // 2)
                        ins = nc.vector.tensor_tensor(og[:, p, :, half].rearrange("p g (h c) -> p g h c", c=CH),
                                                      o_ps[:, 4 * u:4 * u + 4, :, :].rearrange("p h g c -> p g h c"),
                                                      gate[:, p, :, half].rearrange("p g (h c) -> p g h c", c=CH), ALU.mult)
                    ins.then_inc(og_ready, 1)

                def turned(n, p):
                    dve.wait_ge(turn_ready, n + 1)
                    wait_reuse(dve, y_ready, n - 1)
                    nc.vector.tensor_copy(ogT[:, p, 1, :], turn_ps[:, 1, :]).then_inc(turned_d, 1)

                def output(n, p):
                    chain = Chain(dve, chain_sem, n, 1)
                    dve.wait_ge(y_ready, n + 1)
                    hn = hs[:, bass.ds(n * G, G), :]
                    nc.vector.tensor_tensor(hn, hn, y_ps[:, :, :], ALU.add).then_inc(y_used, 1)
                    dve.wait_ge(y_used, n + 1)
                    chain(nc.vector.tensor_tensor(hn, hn, mid(S["A_bo"][:, :], G), ALU.add))
                    chain.end()

                in_order(dve, [(1, lambda n, p: values(n, p, (0, 1))), (2, turned), (1, lambda n, p: values(n, p, (2, 3))),
                               (2, output), (1, gated)], TILES)

            @block.gpsimd
            def _(pool):
                pool.wait_ge(consts_set, 1)

                def fetch(n, p):
                    wait_reuse(pool, vg_ready, (n - 1) * G)
                    nc.gpsimd.tensor_copy(xs[0:D, p, :], mnT[:, bass.ds(n * COLS, COLS)]).then_inc(fetched, 1)

                in_order(pool, [(0, fetch)], TILES)

            @block.scalar
            def _(act):
                def gates(n, p, positions):
                    for g in positions:
                        act.wait_ge(vg_ready, n * G + g + 1)
                        if g == 0:
                            wait_reuse(act, og_ready, n - 1)
                        nc.scalar.activation(gate[:, p, g, :], vg_ps[:, g % 2, HD:2 * HD], ACT.Sigmoid).then_inc(g_ready, 1)

                def turn(n, p):
                    act.wait_ge(turn_ready, n + 1)
                    wait_reuse(act, y_ready, n - 1)
                    nc.scalar.copy(ogT[:, p, 0, :], turn_ps[:, 0, :]).then_inc(turned_a, 1)

                in_order(act, [(1, lambda n, p: gates(n, p, (0, 1))), (2, turn), (1, lambda n, p: gates(n, p, (2, 3)))], TILES)

            @block.tensor
            def _(pe):
                def project(n, p, positions):
                    pe.wait_ge(fetched, n + 1)
                    for g in positions:
                        wait_reuse(pe, v_ready, n * G + g - 1)
                        nc.tensor.matmul(vg_ps[:, g % 2, :], xs[:, p, g * P:(g + 1) * P], S["A_wvg"][:, :],
                                         start=True, stop=True).then_inc(vg_ready, 1)

                def attend(n, p):
                    pe.wait_ge(v_ready, (n + 1) * G)
                    wait_reuse(pe, og_ready, n)
                    for head in range(NH):
                        ins = nc.tensor.matmul(o_ps[:, head, :, :], attT[:, head, :], v[:, p, :, CH * head:CH * (head + 1)],
                                               start=True, stop=True)
                    ins.then_inc(o_ready, 1)

                def turn(n, p):
                    pe.wait_ge(og_ready, n + 1)
                    wait_reuse(pe, turned_a, n)
                    wait_reuse(pe, turned_d, n)
                    for u in range(2):
                        for g in range(G):
                            ins = nc.tensor.transpose(turn_ps[:, u, g * P:(g + 1) * P], og[:, p, g, u * P:(u + 1) * P], ident[:, :])
                    ins.then_inc(turn_ready, 1)

                def output(n, p):
                    pe.wait_ge(turned_a, n + 1)
                    pe.wait_ge(turned_d, n + 1)
                    wait_reuse(pe, y_used, n)
                    for g in range(G):
                        for u in range(2):
                            ins = nc.tensor.matmul(y_ps[:, g, :], ogT[:, p, u, g * P:(g + 1) * P], S["A_wo"][:, u, :],
                                                   start=(u == 0), stop=(u == 1))
                    ins.then_inc(y_ready, 1)

                in_order(pe, [(1, lambda n, p: project(n, p, (0, 1))), (2, turn), (1, lambda n, p: project(n, p, (2, 3))),
                              (2, output), (1, attend)], TILES)


def swap_axes(nc, S, hs):
    h, ident = S["h"], S["ident"]
    with ExitStack() as ctx:
        turn_ps = ctx.enter_context(nc.psum_tensor("Ax_ps", [P, 4, 4, P], F32))
        turned, copied_a, copied_d = map(ctx.enter_context(semaphores(nc, "Ax")), ("turned", "copied_a", "copied_d"))
        with nc.Block() as block:
            @block.tensor
            def _(pe):
                for q in range(D // 4):
                    if q >= 4:
                        pe.wait_ge((copied_a, copied_d)[q % 2], q // 2 - 1)
                    for k in range(4):
                        ins = nc.tensor.transpose(turn_ps[:, q % 4, k, :], hs[:, :, 4 * q + k], ident[:, :])
                    ins.then_inc(turned, 1)

            def copy_out(eng, copy, first, done):
                for q in range(first, D // 4, 2):
                    eng.wait_ge(turned, q + 1)
                    copy(h[:, :, 4 * q:4 * q + 4], turn_ps[:, q % 4, :, :].rearrange("p k s -> p s k")).then_inc(done, 1)

            @block.scalar
            def _(act):
                copy_out(act, nc.scalar.copy, 0, copied_a)

            @block.vector
            def _(dve):
                copy_out(dve, nc.vector.tensor_copy, 1, copied_d)


def loads_moe(nc, S, A, sb, load, zeroed, layer, wr_name, br_name):
    q = f"{layer}_ffn_"
    w1 = sb(q + "w1", [D + 1, NE, HID])
    load(w1[0:D], A[q + "W1"].rearrange("e d f -> d e f"))
    load(w1[D:D + 1], A[q + "b1"].rearrange("(a e) f -> a e f", a=1))
    w2 = sb(q + "w2", [HID, NE, D])
    load(w2[:], A[q + "W2"].rearrange("e f d -> f e d"))
    wr = sb(q + "wr", [D + 1, NE])
    load(wr[0:D], A[q + wr_name][:, :])
    load(wr[D:D + 1], A[q + br_name].rearrange("(a e) -> a e", a=1))
    b2 = sb(q + "b2", [32, D])
    zeroed.append(b2)
    for k in range(3):
        load(b2[k * NE:(k + 1) * NE, :], A[q + "b2"][:, :])
    if layer == "L1":
        for v in ("gamma", "beta"):
            two = sb("L1m_" + v, [2 * D, 1])
            for k in range(2):
                load(two[k * D:(k + 1) * D, :], A[q + v].rearrange("(d a) -> d a", a=1))


def moe_layer(nc, S, pre, w1, w2, b2, wr, affine):
    h, ident, half = S["h"], S["ident"], S["neg_half"]
    with ExitStack() as ctx:
        def sb(name, shape, dt=F32):
            return ctx.enter_context(nc.sbuf_tensor(f"{pre}_{name}", shape, dt))

        def ps(name, shape):
            return ctx.enter_context(nc.psum_tensor(f"{pre}_{name}", shape, F32))

        sem = ctx.enter_context(semaphores(nc, pre))

        xc = sb("xc", [P, G, D])
        sq = sb("sq", [P, G, D])
        total = sb("total", [P, G])
        var = sb("var", [P, G])
        rstd = sb("rstd", [P, G])
        xn = sb("xn", [P, 2, G, D])
        xT = sb("xT", [D + 1, 2, COLS])
        rw = sb("rw", [P, 8, G, NE])
        small = sb("small", [P, 6, G])
        ex_in = sb("ex_in", [P, G, NE])
        ex = sb("ex", [P, G, NE])
        ebase = sb("ebase", [P, G, NE])
        cw = sb("cw", [P, 2, G, NE])
        hid = sb("hid", [P, 4, COLS])
        cw_rest = sb("cw_rest", [P, G, NE])
        cw_parts = sb("cw_parts", [P, 2, G, 32], BF16)
        cwT = sb("cwT", [32, 2, COLS], BF16)
        yT = sb("yT", [P, COLS])
        b2_parts = sb("b2_parts", [32, 3, D], BF16)
        b2_rest = sb("b2_rest", [32, D])
        ident16 = sb("ident16", [P, P], BF16)
        expert_rows = sb("expert_rows", [32, NE, P], BF16)

        xT_ps = ps("xT_ps", [P, G // 2, P])
        logits_ps = xT_ps[:, 0, 0:G * NE].rearrange("p (g e) -> p g e", g=G)
        cwT_ps = ctx.enter_context(nc.psum_tensor(f"{pre}_cwT_ps", [32, COLS], BF16))
        hid_ps, cw_ps = ps("hid_ps", [P, 2, COLS]), ps("cw_ps", [P, 2, COLS])
        yT_ps, back_ps = ps("yT_ps", [D, COLS]), ps("back_ps", [P, G, P])

        stats_chain, route_chain, cw_chain, split_chain = map(sem, ("stats_chain", "route_chain", "cw_chain", "split_chain"))
        parts_ready, cwT_ps_ready, cwT_ready, cw_ps_ready = map(sem, ("parts_ready", "cwT_ps_ready", "cwT_ready", "cw_ps_ready"))
        gated, yT_copied, back_ready, h_done = map(sem, ("gated", "yT_copied", "back_ready", "h_done"))
        var_ready, rstd_ready, xn_ready = sem("var_ready"), sem("rstd_ready"), sem("xn_ready")
        xT_ps_ready, xT_ready = sem("xT_ps_ready"), sem("xT_ready")
        logits_ready, ex_in_ready, ex_ready, cw_ready = sem("logits_ready"), sem("ex_in_ready"), sem("ex_ready"), sem("cw_ready")
        hid_ps_ready, hid_ready, down_done = sem("hid_ps_ready"), sem("hid_ready"), sem("down_done")
        consts_set = sem("consts_set")
        norms = 2 if affine else 1

        with nc.Block() as block:
            @block.vector
            def _(dve):
                nc.vector.memset(xT[D:D + 1, :, :], 1.0)
                nc.vector.memset(ebase[:, :, :], float(np.e))
                nc.vector.memset(yT[:, :], 0.0)
                nc.vector.memset(cw_parts[:, :, :, :], 0.0)
                nc.vector.tensor_copy(ident16[:, :], ident[:, :])
                nc.vector.tensor_copy(expert_rows[:, :, :], bc(S["part_experts"][:, :], P))
                chain = Chain(dve, split_chain, 0, 4)
                rest = b2[:, :]
                for k in range(3):
                    ins = nc.vector.tensor_copy(b2_parts[:, k, :], rest)
                    if k < 2:
                        chain(ins)
                        chain(nc.vector.tensor_tensor(b2_rest[:, :], rest, b2_parts[:, k, :], ALU.subtract))
                        rest = b2_rest[:, :]
                chain.end()
                nc.vector.memset(xT[D:D + 1, :, :], 1.0).then_inc(consts_set, 1)
                dve.wait_ge(consts_set, 1)

                def stats(m, n, p):
                    chain = Chain(dve, stats_chain, n * norms + m, 4)
                    x = h[:, bass.ds(n * G, G), :] if m == 0 else xn[:, p, :, :]
                    norm_stats(dve, nc, chain, x, xc[:, :, :], sq[:, :, :], total[:, :], var[:, :]).then_inc(var_ready, 1)
                    chain.end()

                def scaled(m, n, p):
                    dve.wait_ge(rstd_ready, n * norms + m + 1)
                    if m == 0:
                        wait_reuse(dve, xT_ps_ready, n - 1)
                    nc.vector.tensor_tensor(xn[:, p, :, :], xc[:, :, :], bc(rstd[:, :], D),
                                            ALU.mult).then_inc(xn_ready, 1)
                    dve.wait_ge(xn_ready, n * norms + m + 1)

                def best(chain, score, slot, k):
                    chain(nc.vector.tensor_reduce(small[:, k, :], score, X, ALU.max))
                    chain(nc.vector.tensor_tensor(rw[:, slot, :, :], score, bc(small[:, k, :], NE), ALU.is_equal))
                    chain(nc.vector.tensor_tensor(rw[:, slot, :, :], rw[:, slot, :, :], mid(S["rev8"][:, :], G), ALU.mult))
                    chain(nc.vector.tensor_reduce(small[:, k + 1, :], rw[:, slot, :, :], X, ALU.max))
                    chain(nc.vector.tensor_tensor(rw[:, slot, :, :], rw[:, slot, :, :], bc(small[:, k + 1, :], NE), ALU.is_equal))

                def route(part, n, p):
                    chain = Chain(dve, route_chain, n, 17)
                    if part == 0:
                        dve.wait_ge(logits_ready, n + 1)
                        chain(nc.vector.tensor_copy(rw[:, 0, :, :], logits_ps))
                        chain(nc.vector.tensor_reduce(small[:, 0, :], rw[:, 0, :, :], X, ALU.max))
                        wait_reuse(dve, ex_ready, n)
                        nc.vector.tensor_tensor(ex_in[:, :, :], rw[:, 0, :, :], bc(small[:, 0, :], NE),
                                                ALU.subtract).then_inc(ex_in_ready, 1)
                    if part == 1:
                        chain.k = 2
                        if not affine:
                            dve.wait_ge(ex_ready, n + 1)
                            chain(nc.vector.tensor_reduce(small[:, 1, :], ex[:, :, :], X, ALU.add))
                            chain(nc.vector.reciprocal(small[:, 1, :], small[:, 1, :]))
                            chain(nc.vector.tensor_tensor(rw[:, 0, :, :], ex[:, :, :], bc(small[:, 1, :], NE), ALU.mult))
                        best(chain, rw[:, 0, :, :], 1, 2)
                    if part == 2:
                        chain.k = 7 if affine else 10
                        chain(nc.vector.scalar_tensor_tensor(out=rw[:, 2, :, :], in0=rw[:, 1, :, :], scalar=-1e30,
                                                             in1=rw[:, 0, :, :], op0=ALU.mult, op1=ALU.add))
                        best(chain, rw[:, 2, :, :], 3, 4)
                    if part == 3:
                        chain.k = 13 if affine else 16
                        chain(nc.vector.tensor_tensor(rw[:, 4, :, :], rw[:, 1, :, :], rw[:, 3, :, :], ALU.add))
                        if affine:
                            dve.wait_ge(ex_ready, n + 1)
                            chain(nc.vector.tensor_tensor(rw[:, 5, :, :], ex[:, :, :], rw[:, 4, :, :], ALU.mult))
                            chain(nc.vector.tensor_reduce(small[:, 1, :], rw[:, 5, :, :], X, ALU.add))
                            chain(nc.vector.reciprocal(small[:, 1, :], small[:, 1, :]))
                            nc.vector.tensor_tensor(cw[:, p, :, :], rw[:, 5, :, :], bc(small[:, 1, :], NE), ALU.mult).then_inc(cw_ready, 1)
                        else:
                            nc.vector.tensor_tensor(cw[:, p, :, :], rw[:, 0, :, :], rw[:, 4, :, :], ALU.mult).then_inc(cw_ready, 1)
                        chain.end()
                    if part == 4:
                        dve.wait_ge(cw_ready, n + 1)
                        wait_reuse(dve, cwT_ps_ready, n - 1)
                        chain = Chain(dve, cw_chain, n, 4)
                        rest = cw[:, p, :, :]
                        for k in range(3):
                            ins = nc.vector.tensor_copy(cw_parts[:, p, :, k * NE:(k + 1) * NE], rest)
                            if k < 2:
                                chain(ins)
                                chain(nc.vector.tensor_tensor(cw_rest[:, :, :], rest, cw_parts[:, p, :, k * NE:(k + 1) * NE], ALU.subtract))
                                rest = cw_rest[:, :, :]
                        ins.then_inc(parts_ready, 1)
                        chain.end()

                def gate(e, n):
                    m = n * NE + e
                    dve.wait_ge(hid_ready, m + 1)
                    dve.wait_ge(cw_ps_ready, m + 1)
                    nc.vector.tensor_tensor(hid[:, e % 4, :], hid[:, e % 4, :], cw_ps[:, e % 2, :], ALU.mult).then_inc(gated, 1)

                def slot(e, n, p):
                    if e == 0 and isinstance(n, int) and n == -1:
                        for m in range(norms):
                            stats(m, 0, 0)
                            scaled(m, 0, 0)
                    if exists(n):
                        gate(e, n)
                    if exists(n + 2):
                        if e == 0:
                            stats(0, n + 2, p)
                        if e == 1:
                            scaled(0, n + 2, p)
                            if affine:
                                stats(1, n + 2, p)
                        if e == 3 and affine:
                            scaled(1, n + 2, p)
                    if e == 7 and exists(n - 1):
                        dve.wait_ge(back_ready, n)
                        hn = h[:, bass.ds((n - 1) * G, G), :]
                        nc.vector.tensor_tensor(hn, hn, back_ps[:, :, 0:D], ALU.add).then_inc(h_done, 1)
                    parts = {2: (0,), 3: (1,), 4: (2,), 5: (3,), 6: (4,)} if affine else {2: (0,), 3: (1,), 4: (2,), 5: (3,), 6: (4,)}
                    if exists(n + 1):
                        for part in parts.get(e, ()):
                            route(part, n + 1, 1 - p)

                sweep(dve, slot, NE)

            @block.gpsimd
            def _(pool):
                pool.wait_ge(consts_set, 1)

                def power(n, m):
                    pool.wait_ge(var_ready, n * norms + m + 1)
                    nc.gpsimd.tensor_tensor(rstd[:, :], var[:, :], half[:, 0:G], ALU.pow).then_inc(rstd_ready, 1)

                def slot(_, n, p):
                    if isinstance(n, int) and n == -1:
                        for m in range(norms):
                            power(0, m)
                    if exists(n + 2):
                        for m in range(norms):
                            power(n + 2, m)
                    if affine and exists(n + 1):
                        pool.wait_ge(ex_in_ready, n + 2)
                        nc.gpsimd.tensor_tensor(ex[:, :, :], ebase[:, :, :], ex_in[:, :, :], ALU.pow).then_inc(ex_ready, 1)

                sweep(pool, slot, 1)

            @block.scalar
            def _(act):
                act.wait_ge(consts_set, 1)

                def turn(n, p):
                    act.wait_ge(xT_ps_ready, n + 1)
                    wait_reuse(act, hid_ps_ready, (n - 1) * NE)
                    for q in range(2):
                        src = xT_ps[q * D:(q + 1) * D, :, :]
                        dst = xT[0:D, p, :].rearrange("d (g q t) -> d g q t", g=G // 2, q=2)[:, :, q, :]
                        if affine:
                            ins = nc.scalar.activation(dst, src, ACT.Identity, bias=S[pre + "_beta"][q * D:(q + 1) * D, :],
                                                       scale=S[pre + "_gamma"][q * D:(q + 1) * D, :])
                        else:
                            ins = nc.scalar.copy(dst, src)
                    ins.then_inc(xT_ready, 1)

                def slot(e, n, p):
                    if e == 0 and exists(n):
                        act.wait_ge(cwT_ps_ready, n + 1)
                        wait_reuse(act, cw_ps_ready, (n - 1) * NE)
                        nc.scalar.copy(cwT[:, p, :], cwT_ps[:, :]).then_inc(cwT_ready, 1)
                    if e == 2 and exists(n - 1):
                        act.wait_ge(down_done, n * NE)
                        wait_reuse(act, back_ready, n - 1)
                        nc.scalar.copy(yT[0:D, :], yT_ps[:, :]).then_inc(yT_copied, 1)
                    if exists(n):
                        m = n * NE + e
                        act.wait_ge(hid_ps_ready, m + 1)
                        wait_reuse(act, down_done, m - 3)
                        nc.scalar.activation(hid[:, e % 4, :], hid_ps[:, e % 2, :], ACT.Gelu).then_inc(hid_ready, 1)
                    if e == 0 and exists(n + 1):
                        turn(n + 1, 1 - p)
                    if e == 2 and not affine and exists(n + 1):
                        act.wait_ge(ex_in_ready, n + 2)
                        nc.scalar.activation(ex[:, :, :], ex_in[:, :, :], ACT.Exp).then_inc(ex_ready, 1)

                sweep(act, slot, NE)

            @block.tensor
            def _(pe):
                pe.wait_ge(consts_set, 1)

                def turn(n, p):
                    pe.wait_ge(xn_ready, (n + 1) * norms)
                    wait_reuse(pe, xT_ready, n)
                    wait_reuse(pe, ex_in_ready, n)
                    for q in range(G // 2):
                        ins = nc.tensor.transpose(xT_ps[:, q, :], xn[:, p, 2 * q:2 * q + 2, :].rearrange("p g d -> p (g d)"), ident[:, :])
                    ins.then_inc(xT_ps_ready, 1)

                def logits(n, p):
                    pe.wait_ge(xT_ready, n + 1)
                    for g in range(G):
                        ins = nc.tensor.matmul(logits_ps[:, g, :], xT[:, p, g * P:(g + 1) * P], wr[:, :], start=True, stop=True)
                    ins.then_inc(logits_ready, 1)

                def up(e, n, p):
                    m = n * NE + e
                    if e == 0:
                        pe.wait_ge(xT_ready, n + 1)
                    wait_reuse(pe, hid_ready, m - 1)
                    nc.tensor.matmul(hid_ps[:, e % 2, :], w1[:, e, :], xT[:, p, :], start=True, stop=True).then_inc(hid_ps_ready, 1)

                def down(e, n, p):
                    pe.wait_ge(gated, n * NE + e + 1)
                    if e == 0:
                        wait_reuse(pe, yT_copied, n)
                        for k in range(3):
                            nc.tensor.matmul(yT_ps[:, :], b2_parts[:, k, :], cwT[:, p, :], start=(k == 0), stop=False)
                    nc.tensor.matmul(yT_ps[:, :], w2[:, e, :], hid[:, e % 4, :], start=False, stop=(e == NE - 1)).then_inc(down_done, 1)

                def widen(e, n, p):
                    if e == 0:
                        pe.wait_ge(cwT_ready, n + 1)
                    wait_reuse(pe, gated, n * NE + e - 1)
                    nc.tensor.matmul(cw_ps[:, e % 2, :], expert_rows[:, e, :], cwT[:, p, :], start=True, stop=True).then_inc(cw_ps_ready, 1)

                def slot(e, n, p):
                    if exists(n):
                        up(e, n, p)
                        widen(e, n, p)
                    if e == 0 and exists(n + 1):
                        turn(n + 1, 1 - p)
                    b, tile, parity = (e - 2, n, p) if e >= 2 else (e - 2 + NE, n - 1, 1 - p)
                    if exists(tile):
                        down(b, tile, parity)
                    if e == 1 and exists(n + 1):
                        logits(n + 1, 1 - p)
                    if e == 3 and exists(n - 1):
                        pe.wait_ge(yT_copied, n)
                        wait_reuse(pe, h_done, n - 1)
                        for g in range(G):
                            ins = nc.tensor.transpose(back_ps[:, g, :], yT[:, g * P:(g + 1) * P], ident[:, :])
                        ins.then_inc(back_ready, 1)
                    if e == NE - 1 and exists(n + 1):
                        pe.wait_ge(parts_ready, n + 2)
                        wait_reuse(pe, cwT_ready, n + 1)
                        for g in range(G):
                            ins = nc.tensor.transpose(cwT_ps[:, g * P:(g + 1) * P], cw_parts[:, 1 - p, g, :], ident16[:, :])
                        ins.then_inc(cwT_ps_ready, 1)

                sweep(pe, slot, NE)


def constants_C(c):
    slopes = 2.0 ** -np.arange(1, NH + 1)
    rel = np.arange(T)[None, :] - np.arange(T)[:, None]
    bias = slopes[None, :, None] * rel[:, None, :]
    c["alibi"] = np.where(rel[:, None, :] <= 0, bias, -1e30).astype(np.float32).reshape(T, NH * T)


def loads_C(nc, S, A, sb, load, zeroed):
    q = "L1_attn_"
    for w in "qkv":
        load(sb("C_w" + w, [D, HD])[:, :], A[q + "W" + w][:, :])
    load(sb("C_wo", [P, 2, D])[:], A[q + "Wo"].rearrange("(u p) d -> p u d", p=P))
    load(sb("C_bo", [P, D])[:, :], A[q + "bo"].rearrange("(a n) -> a n", a=1).to_broadcast([P, D]))


def alibi_attention(nc, S, A):
    h, ident = S["h"], S["ident"]
    SCALE = 1.0 / float(np.sqrt(CH))
    with ExitStack() as ctx:
        def sb(name, shape, dt=F32):
            return ctx.enter_context(nc.sbuf_tensor(f"C_{name}", shape, dt))

        def ps(name, shape):
            return ctx.enter_context(nc.psum_tensor(f"C_{name}", shape, F32))

        sem = ctx.enter_context(semaphores(nc, "C"))

        xc, sq = sb("xc", [P, G, D]), sb("sq", [P, G, D])
        total, var, rstd = sb("total", [P, G]), sb("var", [P, G]), sb("rstd", [P, G])
        xn = sb("xn", [P, 2, G, D])
        xT = sb("xT", [D, 2, COLS])
        qT = sb("qT", [P, 2, 2, COLS])
        kD = sb("kD", [P, 2, 2, G, 4, P])
        v = sb("v", [P, 2, G, NH, CH + 1])
        bias = sb("bias", [P, NH, P], BF16)
        ident16 = sb("ident16", [P, P], BF16)
        top = sb("top", [P, NH])
        e = sb("e", [P, 2, NH, P])
        eT = sb("eT", [P, 2, NH, P])
        rsum = sb("rsum", [P, NH])
        o = sb("o", [P, 2, G, HD])
        oT = sb("oT", [P, 2, COLS])
        xT_ps = ps("xT_ps", [P, G // 2, P])
        ring_ps = ps("ring_ps", [P, 2, COLS])
        s_ps = ps("s_ps", [P, NH, P])
        eT_ps = ps("eT_ps", [P, NH, P])
        o_ps = ps("o_ps", [P, NH, CH + 1])
        with ExitStack() as c2:
            alibi = c2.enter_context(nc.sbuf_tensor("C_alibi", [P, NH * P], F32))
            alibi_in = c2.enter_context(semaphores(nc, "C_setup"))("alibi_in")
            with nc.Block() as block:
                @block.sync
                def _(sp):
                    sp.dma_start(alibi[:, :], A["alibi"][:, :]).then_inc(alibi_in, 16)

                @block.vector
                def _(dve):
                    dve.wait_ge(alibi_in, 16)
                    nc.vector.tensor_copy(bias[:, :, :].rearrange("p h s -> p (h s)"), alibi[:, :])
                    nc.vector.tensor_copy(ident16[:, :], ident[:, :])
                    nc.vector.memset(kD[:], 0.0)
                    nc.vector.memset(v[:, :, :, :, CH:CH + 1], 1.0)

        stats_chain, var_ready, rstd_ready, xn_ready = sem("stats_chain"), sem("var_ready"), sem("rstd_ready"), sem("xn_ready")
        xT_ps_ready, xT_ready = sem("xT_ps_ready"), sem("xT_ready")
        filled = [[sem(f"{w}{u}_filled") for w in ("q", "k", "v", "oT")] for u in range(2)]
        emptied = [[sem(f"{w}{u}_emptied") for w in ("q", "k", "v", "oT")] for u in range(2)]
        y_ready, y_used = sem("y_ready"), sem("y_used")
        s_ready, top_ready, shifted, e_ready = sem("s_ready"), sem("top_ready"), sem("shifted"), sem("e_ready")
        eT_ps_ready, eT_a, eT_d = sem("eT_ps_ready"), sem("eT_a"), sem("eT_d")
        o_ready, rsum_ready, o_done = sem("o_ready"), sem("rsum_ready"), sem("o_done")

        def empty(eng, w, n, p, u, copy, scaled):
            eng.wait_ge(filled[u]["qkv".index(w)], n + 1)
            if w == "q":
                wait_reuse(eng, eT_ps_ready, (n - 1) * G)
                scaled(qT[:, p, u, :], ring_ps[:, u, :]).then_inc(emptied[u][0], 1)
            if w == "k":
                for j in range(4):
                    rows = slice(32 * j, 32 * j + 32)
                    ins = copy(kD[rows, p, u, :, j, :], ring_ps[rows, u, :].rearrange("p (g t) -> p g t", g=G))
                ins.then_inc(emptied[u][1], 1)
            if w == "v":
                wait_reuse(eng, o_ready, (n - 1) * G)
                for g in range(2):
                    ins = copy(v[:, p, 2 * u + g, :, 0:CH], ring_ps[:, u, HD * g:HD * (g + 1)].rearrange("p (h c) -> p h c", c=CH))
                ins.then_inc(emptied[u][2], 1)

        with nc.Block() as block:
            @block.vector
            def _(dve):
                def softmax(g, n, p):
                    m = n * G + g
                    dve.wait_ge(s_ready, m + 1)
                    nc.vector.tensor_reduce(top[:, :], s_ps[:, :, :], X, ALU.max).then_inc(top_ready, 1)
                    dve.wait_ge(top_ready, m + 1)
                    wait_reuse(dve, eT_ps_ready, m - 1)
                    nc.vector.tensor_tensor(e[:, g % 2, :, :], s_ps[:, :, :], bc(top[:, :], P), ALU.subtract).then_inc(shifted, 1)

                def turned(g, n, p):
                    m = n * G + g
                    dve.wait_ge(eT_ps_ready, m + 1)
                    wait_reuse(dve, o_ready, m - 1)
                    nc.vector.tensor_copy(eT[:, g % 2, 4:8, :], eT_ps[:, 4:8, :]).then_inc(eT_d, 1)

                def output(g, n, p):
                    m = n * G + g
                    dve.wait_ge(o_ready, m + 1)
                    nc.vector.reciprocal(rsum[:, :], o_ps[:, :, CH]).then_inc(rsum_ready, 1)
                    dve.wait_ge(rsum_ready, m + 1)
                    if g == 0:
                        wait_reuse(dve, filled[1][3], n - 1)
                    nc.vector.tensor_tensor(o[:, p, g, :].rearrange("p (h c) -> p h c", c=CH), o_ps[:, :, 0:CH],
                                            bc(rsum[:, :], CH), ALU.mult).then_inc(o_done, 1)

                def front(w, n, p):
                    empty(dve, w, n, p, 1, nc.vector.tensor_copy,
                          lambda out, in_: nc.vector.tensor_scalar(out, in_, SCALE, None, ALU.mult))

                def slot(g, n, p):
                    f = n + 1
                    if g == 0 and exists(f):
                        chain = Chain(dve, stats_chain, f, 4)
                        norm_stats(dve, nc, chain, h[:, bass.ds(f * G, G), :], xc[:, :, :], sq[:, :, :], total[:, :], var[:, :]).then_inc(var_ready, 1)
                        chain.end()
                    if g == 2 and exists(f):
                        front("q", f, 1 - p)
                    if g == 3 and exists(f):
                        front("v", f, 1 - p)
                    if exists(n):
                        softmax(g, n, p)
                    if g == 2 and exists(f):
                        front("k", f, 1 - p)
                    if g == 0 and exists(f):
                        dve.wait_ge(rstd_ready, f + 1)
                        wait_reuse(dve, xT_ps_ready, f - 1)
                        nc.vector.tensor_tensor(xn[:, 1 - p, :, :], xc[:, :, :], bc(rstd[:, :], D), ALU.mult).then_inc(xn_ready, 1)
                        dve.wait_ge(xn_ready, f + 1)
                    if g == 3 and exists(n - 1):
                        dve.wait_ge(filled[1][3], n)
                        wait_reuse(dve, y_ready, n - 1)
                        nc.vector.tensor_copy(oT[:, 1, :], ring_ps[:, 1, :]).then_inc(emptied[1][3], 1)
                    for back, piece in ((1, turned), (2, output)):
                        at = before(g, n, p, back)
                        if exists(at[1]):
                            piece(*at)
                    if g == 3 and exists(n - 1):
                        dve.wait_ge(y_ready, n)
                        hn = h[:, bass.ds((n - 1) * G, G), :]
                        nc.vector.tensor_tensor(hn, hn, ring_ps[:, 1, 0:G * D].rearrange("p (g d) -> p g d", g=G), ALU.add).then_inc(y_used, 1)
                        dve.wait_ge(y_used, 2 * n - 1)
                        nc.vector.tensor_tensor(hn, hn, mid(S["C_bo"][:, :], G), ALU.add).then_inc(y_used, 1)

                sweep(dve, slot, G)

            @block.gpsimd
            def _(pool):
                def powers(n, p):
                    pool.wait_ge(var_ready, n + 1)
                    nc.gpsimd.tensor_tensor(rstd[:, :], var[:, :], S["neg_half"][:, 0:G], ALU.pow).then_inc(rstd_ready, 1)

                pipeline(pool, [powers], TILES)

            @block.scalar
            def _(act):
                def front(w, n, p):
                    empty(act, w, n, p, 0, nc.scalar.copy, lambda out, in_: nc.scalar.mul(out, in_, SCALE))

                def slot(g, n, p):
                    f = n + 1
                    if g == 2 and exists(f):
                        front("q", f, 1 - p)
                    if g == 3 and exists(f):
                        front("v", f, 1 - p)
                    if exists(n):
                        m = n * G + g
                        act.wait_ge(shifted, m + 1)
                        nc.scalar.activation(e[:, g % 2, :, :], e[:, g % 2, :, :], ACT.Exp).then_inc(e_ready, 1)
                    if g == 2 and exists(f):
                        front("k", f, 1 - p)
                    if g == 1 and exists(f):
                        act.wait_ge(xT_ps_ready, f + 1)
                        wait_reuse(act, filled[1][2], f - 1)
                        for q in range(2):
                            ins = nc.scalar.copy(xT[:, 1 - p, :].rearrange("d (g q t) -> d g q t", g=G // 2, q=2)[:, :, q, :],
                                                 xT_ps[q * D:(q + 1) * D, :, :])
                        ins.then_inc(xT_ready, 1)
                    if g == 3 and exists(n - 1):
                        act.wait_ge(filled[0][3], n)
                        wait_reuse(act, y_ready, n - 1)
                        nc.scalar.copy(oT[:, 0, :], ring_ps[:, 0, :]).then_inc(emptied[0][3], 1)
                    b, tile, _ = before(g, n, p, 1)
                    if exists(tile):
                        m = tile * G + b
                        act.wait_ge(eT_ps_ready, m + 1)
                        wait_reuse(act, o_ready, m - 1)
                        nc.scalar.copy(eT[:, b % 2, 0:4, :], eT_ps[:, 0:4, :]).then_inc(eT_a, 1)

                sweep(act, slot, G)

            @block.tensor
            def _(pe):
                def scores(g, n, p):
                    wait_reuse(pe, shifted, n * G + g)
                    if g == 0:
                        pe.wait_ge(emptied[0][1], n + 1)
                        pe.wait_ge(emptied[1][1], n + 1)
                    for u in range(2):
                        nc.tensor.matmul(s_ps[:, 4 * u:4 * u + 4, :], ident16[:, :], bias[:, 4 * u:4 * u + 4, :], start=True, stop=False)
                        ins = nc.tensor.matmul(s_ps[:, 4 * u:4 * u + 4, :], qT[:, p, u, g * P:(g + 1) * P], kD[:, p, u, g, :, :], start=False, stop=True)
                    ins.then_inc(s_ready, 1)

                def turn(g, n, p):
                    m = n * G + g
                    pe.wait_ge(e_ready, m + 1)
                    wait_reuse(pe, eT_a, m)
                    wait_reuse(pe, eT_d, m)
                    for head in range(NH):
                        ins = nc.tensor.transpose(eT_ps[:, head, :], e[:, g % 2, head, :], ident[:, :])
                    ins.then_inc(eT_ps_ready, 1)

                def values(g, n, p):
                    m = n * G + g
                    pe.wait_ge(eT_a, m + 1)
                    pe.wait_ge(eT_d, m + 1)
                    if g == 0:
                        pe.wait_ge(emptied[0][2], n + 1)
                        pe.wait_ge(emptied[1][2], n + 1)
                    wait_reuse(pe, o_done, m)
                    for head in range(NH):
                        ins = nc.tensor.matmul(o_ps[:, head, :], eT[:, g % 2, head, :], v[:, p, g, head, :], start=True, stop=True)
                    ins.then_inc(o_ready, 1)

                def front(w, n, p):
                    for u in range(2):
                        if w == "q":
                            wait_reuse(pe, emptied[u][2], n)
                            if u == 0:
                                wait_reuse(pe, emptied[0][3], n - 2)
                            else:
                                wait_reuse(pe, y_used, 2 * (n - 2))
                        else:
                            pe.wait_ge(emptied[u]["kv".index(w)], n + 1)
                        if w == "v":
                            for g in range(2):
                                b = 2 * u + g
                                ins = nc.tensor.matmul(ring_ps[:, u, HD * g:HD * (g + 1)], xT[:, p, b * P:(b + 1) * P], S["C_wv"][:, :], start=True, stop=True)
                        else:
                            if w == "q" and u == 0:
                                pe.wait_ge(xT_ready, n + 1)
                            ins = nc.tensor.matmul(ring_ps[:, u, :], S["C_w" + w][:, u * P:(u + 1) * P], xT[:, p, :], start=True, stop=True)
                        ins.then_inc(filled[u]["qkv".index(w)], 1)

                def slot(g, n, p):
                    f = n + 1
                    if exists(n):
                        scores(g, n, p)
                    if g == 1 and exists(f):
                        pe.wait_ge(xn_ready, f + 1)
                        wait_reuse(pe, xT_ready, f)
                        for q in range(G // 2):
                            ins = nc.tensor.transpose(xT_ps[:, q, :], xn[:, 1 - p, 2 * q:2 * q + 2, :].rearrange("p g d -> p (g d)"), ident[:, :])
                        ins.then_inc(xT_ps_ready, 1)
                    if g == 2 and exists(f):
                        front("k", f, 1 - p)
                    if g == 3 and exists(n - 1):
                        pe.wait_ge(o_done, n * G)
                        for u in range(2):
                            pe.wait_ge(emptied[u][2], n + 2 if exists(f) else TILES)
                            for q in range(G):
                                ins = nc.tensor.transpose(ring_ps[:, u, q * P:(q + 1) * P], o[:, 1 - p, q, u * P:(u + 1) * P], ident[:, :])
                            ins.then_inc(filled[u][3], 1)
                    for back, piece in ((1, turn), (2, values)):
                        at = before(g, n, p, back)
                        if exists(at[1]):
                            piece(*at)
                    if g == 1 and exists(f):
                        front("q", f, 1 - p)
                    if g == 2 and exists(f):
                        front("v", f, 1 - p)
                    if g == 3 and exists(n - 1):
                        pe.wait_ge(emptied[0][3], n)
                        pe.wait_ge(emptied[1][3], n)
                        for q in range(G):
                            for u in range(2):
                                ins = nc.tensor.matmul(ring_ps[:, 1, D * q:D * (q + 1)], oT[:, u, q * P:(q + 1) * P], S["C_wo"][:, u, :],
                                                       start=(u == 0), stop=(u == 1))
                        ins.then_inc(y_ready, 1)

                sweep(pe, slot, G)


PERIODS = (24.0, 720.0)
NS = len(PERIODS)


def constants_E(c):
    idx = np.arange(T, dtype=np.float32)
    dist = np.abs(idx[:, None] - idx[None, :])
    c["cosines"] = np.stack([np.cos(np.float32(2.0 * np.pi) * dist / np.float32(t)) for t in PERIODS], axis=1).astype(np.float32)


def loads_E(nc, S, A, sb, load, zeroed):
    q = "L2_attn_"
    for w in "qkv":
        tile = sb("E_w" + w, [D + 1, D])
        load(tile[0:D, :], A[q + "W" + w][:, :])
        load(tile[D:D + 1, :], A[q + "b" + w].rearrange("(a e) -> a e", a=1))
    load(sb("E_beta", [P, NS])[:, :], A[q + "beta"].rearrange("(a n) -> a n", a=1).to_broadcast([P, NS]))
    load(sb("E_cos", [P, NS, T])[:], A["cosines"][:, :, :])


def periodic_attention(nc, S):
    h, ident = S["h"], S["ident"]
    SCALE = 1.0 / float(np.sqrt(D))
    with ExitStack() as ctx:
        def sb(name, shape, dt=F32):
            return ctx.enter_context(nc.sbuf_tensor(f"E_{name}", shape, dt))

        def ps(name, shape):
            return ctx.enter_context(nc.psum_tensor(f"E_{name}", shape, F32))

        sem = ctx.enter_context(semaphores(nc, "E"))

        xc, sq = sb("xc", [P, G, D]), sb("sq", [P, G, D])
        total, var, rstd = sb("total", [P, G]), sb("var", [P, G]), sb("rstd", [P, G])
        xn = sb("xn", [P, 2, G, D])
        xT = sb("xT", [D + 1, 2, COLS])
        qT, kT = sb("qT", [D, 2, COLS]), sb("kT", [D, 2, COLS])
        v = sb("v", [P, 2, G, D + 1])
        bias = sb("bias", [P, NS, T])
        s = sb("s", [P, G, T])
        top = sb("top", [P, G])
        e = sb("e", [P, G, T])
        eT = sb("eT", [P, G, P])
        rsum = sb("rsum", [P, G])
        o = sb("o", [P, G, D])
        xT_ps = ps("xT_ps", [P, G // 2, P])
        q_ps, k_ps, v_ps = ps("q_ps", [D, COLS]), ps("k_ps", [D, COLS]), ps("v_ps", [P, G, D])
        s_ps, eT_ps, o_ps = ps("s_ps", [P, G, T]), ps("eT_ps", [P, G, P]), ps("o_ps", [P, G, D + 1])
        names = ("stats_chain var_ready rstd_ready xn_ready xT_ps_ready xT_ready q_ready q_done k_ready k_done v_ready v_done "
                 "s_ready back_chain biased shifted e_ready eT_ready eT_done o_ready o_chain consts_set").split()
        (stats_chain, var_ready, rstd_ready, xn_ready, xT_ps_ready, xT_ready, q_ready, q_done, k_ready, k_done, v_ready, v_done,
         s_ready, back_chain, biased, shifted, e_ready, eT_ready, eT_done, o_ready, o_chain, consts_set) = map(sem, names)

        with nc.Block() as block:
            @block.vector
            def _(dve):
                nc.vector.memset(xT[D:D + 1, :, :], 1.0)
                nc.vector.memset(v[:, :, :, D:D + 1], 1.0)
                nc.vector.tensor_scalar(bias[:, 0, :], S["E_cos"][:, 0, :], S["E_beta"][:, 0:1], None, ALU.mult).then_inc(consts_set, 1)
                dve.wait_ge(consts_set, 1)
                nc.vector.scalar_tensor_tensor(out=bias[:, 1, :], in0=S["E_cos"][:, 1, :], scalar=S["E_beta"][:, 1:2],
                                               in1=bias[:, 0, :], op0=ALU.mult, op1=ALU.add).then_inc(consts_set, 1)
                dve.wait_ge(consts_set, 2)

                def stats(n, p):
                    chain = Chain(dve, stats_chain, n, 4)
                    norm_stats(dve, nc, chain, h[:, bass.ds(n * G, G), :], xc[:, :, :], sq[:, :, :], total[:, :], var[:, :]).then_inc(var_ready, 1)
                    chain.end()

                def norm(n, p):
                    dve.wait_ge(rstd_ready, n + 1)
                    wait_reuse(dve, xT_ps_ready, n - 1)
                    nc.vector.tensor_tensor(xn[:, p, :, :], xc[:, :, :], bc(rstd[:, :], D), ALU.mult).then_inc(xn_ready, 1)
                    dve.wait_ge(xn_ready, n + 1)

                def front(n, p):
                    dve.wait_ge(k_ready, n + 1)
                    wait_reuse(dve, s_ready, n - 1)
                    nc.vector.tensor_copy(kT[:, p, :], k_ps[:, :]).then_inc(k_done, 1)
                    dve.wait_ge(v_ready, n + 1)
                    wait_reuse(dve, o_ready, n - 1)
                    nc.vector.tensor_copy(v[:, p, :, 0:D], v_ps[:, :, :]).then_inc(v_done, 1)

                def softmax(n, p):
                    chain = Chain(dve, back_chain, n, 1)
                    dve.wait_ge(s_ready, n + 1)
                    nc.vector.tensor_tensor(s[:, :, :], s_ps[:, :, :], mid(bias[:, 1, :], G), ALU.add).then_inc(biased, 1)
                    dve.wait_ge(biased, n + 1)
                    chain(nc.vector.tensor_reduce(top[:, :], s[:, :, :], X, ALU.max))
                    chain.end()
                    wait_reuse(dve, eT_ready, n)
                    nc.vector.tensor_tensor(e[:, :, :], s[:, :, :], bc(top[:, :], T), ALU.subtract).then_inc(shifted, 1)

                def turned(n, p):
                    dve.wait_ge(eT_ready, n + 1)
                    wait_reuse(dve, o_ready, n)
                    nc.vector.tensor_copy(eT[:, :, :], eT_ps[:, :, :]).then_inc(eT_done, 1)

                def output(n, p):
                    chain = Chain(dve, o_chain, n, 3)
                    dve.wait_ge(o_ready, n + 1)
                    chain(nc.vector.reciprocal(rsum[:, :], o_ps[:, :, D]))
                    chain(nc.vector.tensor_tensor(o[:, :, :], o_ps[:, :, 0:D], bc(rsum[:, :], D), ALU.mult))
                    hn = h[:, bass.ds(n * G, G), :]
                    chain(nc.vector.tensor_tensor(hn, hn, o[:, :, :], ALU.add))
                    chain.end()

                in_order(dve, [(3, output), (0, stats), (2, softmax), (0, norm), (1, front), (2, turned)], TILES)

            @block.gpsimd
            def _(pool):
                def powers(n, p):
                    pool.wait_ge(var_ready, n + 1)
                    nc.gpsimd.tensor_tensor(rstd[:, :], var[:, :], S["neg_half"][:, 0:G], ALU.pow).then_inc(rstd_ready, 1)

                in_order(pool, [(0, powers)], TILES)

            @block.scalar
            def _(act):
                def turned(n, p):
                    act.wait_ge(xT_ps_ready, n + 1)
                    wait_reuse(act, v_ready, n - 1)
                    for q in range(2):
                        ins = nc.scalar.copy(xT[0:D, p, :].rearrange("d (g q t) -> d g q t", g=G // 2, q=2)[:, :, q, :],
                                             xT_ps[q * D:(q + 1) * D, :, :])
                    ins.then_inc(xT_ready, 1)

                def queries(n, p):
                    act.wait_ge(q_ready, n + 1)
                    wait_reuse(act, s_ready, n - 1)
                    nc.scalar.mul(qT[:, p, :], q_ps[:, :], SCALE).then_inc(q_done, 1)

                def exponentials(n, p):
                    act.wait_ge(shifted, n + 1)
                    nc.scalar.activation(e[:, :, :], e[:, :, :], ACT.Exp).then_inc(e_ready, 1)

                in_order(act, [(1, turned), (2, exponentials), (1, queries)], TILES)

            @block.tensor
            def _(pe):
                pe.wait_ge(consts_set, 2)

                def turn(n, p):
                    pe.wait_ge(xn_ready, n + 1)
                    wait_reuse(pe, xT_ready, n)
                    for q in range(G // 2):
                        ins = nc.tensor.transpose(xT_ps[:, q, :], xn[:, p, 2 * q:2 * q + 2, :].rearrange("p g d -> p (g d)"), ident[:, :])
                    ins.then_inc(xT_ps_ready, 1)

                def project(n, p):
                    pe.wait_ge(xT_ready, n + 1)
                    wait_reuse(pe, v_done, n)
                    for g in range(G):
                        ins = nc.tensor.matmul(v_ps[:, g, :], xT[:, p, g * P:(g + 1) * P], S["E_wv"][:, :], start=True, stop=True)
                    ins.then_inc(v_ready, 1)
                    wait_reuse(pe, q_done, n)
                    nc.tensor.matmul(q_ps[:, :], S["E_wq"][:, :], xT[:, p, :], start=True, stop=True).then_inc(q_ready, 1)
                    wait_reuse(pe, k_done, n)
                    nc.tensor.matmul(k_ps[:, :], S["E_wk"][:, :], xT[:, p, :], start=True, stop=True).then_inc(k_ready, 1)

                def scores(n, p):
                    pe.wait_ge(q_done, n + 1)
                    pe.wait_ge(k_done, n + 1)
                    wait_reuse(pe, biased, n)
                    for g in range(G):
                        ins = nc.tensor.matmul(s_ps[:, g, :], qT[:, p, g * P:(g + 1) * P], kT[:, p, g * P:(g + 1) * P], start=True, stop=True)
                    ins.then_inc(s_ready, 1)

                def turn_e(n, p):
                    pe.wait_ge(e_ready, n + 1)
                    wait_reuse(pe, eT_done, n)
                    for g in range(G):
                        ins = nc.tensor.transpose(eT_ps[:, g, :], e[:, g, :], ident[:, :])
                    ins.then_inc(eT_ready, 1)

                def values(n, p):
                    pe.wait_ge(eT_done, n + 1)
                    pe.wait_ge(v_done, n + 1)
                    wait_reuse(pe, o_chain, n * 3)
                    for g in range(G):
                        ins = nc.tensor.matmul(o_ps[:, g, :], eT[:, g, :], v[:, p, g, :], start=True, stop=True)
                    ins.then_inc(o_ready, 1)

                in_order(pe, [(3, values), (1, turn), (2, scores), (1, project), (2, turn_e)], TILES)


NR = 16
NL = 2
PER_ROUTE = 2


def loads_F(nc, S, A, sb, load, zeroed):
    q = "L2_ffn_"
    load(sb("F_wi", [D + 1, HID])[0:D, :], A[q + "Wi"][:, :])
    load(S["F_wi"][D:D + 1, :], A[q + "bi"].rearrange("(a e) -> a e", a=1))
    mix = sb("F_mix", [HID, NL, NR, HID + 1])
    for l in range(NL):
        load(mix[:, l, :, 0:HID], A[q + "Wr"][l].rearrange("e d j -> d e j"))
    load(sb("F_ws", [HID, NL, HID])[:], A[q + "Ws"].rearrange("l a d j -> d (l a) j"))
    load(sb("F_br", [HID, NL, NR])[:], A[q + "br"][:, :, :])
    load(sb("F_bs", [HID, NL])[:, :], A[q + "bs"].rearrange("j l a -> j (l a)"))
    load(sb("F_wo", [HID, D])[:, :], A[q + "Wo"][:, :])
    load(sb("F_bo", [P, D])[:, :], A[q + "bo"].rearrange("(a n) -> a n", a=1).to_broadcast([P, D]))
    load(sb("F_route", [1, B // PER_ROUTE], I32)[:, :], A[q + "route_id"].rearrange("(a n) -> a n", a=1))


def routed_mlp(nc, S):
    h, ident, mix = S["h"], S["ident"], S["F_mix"]
    R = G // PER_ROUTE
    with ExitStack() as ctx:
        def sb(name, shape, dt=F32):
            return ctx.enter_context(nc.sbuf_tensor(f"F_{name}", shape, dt))

        def ps(name, shape):
            return ctx.enter_context(nc.psum_tensor(f"F_{name}", shape, F32))

        sem = ctx.enter_context(semaphores(nc, "F"))

        xc, sq = sb("xc", [P, G, D]), sb("sq", [P, G, D])
        total, var, rstd = sb("total", [P, G]), sb("var", [P, G]), sb("rstd", [P, G])
        xn = sb("xn", [P, 2, G, D])
        xT = sb("xT", [D + 1, 2, COLS])
        chosen = sb("chosen", [HID, 2, R, NL, HID + 1])
        hid = sb("hid", [HID, 2, COLS])
        deep = sb("deep", [HID, NL, COLS])
        xT_ps = ps("xT_ps", [P, G // 2, P])
        hid_ps, deep_ps, y_ps = ps("hid_ps", [P, COLS]), ps("deep_ps", [P, NL, COLS]), ps("y_ps", [P, G, D])
        names = ("stats_chain var_ready rstd_ready xn_ready xT_ps_ready xT_ready hid_ps_ready hid_ready chosen_ready "
                 "y_ready y_used mixed").split()
        (stats_chain, var_ready, rstd_ready, xn_ready, xT_ps_ready, xT_ready, hid_ps_ready, hid_ready, chosen_ready,
         y_ready, y_used, mixed) = map(sem, names)
        deep_ps_ready = [sem(f"deep{l}_ps_ready") for l in range(NL)]
        deep_ready = [sem(f"deep{l}_ready") for l in range(NL)]

        with nc.Block() as block:
            @block.vector
            def _(dve):
                nc.vector.memset(xT[D:D + 1, :, :], 1.0)
                for l in range(NL):
                    nc.vector.tensor_tensor(S["F_ws"][:, l, :], S["F_ws"][:, l, :], ident[:, :], ALU.add).then_inc(mixed, 1)
                dve.wait_ge(mixed, NL)
                for l in range(NL):
                    nc.vector.tensor_tensor(mix[:, l, :, 0:HID], mix[:, l, :, 0:HID], mid(S["F_ws"][:, l, :], NR), ALU.add)
                    ins = nc.vector.tensor_tensor(mix[:, l, :, HID], S["F_br"][:, l, :],
                                                  S["F_bs"][:, l:l + 1].to_broadcast([HID, NR]), ALU.add)
                ins.then_inc(mixed, 1)

                def norm(n, p):
                    chain = Chain(dve, stats_chain, n, 4)
                    norm_stats(dve, nc, chain, h[:, bass.ds(n * G, G), :], xc[:, :, :], sq[:, :, :], total[:, :], var[:, :]).then_inc(var_ready, 1)
                    dve.wait_ge(rstd_ready, n + 1)
                    wait_reuse(dve, xT_ps_ready, n - 1)
                    nc.vector.tensor_tensor(xn[:, p, :, :], xc[:, :, :], bc(rstd[:, :], D), ALU.mult).then_inc(xn_ready, 1)
                    dve.wait_ge(xn_ready, n + 1)
                    chain.end()

                def output(n, p):
                    dve.wait_ge(y_ready, n + 1)
                    hn = h[:, bass.ds(n * G, G), :]
                    nc.vector.tensor_tensor(hn, hn, y_ps[:, :, :], ALU.add).then_inc(y_used, 1)
                    dve.wait_ge(y_used, 2 * n + 1)
                    nc.vector.tensor_tensor(hn, hn, mid(S["F_bo"][:, :], G), ALU.add).then_inc(y_used, 1)

                pipeline(dve, [norm, None, None, None, None, output], TILES)

            @block.gpsimd
            def _(pool):
                pool.wait_ge(mixed, NL + 1)

                def powers(n, p):
                    pool.wait_ge(var_ready, n + 1)
                    nc.gpsimd.tensor_tensor(rstd[:, :], var[:, :], S["neg_half"][:, 0:G], ALU.pow).then_inc(rstd_ready, 1)

                def choose(n, p):
                    wait_reuse(pool, deep_ready[NL - 1], n - 1)
                    for r in range(R):
                        expert = nc.gpsimd.value_load(S["F_route"][0:1, bass.ds(n * R + r, 1)], min_val=0, max_val=NR - 1)
                        ins = nc.gpsimd.tensor_copy(chosen[:, p, r, :, :], mix[:, :, bass.ds(expert, 1), :].rearrange("p l a j -> p l (a j)"))
                    ins.then_inc(chosen_ready, 1)

                pipeline(pool, [powers, None, choose], TILES)

            @block.scalar
            def _(act):
                def turned(n, p):
                    act.wait_ge(xT_ps_ready, n + 1)
                    wait_reuse(act, hid_ps_ready, n - 1)
                    for q in range(2):
                        ins = nc.scalar.copy(xT[0:D, p, :].rearrange("d (g q t) -> d g q t", g=G // 2, q=2)[:, :, q, :],
                                             xT_ps[q * D:(q + 1) * D, :, :])
                    ins.then_inc(xT_ready, 1)

                def first(n, p):
                    act.wait_ge(hid_ps_ready, n + 1)
                    wait_reuse(act, deep_ps_ready[0], n - 1)
                    nc.scalar.activation(hid[:, p, :], hid_ps[:, :], ACT.Relu).then_inc(hid_ready, 1)

                def layer(l):
                    def piece(n, p):
                        act.wait_ge(deep_ps_ready[l], n + 1)
                        wait_reuse(act, y_ready if l == NL - 1 else deep_ps_ready[l + 1], n)
                        for r in range(R):
                            cols = slice(r * COLS // R, (r + 1) * COLS // R)
                            ins = nc.scalar.activation(deep[:, l, cols], deep_ps[:, l, cols], ACT.Relu,
                                                       bias=chosen[:, p, r, l, HID:HID + 1])
                        ins.then_inc(deep_ready[l], 1)
                    return piece

                pipeline(act, [None, turned, first, layer(0), layer(1), None], TILES)

            @block.tensor
            def _(pe):
                pe.wait_ge(mixed, NL + 1)

                def turn(n, p):
                    pe.wait_ge(xn_ready, n + 1)
                    wait_reuse(pe, xT_ready, n)
                    for q in range(G // 2):
                        ins = nc.tensor.transpose(xT_ps[:, q, :], xn[:, p, 2 * q:2 * q + 2, :].rearrange("p g d -> p (g d)"), ident[:, :])
                    ins.then_inc(xT_ps_ready, 1)

                def first(n, p):
                    pe.wait_ge(xT_ready, n + 1)
                    wait_reuse(pe, hid_ready, n)
                    nc.tensor.matmul(hid_ps[:, :], S["F_wi"][:, :], xT[:, p, :], start=True, stop=True).then_inc(hid_ps_ready, 1)

                def layer(l):
                    def piece(n, p):
                        if l == 0:
                            pe.wait_ge(chosen_ready, n + 1)
                            pe.wait_ge(hid_ready, n + 1)
                        else:
                            pe.wait_ge(deep_ready[l - 1], n + 1)
                        wait_reuse(pe, deep_ready[l], n)
                        src = deep[:, l - 1, :] if l else hid[:, p, :]
                        for r in range(R):
                            cols = slice(r * COLS // R, (r + 1) * COLS // R)
                            ins = nc.tensor.matmul(deep_ps[:, l, cols], chosen[:, p, r, l, 0:HID], src[:, cols], start=True, stop=True)
                        ins.then_inc(deep_ps_ready[l], 1)
                    return piece

                def last(n, p):
                    pe.wait_ge(deep_ready[NL - 1], n + 1)
                    wait_reuse(pe, y_used, 2 * n)
                    for g in range(G):
                        ins = nc.tensor.matmul(y_ps[:, g, :], deep[:, NL - 1, g * P:(g + 1) * P], S["F_wo"][:, :], start=True, stop=True)
                    ins.then_inc(y_ready, 1)

                pipeline(pe, [None, turn, first, layer(0), layer(1), last], TILES)


NST = 16
TAPS = 4
RANK = 4
DIRS = "fb"
PAD = T + TAPS


def constants_G(c):
    c["part_rows"] = np.tile(np.eye(2 * NST, dtype=np.float32), (3, 1))


def loads_G(nc, S, A, sb, load, zeroed):
    load(sb("G_rows", [96, 2 * NST])[:, :], A["part_rows"][:, :])
    for k, c in enumerate(DIRS):
        q = f"L3_attn_{c}_"
        w_in = sb("G_in" + c, [2 * D, 2 * P])
        for u in range(2):
            load(w_in[u * D:(u + 1) * D, :], A[q + "in_w"][:, :])
        taps = sb("G_taps" + c, [2 * D, 2, P])
        for u in range(2):
            for j in range(2):
                k_tap = TAPS - 1 - (2 * j + u)
                load(taps[u * D:(u + 1) * D, j, :], A[q + "conv_w"][k_tap:k_tap + 1, :].to_broadcast([D, P]))
        xp = sb("G_xproj" + c, [P, 2 * NST + RANK])
        load(xp[:, 0:2 * NST], A[q + "xproj_w"][:, RANK:])
        load(xp[:, 2 * NST:], A[q + "xproj_w"][:, 0:RANK])
        load(sb("G_dt" + c, [2 * NST + RANK, P])[2 * NST:, :], A[q + "dt_w"][:, :])
        for v in ("conv_b", "dt_b", "D"):
            load(sb(f"G_{v}{c}", [P, 1])[:, :], A[q + v].rearrange("(d a) -> d a", a=1))
        load(sb("G_a" + c, [P, NST])[:, :], A[q + "A_log"][:, :])
        load(sb("G_out" + c, [P, D])[:, :], A[q + "out_w"][:, :])


def mamba(nc, S):
    h, ident = S["h"], S["ident"]
    SLOTS = 2 * NST
    RING = 8
    LAG = 4
    with ExitStack() as ctx:
        def sb(name, shape, dt=F32):
            return ctx.enter_context(nc.sbuf_tensor(f"G_{name}", shape, dt))

        def ps(name, shape):
            return ctx.enter_context(nc.psum_tensor(f"G_{name}", shape, F32))

        sem = ctx.enter_context(semaphores(nc, "G"))

        xc, sq = sb("xc", [P, G, D]), sb("sq", [P, G, D])
        total, var, rstd = sb("total", [P, G]), sb("var", [P, G]), sb("rstd", [P, G])
        xn = sb("xn", [P, 2, G, D])
        xp = sb("xp", [2 * D, 2, G, PAD])
        conv = sb("conv", [2 * D, 2, 2, P])
        u = sb("u", [P, 2, 2, COLS])
        zg = sb("zg", [P, 2, 2, COLS])
        low = sb("low", [2 * NST + RANK, 2, COLS])
        parts = sb("parts", [96, 2, 2, COLS], BF16)
        rest = sb("rest", [2 * NST, COLS])
        middle = sb("middle", [2 * NST, COLS], BF16)
        rows = sb("rows16", [96, 2 * NST], BF16)
        mag, ln = sb("mag", [P, 2, COLS]), sb("ln", [P, 2, COLS])
        round1, one = sb("round1", [P, COLS]), sb("one", [P, 1])
        positive = sb("positive", [P, 2, COLS])
        dt, du = sb("dt", [P, 2, 2, COLS]), sb("du", [P, 2, 2, COLS])
        decay = sb("decay", [P, 4, G, T])
        drive = sb("drive", [P, 2, COLS])
        state = sb("state", [P, RING, COLS])
        c_wide = sb("c_wide", [P, RING, COLS])
        mixed, gated = sb("mixed", [P, COLS]), sb("gated", [P, COLS])
        ring_ps, b_ps, c_ps = ps("ring_ps", [P, 2, COLS]), ps("b_ps", [P, 2, COLS]), ps("c_ps", [P, 2, COLS])
        y_ps, out_ps = ps("y_ps", [P, COLS]), ps("out_ps", [P, G, D])
        names = ("stats_chain var_ready rstd_ready xn_ready h_plus turned xp_ready conv_ready u_ready z_ready zg_ready low_ps low_ready "
                 "high_ready split_chain parts_ready dt_ps mag_ready exp_ready ln_ready positive_ready dt_chain dt_ready du_ready "
                 "b_ready c_ready decay_ready c_copied driven scanned weighted_done summed mixed_done gated_done out_ready h_done "
                 "setup setup_a").split()
        (stats_chain, var_ready, rstd_ready, xn_ready, h_plus, turned, xp_ready, conv_ready, u_ready, z_ready, zg_ready, low_ps, low_ready,
         high_ready, split_chain, parts_ready, dt_ps, mag_ready, exp_ready, ln_ready, positive_ready, dt_chain, dt_ready, du_ready,
         b_ready, c_ready, decay_ready, c_copied, driven, scanned, weighted_done, summed, mixed_done, gated_done, out_ready, h_done,
         setup, setup_a) = map(sem, names)

        with nc.Block() as block:
            @block.vector
            def _(dve):
                nc.vector.memset(xp[:], 0.0)
                nc.vector.memset(one[:], 1.0)
                nc.vector.memset(decay[:], 0.0)
                nc.vector.tensor_copy(rows[:, :], S["G_rows"][:, :])
                for k, c in enumerate(DIRS):
                    for j in range(2):
                        nc.vector.tensor_tensor(conv[:, k, j, :], S["G_in" + c][:, 0:P], S["G_taps" + c][:, j, :], ALU.mult)
                    nc.vector.tensor_scalar(S["G_a" + c][:, :], S["G_a" + c][:, :], 80.0, None, ALU.min).then_inc(setup, 1)
                dve.wait_ge(setup_a, 2)
                for c in DIRS:
                    nc.vector.tensor_scalar(S["G_a" + c][:, :], S["G_a" + c][:, :], -1.0, None, ALU.mult)

            @block.scalar
            def _(act):
                act.wait_ge(setup, 2)
                for c in DIRS:
                    nc.scalar.activation(S["G_a" + c][:, :], S["G_a" + c][:, :], ACT.Exp).then_inc(setup_a, 1)

        def run(eng, front, finish, slot_work):
            def work(n, p):
                if isinstance(n, int) and n == 0:
                    for slot in range(SLOTS):
                        front(slot, 0, p)
                for slot in range(SLOTS):
                    if not (isinstance(n, int) and n == 0 and slot < SLOTS // 2):
                        finish(slot, n - 1 if slot < NST else n, 1 - p if slot < NST else p)
                    if not (isinstance(n, int) and n == TILES - 1):
                        front(slot, n + 1, 1 - p)
                    slot_work(slot, n, p)

            pipeline(eng, [None, work], TILES)
            for slot in range(NST):
                finish(slot, TILES - 1, (TILES - 1) % 2)

        def nothing(*_):
            pass

        with nc.Block() as block:
            @block.vector
            def _(dve):
                def front(slot, n, p):
                    hn = h[:, bass.ds(n * G, G), :]
                    if slot in (0, 1, 2, 3):
                        if slot > 0:
                            dve.wait_ge(stats_chain, n * 4 + slot)
                        if slot == 0:
                            ins = nc.vector.tensor_reduce(total[:, :], hn, X, ALU.add)
                        if slot == 1:
                            ins = nc.vector.scalar_tensor_tensor(out=xc[:, :, :], in0=bc(total[:, :], D), scalar=-1.0 / D, in1=hn,
                                                                 op0=ALU.mult, op1=ALU.add)
                        if slot == 2:
                            ins = nc.vector.tensor_tensor(sq[:, :, :], xc[:, :, :], xc[:, :, :], ALU.mult)
                        if slot == 3:
                            ins = nc.vector.tensor_reduce(total[:, :], sq[:, :, :], X, ALU.add)
                        ins.then_inc(stats_chain, 1)
                    if slot == 4:
                        dve.wait_ge(stats_chain, n * 4 + 4)
                        nc.vector.tensor_scalar(var[:, :], total[:, :], 1.0 / D, EPS, ALU.mult, ALU.add).then_inc(var_ready, 1)
                    if slot == 7:
                        dve.wait_ge(rstd_ready, n + 1)
                        wait_reuse(dve, turned, n - 1)
                        nc.vector.tensor_tensor(xn[:, p, :, :], xc[:, :, :], bc(rstd[:, :], D), ALU.mult).then_inc(xn_ready, 1)
                    if slot == 8:
                        dve.wait_ge(xn_ready, n + 1)
                        nc.vector.tensor_tensor(hn, hn, xn[:, p, :, :], ALU.add).then_inc(h_plus, 1)
                    for k, first in ((0, 18), (1, 25)):
                        m = n * 2 + k
                        if slot == first:
                            dve.wait_ge(high_ready, m + 1)
                            wait_reuse(dve, c_ready, (m - 3) * NST)
                            wait_reuse(dve, parts_ready, m)
                            nc.vector.tensor_tensor(rest[:, :], low[0:32, k, :], parts[0:32, p, k, :], ALU.subtract).then_inc(split_chain, 1)
                            dve.wait_ge(split_chain, m * 2 + 1)
                            nc.vector.tensor_copy(middle[:, :], rest[:, :]).then_inc(split_chain, 1)
                        if slot == first + 1:
                            dve.wait_ge(split_chain, m * 2 + 2)
                            nc.vector.tensor_copy(parts[32:64, p, k, :], middle[:, :])
                            nc.vector.tensor_tensor(parts[64:96, p, k, :], rest[:, :], middle[:, :], ALU.subtract).then_inc(parts_ready, 1)
                    if slot in (23, 24):
                        k = slot - 23
                        dve.wait_ge(mag_ready, n * 2 + k + 1)
                        wait_reuse(dve, dt_ready, (n - 1) * 2 + k + 1)
                        nc.vector.tensor_scalar(positive[:, k, :], ring_ps[:, k, :], S["G_dt_b" + DIRS[k]][:, 0:1], 0.0,
                                                ALU.add, ALU.max).then_inc(positive_ready, 1)

                def finish(slot, n, p):
                    k = 1 if slot < NST else 0
                    m = n * 2 + k
                    if slot % NST == LAG:
                        dve.wait_ge(summed, (m + 1) * NST)
                        nc.vector.scalar_tensor_tensor(out=mixed[:, :], in0=u[:, p, k, :], scalar=S["G_D" + DIRS[k]][:, 0:1],
                                                       in1=y_ps[:, :], op0=ALU.mult, op1=ALU.add).then_inc(mixed_done, 1)
                    if slot % NST == LAG + 1:
                        dve.wait_ge(mixed_done, m + 1)
                        wait_reuse(dve, out_ready, m)
                        nc.vector.tensor_tensor(gated[:, :], mixed[:, :], zg[:, p, k, :], ALU.mult).then_inc(gated_done, 1)
                    if slot % NST == LAG + 4:
                        dve.wait_ge(out_ready, m + 1)
                        wait_reuse(dve, h_done, m)
                        dve.wait_ge(h_plus, n + 1)
                        hn = h[:, bass.ds(n * G, G), :]
                        nc.vector.tensor_tensor(hn, hn, out_ps[:, :, :], ALU.add).then_inc(h_done, 1)

                def slot_work(slot, n, p):
                    k, s, m = slot // NST, slot % NST, n * SLOTS + slot
                    if s == 0:
                        dve.wait_ge(du_ready, n * 2 + k + 1)
                    dve.wait_ge(b_ready, m + 1)
                    wait_reuse(dve, scanned, m - 1)
                    nc.vector.tensor_tensor(drive[:, slot % 2, :], b_ps[:, slot % 2, :], du[:, p, k, :], ALU.mult).then_inc(driven, 1)
                    dve.wait_ge(decay_ready, m + 1)
                    wait_reuse(dve, summed, m - RING + 1)
                    dve.wait_ge(driven, m + 1)
                    nc.vector.tensor_tensor_scan(state[:, slot % RING, :], decay[:, slot % 4, :, :].rearrange("p g t -> p (g t)"),
                                                 drive[:, slot % 2, :], 0.0, ALU.mult, ALU.add).then_inc(scanned, 1)

                run(dve, front, finish, slot_work)

            @block.gpsimd
            def _(pool):
                def dt_step(step, k, n, p):
                    m = n * 2 + k
                    r, ones = round1[:, :], one[:, :].to_broadcast([P, COLS])
                    if step == 0:
                        pool.wait_ge(exp_ready, m + 1)
                        wait_reuse(pool, dt_ready, m)
                        nc.gpsimd.tensor_tensor(r, mag[:, k, :], ones, ALU.add).then_inc(dt_chain, 1)
                    if step in (1, 2, 3):
                        pool.wait_ge(dt_chain, m * 4 + step)
                    if step == 1:
                        nc.gpsimd.tensor_tensor(r, r, ones, ALU.subtract).then_inc(dt_chain, 1)
                    if step == 2:
                        nc.gpsimd.tensor_tensor(r, r, mag[:, k, :], ALU.subtract).then_inc(dt_chain, 1)
                    if step == 3:
                        pool.wait_ge(ln_ready, m + 1)
                        nc.gpsimd.tensor_tensor(r, ln[:, k, :], r, ALU.subtract).then_inc(dt_chain, 1)
                    if step == 4:
                        pool.wait_ge(dt_chain, m * 4 + 4)
                        pool.wait_ge(positive_ready, m + 1)
                        wait_reuse(pool, decay_ready, (m - 3) * NST)
                        nc.gpsimd.tensor_tensor(dt[:, p, k, :], r, positive[:, k, :], ALU.add).then_inc(dt_ready, 1)
                    if step == 5:
                        pool.wait_ge(dt_ready, m + 1)
                        wait_reuse(pool, driven, (m - 3) * NST)
                        nc.gpsimd.tensor_tensor(du[:, p, k, :], dt[:, p, k, :], u[:, p, k, :], ALU.mult).then_inc(du_ready, 1)

                def front(slot, n, p):
                    if slot == 5:
                        pool.wait_ge(var_ready, n + 1)
                        nc.gpsimd.tensor_tensor(rstd[:, :], var[:, :], S["neg_half"][:, 0:G], ALU.pow).then_inc(rstd_ready, 1)
                    if 26 <= slot < 32:
                        dt_step(slot - 26, 0, n, p)

                def slot_work(slot, n, p):
                    m = n * SLOTS + slot
                    if slot < 6:
                        dt_step(slot, 1, n, p)
                    pool.wait_ge(scanned, m + 1)
                    pool.wait_ge(c_copied, m + 1)
                    nc.gpsimd.tensor_tensor(state[:, slot % RING, :], state[:, slot % RING, :], c_wide[:, slot % RING, :], ALU.mult).then_inc(weighted_done, 1)

                run(pool, front, nothing, slot_work)

            @block.scalar
            def _(act):
                def front(slot, n, p):
                    if slot == 10:
                        act.wait_ge(turned, n + 1)
                        wait_reuse(act, z_ready, (n - 1) * 2)
                        for q in range(2):
                            src = ring_ps[q * D:(q + 1) * D, 0, 0:2 * P].rearrange("p (g t) -> p g t", g=2)
                            for later in range(2):
                                dst = xp[later * D:(later + 1) * D, p, :, TAPS - 1 + later:TAPS - 1 + later + T]
                                ins = nc.scalar.copy(dst.rearrange("d (g q) t -> d g q t", q=2)[:, :, q, :], src)
                        ins.then_inc(xp_ready, 1)
                    if slot == 14:
                        for k in range(2):
                            act.wait_ge(conv_ready, n * 2 + k + 1)
                            wait_reuse(act, gated_done, (n - 1) * 2)
                            nc.scalar.activation(u[:, p, k, :], ring_ps[:, k, :], ACT.Silu, bias=S["G_conv_b" + DIRS[k]][:, :]).then_inc(u_ready, 1)
                    if slot == 27:
                        for k in range(2):
                            act.wait_ge(z_ready, n * 2 + k + 1)
                            nc.scalar.activation(zg[:, p, k, :], ring_ps[:, k, :], ACT.Silu).then_inc(zg_ready, 1)
                    if slot in (17, 18):
                        for k in (slot - 17,):
                            m = n * 2 + k
                            act.wait_ge(low_ps, m + 1)
                            wait_reuse(act, parts_ready, m - 1)
                            wait_reuse(act, dt_ps, m - 1)
                            nc.scalar.copy(low[:, k, :], ring_ps[0:2 * NST + RANK, k, :]).then_inc(low_ready, 1)
                            act.wait_ge(low_ready, m + 1)
                            wait_reuse(act, c_ready, (m - 3) * NST)
                            nc.scalar.copy(parts[0:32, p, k, :], low[0:32, k, :]).then_inc(high_ready, 1)
                    if slot in (21, 22):
                        for k in (slot - 21,):
                            m = n * 2 + k
                            act.wait_ge(dt_ps, m + 1)
                            wait_reuse(act, dt_ready, m - 1)
                            nc.scalar.activation(mag[:, k, :], ring_ps[:, k, :], ACT.Abs, bias=S["G_dt_b" + DIRS[k]][:, :]).then_inc(mag_ready, 1)
                    if slot == 24:
                        for k in range(2):
                            act.wait_ge(mag_ready, n * 2 + k + 1)
                            nc.scalar.activation(mag[:, k, :], mag[:, k, :], ACT.Exp, scale=-1.0).then_inc(exp_ready, 1)
                        for k in range(2):
                            act.wait_ge(exp_ready, n * 2 + k + 1)
                            nc.scalar.activation(ln[:, k, :], mag[:, k, :], ACT.Ln, bias=1.0).then_inc(ln_ready, 1)

                def slot_work(slot, n, p):
                    k, s, m = slot // NST, slot % NST, n * SLOTS + slot
                    if s == 0:
                        act.wait_ge(dt_ready, n * 2 + k + 1)
                    wait_reuse(act, scanned, m - 3)
                    nc.scalar.activation(decay[:, slot % 4, :, 1:], dt[:, p, k, :].rearrange("p (g t) -> p g t", g=G)[:, :, 1:],
                                         ACT.Exp, scale=S["G_a" + DIRS[k]][:, s:s + 1]).then_inc(decay_ready, 1)
                    act.wait_ge(c_ready, m + 1)
                    wait_reuse(act, weighted_done, m - RING + 1)
                    nc.scalar.copy(c_wide[:, slot % RING, :], c_ps[:, slot % 2, :]).then_inc(c_copied, 1)

                run(act, front, nothing, slot_work)

            @block.tensor
            def _(pe):
                def front(slot, n, p):
                    if slot == 9:
                        pe.wait_ge(xn_ready, n + 1)
                        wait_reuse(pe, zg_ready, n * 2)
                        for q in range(G // 2):
                            ins = nc.tensor.transpose(ring_ps[:, 0, q * P:(q + 1) * P], xn[:, p, 2 * q:2 * q + 2, :].rearrange("p g d -> p (g d)"), ident[:, :])
                        ins.then_inc(turned, 1)
                    if slot in (12, 13):
                        pe.wait_ge(xp_ready, n + 1)
                        for k in (slot - 12,):
                            for j in range(2):
                                at = TAPS - 1 - 2 * j
                                ins = nc.tensor.matmul(ring_ps[:, k, :], conv[:, k, j, :], xp[:, p, :, at:at + T], start=(j == 0), stop=(j == 1))
                            ins.then_inc(conv_ready, 1)
                    if slot in (25, 26):
                        for k in (slot - 25,):
                            pe.wait_ge(positive_ready, n * 2 + k + 1)
                            nc.tensor.matmul(ring_ps[:, k, :], S["G_in" + DIRS[k]][0:D, P:], xp[0:D, p, :, TAPS - 1:TAPS - 1 + T],
                                             start=True, stop=True).then_inc(z_ready, 1)
                    if slot in (15, 16):
                        for k in (slot - 15,):
                            pe.wait_ge(u_ready, n * 2 + k + 1)
                            nc.tensor.matmul(ring_ps[0:2 * NST + RANK, k, :], S["G_xproj" + DIRS[k]][:, :], u[:, p, k, :],
                                             start=True, stop=True).then_inc(low_ps, 1)
                    if slot in (19, 20):
                        for k in (slot - 19,):
                            pe.wait_ge(low_ready, n * 2 + k + 1)
                            nc.tensor.matmul(ring_ps[:, k, :], S["G_dt" + DIRS[k]][2 * NST:, :], low[2 * NST:, k, :],
                                             start=True, stop=True).then_inc(dt_ps, 1)

                def finish(slot, n, p):
                    k = 1 if slot < NST else 0
                    m = n * 2 + k
                    if slot % NST < LAG:
                        add_state(NST - LAG + slot % NST, k, m)
                    if slot % NST == LAG + 2:
                        pe.wait_ge(gated_done, m + 1)
                        wait_reuse(pe, h_done, m)
                        for g in range(G):
                            ins = nc.tensor.matmul(out_ps[:, g, :], gated[:, g * P:(g + 1) * P], S["G_out" + DIRS[k]][:, :], start=True, stop=True)
                        ins.then_inc(out_ready, 1)

                def add_state(s, k, m):
                    pe.wait_ge(weighted_done, m * NST + s + 1)
                    if s == 0:
                        wait_reuse(pe, mixed_done, m)
                    nc.tensor.matmul(y_ps[:, :], ident[:, :], state[:, s % RING, :], start=(s == 0), stop=(s == NST - 1)).then_inc(summed, 1)

                def slot_work(slot, n, p):
                    k, s, m = slot // NST, slot % NST, n * SLOTS + slot
                    if s == 0:
                        pe.wait_ge(parts_ready, n * 2 + k + 1)
                    wait_reuse(pe, driven, m - 1)
                    nc.tensor.matmul(b_ps[:, slot % 2, :], rows[:, s:s + 1].to_broadcast([96, P]), parts[:, p, k, :], start=True, stop=True).then_inc(b_ready, 1)
                    wait_reuse(pe, c_copied, m - 1)
                    nc.tensor.matmul(c_ps[:, slot % 2, :], rows[:, NST + s:NST + s + 1].to_broadcast([96, P]), parts[:, p, k, :],
                                     start=True, stop=True).then_inc(c_ready, 1)
                    if s >= LAG:
                        add_state(s - LAG, k, n * 2 + k)

                run(pe, front, finish, slot_work)


NP = NE // 2
BN_EPS = 1e-3


def loads_H(nc, S, A, sb, load, zeroed):
    q = "L3_ffn_"
    load(sb("H_wr", [D + 1, NE])[0:D, :], A[q + "Wr"][:, :])
    load(S["H_wr"][D:D + 1, :], A[q + "br"].rearrange("(a e) -> a e", a=1))
    load(sb("H_w1", [D, NE, D])[:], A[q + "W1"].rearrange("e d k -> d e k"))
    w2 = sb("H_w2", [P, NP, P])
    zeroed.append(w2)
    wo = sb("H_wo", [P, NP, D])
    for k in range(2):
        rows = slice(k * D, (k + 1) * D)
        load(w2[rows, :, rows], A[q + "W2"].rearrange("(u k) h j -> k h u j", k=2)[k])
        load(wo[rows, :, :], A[q + "Wo"].rearrange("(u k) h d -> k h u d", k=2)[k])
    load(sb("H_bo", [NE, D])[:, :], A[q + "bo"][:, :])
    for k in "12":
        for v in ("b", "g", "be", "m", "v"):
            load(sb(f"H_{v}{k}", [P, NP])[:, :], A[f"{q}{v}{k}"][:, :])


def gated_towers(nc, S):
    h, ident = S["h"], S["ident"]
    with ExitStack() as ctx:
        def prior(u, n, p, back):
            return (u - back, n, p) if u >= back else (u - back + NP, n - 1, 1 - p)

        def sb(name, shape, dt=F32):
            return ctx.enter_context(nc.sbuf_tensor(f"H_{name}", shape, dt))

        def ps(name, shape):
            return ctx.enter_context(nc.psum_tensor(f"H_{name}", shape, F32))

        sem = ctx.enter_context(semaphores(nc, "H"))

        xn_all = sb("xn_all", [P, B, D])
        xc, sq = sb("xc", [P, 2, G, D]), sb("sq", [P, G, D])
        total, var, rstd = sb("total", [P, G]), sb("var", [P, 2, G]), sb("rstd", [P, 2, G])
        stats_chain, var_ready, rstd_ready, xn_ready = sem("stats_chain"), sem("var_ready"), sem("rstd_ready"), sem("xn_ready")
        scale = [sb("scale1", [P, NP]), sb("scale2", [P, NP])]
        shift = [sb("shift1", [P, NP]), sb("shift2", [P, NP])]
        feat = sb("feat", [P, D])
        featT = sb("featT", [D + 1, P])
        w = sb("w", [P, NE])
        w_wide = sb("w_wide", [P, NE, D])
        wT = sb("wT", [NE, P])
        w_pair = sb("w_pair", [P, NP, P])
        bo_mix = sb("bo_mix", [P, D])
        small = sb("small", [P, 2])

        with nc.Block() as block:
            @block.vector
            def _(dve):
                def stats(n, p):
                    chain = Chain(dve, stats_chain, n, 4)
                    wait_reuse(dve, xn_ready, n - 1)
                    norm_stats(dve, nc, chain, h[:, bass.ds(n * G, G), :], xc[:, p, :, :], sq[:, :, :], total[:, :], var[:, p, :]).then_inc(var_ready, 1)
                    dve.wait_ge(var_ready, n + 1)
                    chain.end()

                def scaled(n, p):
                    dve.wait_ge(rstd_ready, n + 1)
                    nc.vector.tensor_tensor(xn_all[:, bass.ds(n * G, G), :], xc[:, p, :, :], bc(rstd[:, p, :], D), ALU.mult).then_inc(xn_ready, 1)

                in_order(dve, [(0, stats), (1, scaled)], TILES)

            @block.gpsimd
            def _(pool):
                def powers(n, p):
                    pool.wait_ge(var_ready, n + 1)
                    wait_reuse(pool, xn_ready, n - 1)
                    nc.gpsimd.tensor_tensor(rstd[:, p, :], var[:, p, :], S["neg_half"][:, 0:G], ALU.pow).then_inc(rstd_ready, 1)

                in_order(pool, [(0, powers)], TILES)

        with ExitStack() as c2:
            once = c2.enter_context(semaphores(nc, "H_once"))

            featT_ps = c2.enter_context(nc.psum_tensor("H_featT_ps", [D, P], F32))
            w_ps = c2.enter_context(nc.psum_tensor("H_w_ps", [P, NE], F32))
            wT_ps = c2.enter_context(nc.psum_tensor("H_wT_ps", [NE, P], F32))
            pair_ps = c2.enter_context(nc.psum_tensor("H_pair_ps", [P, NP, P], F32))
            mix_ps = c2.enter_context(nc.psum_tensor("H_mix_ps", [P, D], F32))
            chain_sem, feat_ready, turned, featT_ready, logits, shifted, exps, w_ready, wT_turned, wT_ready, mixed, vplus, vroot = map(
                once, "chain feat_ready turned featT_ready logits shifted exps w_ready wT_turned wT_ready mixed vplus vroot".split())
            with nc.Block() as block:
                @block.vector
                def _(dve):
                    chain = Chain(dve, chain_sem, 0, 14)
                    nc.vector.tensor_scalar(scale[0][:, :], S["H_v1"][:, :], BN_EPS, None, ALU.add)
                    nc.vector.tensor_scalar(scale[1][:, :], S["H_v2"][:, :], BN_EPS, None, ALU.add).then_inc(vplus, 1)
                    nc.vector.memset(featT[D:D + 1, :], 1.0)
                    chain(nc.vector.tensor_reduce(feat[:, :], xn_all[:, :, :].rearrange("p b d -> p d b"), X, ALU.add))
                    nc.vector.tensor_scalar(feat[:, :], feat[:, :], 1.0 / B, None, ALU.mult).then_inc(feat_ready, 1)
                    dve.wait_ge(turned, 1)
                    nc.vector.tensor_copy(featT[0:D, :], featT_ps[:, :]).then_inc(featT_ready, 1)
                    dve.wait_ge(vroot, 2)
                    for k in range(2):
                        c = "12"[k]
                        chain(nc.vector.tensor_tensor(scale[k][:, :], scale[k][:, :], S["H_g" + c][:, :], ALU.mult))
                        chain(nc.vector.tensor_tensor(shift[k][:, :], S["H_b" + c][:, :], S["H_m" + c][:, :], ALU.subtract))
                        chain(nc.vector.tensor_tensor(shift[k][:, :], shift[k][:, :], scale[k][:, :], ALU.mult))
                        chain(nc.vector.tensor_tensor(shift[k][:, :], shift[k][:, :], S["H_be" + c][:, :], ALU.add))
                    dve.wait_ge(logits, 1)
                    chain(nc.vector.tensor_reduce(small[:, 0:1], w_ps[:, :], X, ALU.max))
                    nc.vector.tensor_scalar(w[:, :], w_ps[:, :], small[:, 0:1], None, ALU.subtract).then_inc(shifted, 1)
                    dve.wait_ge(exps, 1)
                    chain(nc.vector.tensor_reduce(small[:, 0:1], w[:, :], X, ALU.add))
                    chain(nc.vector.reciprocal(small[:, 1:2], small[:, 0:1]))
                    chain(nc.vector.tensor_scalar(w[:, :], w[:, :], small[:, 1:2], None, ALU.mult))
                    nc.vector.tensor_copy(w_wide[:, :, :], bc(w[:, :], D)).then_inc(w_ready, 1)
                    dve.wait_ge(wT_turned, 1)
                    chain(nc.vector.tensor_copy(wT[:, :], wT_ps[:, :]))
                    nc.vector.tensor_copy(w_pair[:, :, :], pair_ps[:, :, :]).then_inc(wT_ready, 1)
                    dve.wait_ge(mixed, 1)
                    nc.vector.tensor_copy(bo_mix[:, :], mix_ps[:, :])
                    chain.end()

                @block.gpsimd
                def _(pool):
                    pool.wait_ge(vplus, 1)
                    for k in range(2):
                        nc.gpsimd.tensor_tensor(scale[k][:, :], scale[k][:, :], S["neg_half"][:, 0:NP], ALU.pow).then_inc(vroot, 1)

                @block.scalar
                def _(act):
                    act.wait_ge(shifted, 1)
                    nc.scalar.activation(w[:, :], w[:, :], ACT.Exp).then_inc(exps, 1)

                @block.tensor
                def _(pe):
                    pe.wait_ge(feat_ready, 1)
                    nc.tensor.transpose(featT_ps[:, :], feat[:, :], ident[:, :]).then_inc(turned, 1)
                    pe.wait_ge(featT_ready, 1)
                    nc.tensor.matmul(w_ps[:, :], featT[:, :], S["H_wr"][:, :], start=True, stop=True).then_inc(logits, 1)
                    pe.wait_ge(w_ready, 1)
                    for u in range(NP):
                        nc.tensor.transpose(pair_ps[:, u, :], w_wide[:, 2 * u:2 * u + 2, :].rearrange("p e d -> p (e d)"), ident[:, :])
                    nc.tensor.transpose(wT_ps[:, :], w[:, :], ident[:, :]).then_inc(wT_turned, 1)
                    pe.wait_ge(wT_ready, 1)
                    nc.tensor.matmul(mix_ps[:, :], wT[:, :], S["H_bo"][:, :], start=True, stop=True).then_inc(mixed, 1)

        xs = sb("xs", [P, 2, G, D])
        xT = sb("xT", [D, 2, COLS])
        one = sb("one", [P, NP, COLS])
        two = sb("two", [P, NP, COLS])
        out = sb("out", [P, COLS])
        xT_ps = ps("xT_ps", [P, G // 2, P])
        one_ps, two_ps = ps("one_ps", [P, 2, COLS]), ps("two_ps", [P, 2, COLS])
        out_ps, back_ps = ps("out_ps", [D, COLS]), ps("back_ps", [P, G, P])
        (fetched, xT_ps_ready, xT_ready, one_filled, one_ready, two_filled, two_ready, gated, out_done, out_ready,
         back_ready, h_done, cleared) = map(sem, "fetched xT_ps_ready xT_ready one_filled one_ready two_filled two_ready gated out_done out_ready back_ready h_done cleared".split())
        with nc.Block() as block:
            @block.gpsimd
            def _(pool):
                def fetch(n, p):
                    wait_reuse(pool, xT_ps_ready, n - 1)
                    nc.gpsimd.tensor_copy(xs[:, p, :, :], xn_all[:, bass.ds(n * G, G), :]).then_inc(fetched, 1)

                nc.gpsimd.memset(out[D:, :], 0.0).then_inc(cleared, 1)
                pool.wait_ge(cleared, 1)
                in_order(pool, [(0, fetch)], TILES)

            @block.vector
            def _(dve):
                def slot(u, n, p):
                    if exists(n):
                        dve.wait_ge(two_ready, n * NP + u + 1)
                        nc.vector.tensor_tensor(two[:, u, :].rearrange("p (g t) -> p g t", g=G), two[:, u, :].rearrange("p (g t) -> p g t", g=G),
                                                mid(w_pair[:, u, :], G), ALU.mult).then_inc(gated, 1)
                    if u == NP - 1 and exists(n - 1):
                        dve.wait_ge(back_ready, n)
                        hn = h[:, bass.ds((n - 1) * G, G), :]
                        nc.vector.tensor_tensor(hn, hn, back_ps[:, :, 0:D], ALU.add).then_inc(h_done, 1)
                        dve.wait_ge(h_done, 2 * n - 1)
                        nc.vector.tensor_tensor(hn, hn, mid(bo_mix[:, :], G), ALU.add).then_inc(h_done, 1)

                sweep(dve, slot, NP)

            @block.scalar
            def _(act):
                def front(n, p):
                    act.wait_ge(xT_ps_ready, n + 1)
                    wait_reuse(act, one_filled, (n - 1) * NP)
                    for q in range(2):
                        ins = nc.scalar.copy(xT[:, p, :].rearrange("d (g q t) -> d g q t", g=G // 2, q=2)[:, :, q, :],
                                             xT_ps[q * D:(q + 1) * D, :, :])
                    ins.then_inc(xT_ready, 1)

                def slot(u, n, p):
                    if u == 3 and exists(n - 1):
                        act.wait_ge(out_done, n * NP)
                        wait_reuse(act, back_ready, n - 1)
                        nc.scalar.copy(out[0:D, :], out_ps[:, :]).then_inc(out_ready, 1)
                    b, tile, _ = prior(u, n, p, 1)
                    if exists(n):
                        m = n * NP + u
                        act.wait_ge(one_filled, m + 1)
                        wait_reuse(act, two_filled, m - NP + 1)
                        nc.scalar.activation(one[:, u, :], one_ps[:, u % 2, :], ACT.Relu, bias=shift[0][:, u:u + 1],
                                             scale=scale[0][:, u:u + 1]).then_inc(one_ready, 1)
                    if u == 1 and exists(n + 1):
                        front(n + 1, 1 - p)
                    if exists(tile):
                        m = tile * NP + b
                        act.wait_ge(two_filled, m + 1)
                        wait_reuse(act, out_done, m - NP + 1)
                        nc.scalar.activation(two[:, b, :], two_ps[:, b % 2, :], ACT.Relu, bias=shift[1][:, b:b + 1],
                                             scale=scale[1][:, b:b + 1]).then_inc(two_ready, 1)

                sweep(act, slot, NP)

            @block.tensor
            def _(pe):
                def front(n, p):
                    pe.wait_ge(fetched, n + 1)
                    wait_reuse(pe, xT_ready, n)
                    for q in range(G // 2):
                        ins = nc.tensor.transpose(xT_ps[:, q, :], xs[:, p, 2 * q:2 * q + 2, :].rearrange("p g d -> p (g d)"), ident[:, :])
                    ins.then_inc(xT_ps_ready, 1)

                def back(n):
                    pe.wait_ge(out_ready, n + 1)
                    wait_reuse(pe, h_done, 2 * n)
                    for g in range(G):
                        ins = nc.tensor.transpose(back_ps[:, g, :], out[:, g * P:(g + 1) * P], ident[:, :])
                    ins.then_inc(back_ready, 1)

                def slot(u, n, p):
                    if exists(n):
                        if u == 0:
                            pe.wait_ge(xT_ready, n + 1)
                        wait_reuse(pe, one_ready, n * NP + u - 1)
                        nc.tensor.matmul(one_ps[:, u % 2, :], S["H_w1"][:, 2 * u:2 * u + 2, :].rearrange("d e k -> d (e k)"), xT[:, p, :],
                                         start=True, stop=True).then_inc(one_filled, 1)
                    if u == 0 and exists(n + 1):
                        front(n + 1, 1 - p)
                    b, tile, _ = prior(u, n, p, 1)
                    if exists(tile):
                        m = tile * NP + b
                        pe.wait_ge(one_ready, m + 1)
                        wait_reuse(pe, two_ready, m - 1)
                        nc.tensor.matmul(two_ps[:, b % 2, :], S["H_w2"][:, b, :], one[:, b, :], start=True, stop=True).then_inc(two_filled, 1)
                    b, tile, _ = prior(u, n, p, 3)
                    if exists(tile):
                        pe.wait_ge(gated, tile * NP + b + 1)
                        if b == 0:
                            wait_reuse(pe, out_ready, tile)
                        nc.tensor.matmul(out_ps[:, :], S["H_wo"][:, b, :], two[:, b, :], start=(b == 0), stop=(b == NP - 1)).then_inc(out_done, 1)
                    if u == NP - 1 and exists(n - 1):
                        back(n - 1)

                sweep(pe, slot, NP)


def load_weights(nc, S, A, layers):
    def sb(name, shape, dt=F32):
        S[name] = S["ctx"].enter_context(nc.sbuf_tensor(name, shape, dt))
        return S[name]

    loads, zeroed = [], []

    def load(dst, src):
        loads.append((dst, src))

    if "first" in layers:
        S["h"] = sb("h", [P, B, D])
        load(sb("ident", [P, P])[:, :], A["ident"][:, :])
        load(sb("part_experts", [32, NE])[:, :], A["part_experts"][:, :])
        load(sb("rev8", [P, NE])[:, :], A["rev8"][:, :])
        sb("neg_half", [P, NE])
    for layer, names in (("L0", ("gate_w", "gate_b")), ("L1", ("Wr", "br"))):
        if layer in layers:
            loads_moe(nc, S, A, sb, load, zeroed, layer, *names)
    if "A" in layers:
        loads_A(nc, S, A, sb, load, zeroed)
    if "C" in layers:
        loads_C(nc, S, A, sb, load, zeroed)
    if "E" in layers:
        loads_E(nc, S, A, sb, load, zeroed)
    if "F" in layers:
        loads_F(nc, S, A, sb, load, zeroed)
    if "G" in layers:
        loads_G(nc, S, A, sb, load, zeroed)
    if "H" in layers:
        loads_H(nc, S, A, sb, load, zeroed)
    tag = "_".join(layers)
    loaded = S["ctx"].enter_context(nc.semaphore("loaded_" + tag))
    cleared = S["ctx"].enter_context(nc.semaphore("cleared_" + tag))
    with nc.Block() as block:
        @block.vector
        def _(dve):
            for tile in zeroed:
                nc.vector.memset(tile[:], 0.0)
            if "first" in layers:
                nc.vector.memset(S["neg_half"][:], -0.5)
            nc.vector.drain().then_inc(cleared, 1)

        @block.sync
        def _(sp):
            sp.wait_ge(cleared, 1)
            for dst, src in loads:
                sp.dma_start(dst, src).then_inc(loaded, 16)
    return loaded, 16 * len(loads)


def await_loads(nc, started):
    loaded, count = started
    with nc.Block() as block:
        @block.sync
        def _(sp):
            sp.wait_ge(loaded, count)


def build(nc, A, out):
    with ExitStack() as ctx:
        S = {"ctx": ctx}
        first = load_weights(nc, S, A, ["first", "A"])
        early = load_weights(nc, S, A, ["L0", "C", "L1"])
        await_loads(nc, first)
        column_attention(nc, S, A)
        late = load_weights(nc, S, A, ["E", "F", "G", "H"])
        await_loads(nc, early)
        moe_layer(nc, S, "L0m", S["L0_ffn_w1"], S["L0_ffn_w2"], S["L0_ffn_b2"], S["L0_ffn_wr"], False)
        alibi_attention(nc, S, A)
        moe_layer(nc, S, "L1m", S["L1_ffn_w1"], S["L1_ffn_w2"], S["L1_ffn_b2"], S["L1_ffn_wr"], True)
        await_loads(nc, late)
        periodic_attention(nc, S)
        routed_mlp(nc, S)
        mamba(nc, S)
        gated_towers(nc, S)
        stored = ctx.enter_context(nc.semaphore("stored"))
        with nc.Block() as block:
            @block.sync
            def _(sp):
                sp.dma_start(out.rearrange("b t d -> t b d"), S["h"][:]).then_inc(stored, 16)
                sp.wait_ge(stored, 16)


def shape_constants():
    c = {"ident": np.eye(P, dtype=np.float32),
         "rev8": np.tile(np.arange(NE, 0, -1, dtype=np.float32), (P, 1))}
    c["part_experts"] = np.eye(NE, dtype=np.float32)[np.arange(32) % NE]
    c["part_experts"][3 * NE:] = 0
    constants_A(c)
    constants_C(c)
    constants_E(c)
    constants_G(c)
    return c


TURNED = ("L2_attn_Wq", "L2_attn_Wk", "L2_attn_Wv", "L2_ffn_Wi", "L2_ffn_Wr", "L2_ffn_Ws", "L2_ffn_Wo",
          *(f"L3_attn_{c}_{w}" for c in "fb" for w in ("in_w", "conv_w", "xproj_w", "dt_w", "out_w")))
LAST_IN_FRONT = ("L2_ffn_br", "L2_ffn_bs")
PAIRED = tuple("L3_ffn_" + v + k for v in ("b", "g", "be", "m", "v") for k in "12")


def kernel(**inputs):
    import numpy as _np
    import concourse.bacc as _bacc
    from concourse import mybir as _mybir
    from concourse.bass_utils import run_bass_kernel_spmd as _run

    nc = _bacc.Bacc("TRN2", target_bir_lowering=False, num_devices=1)
    arrays, args = {}, {}
    for name, a in list(inputs.items()) + list(shape_constants().items()):
        a = _np.asarray(a)
        if name == "L3_attn_b_in_w":
            a = a[:, ::-1]
        if name == "L3_attn_b_out_w":
            a = a[::-1, :]
        if name in TURNED:
            a = _np.swapaxes(a, -1, -2)
        if name in LAST_IN_FRONT:
            a = _np.moveaxis(a, -1, 0)
        if name in PAIRED:
            a = a.reshape(NE // 2, 2 * D).T
        a = _np.ascontiguousarray(a)
        arrays[f"in_{name}_dram"] = a
        args[name] = nc.dram_tensor(f"in_{name}_dram", a.shape, _mybir.dt.from_np(a.dtype), kind="ExternalInput").ap()
    out = nc.dram_tensor("out_0_dram", (B, T, D), _mybir.dt.from_np(_np.dtype("float32")), kind="ExternalOutput").ap()
    build(nc, args, out)
    r = _run(nc, [arrays], core_ids=[0])
    return r.results[0]["out_0_dram"]
```
